# Optimizing a Trainium2 kernel written in Bass

```python
import numpy as np
import jax
import jax.numpy as jnp

def _softmax(x, axis=-1):
    return jax.nn.softmax(x, axis=axis)

def _gelu(x):
    return jax.nn.gelu(x, approximate=True)

def _silu(x):
    return jax.nn.silu(x)

def _sigmoid(x):
    return jax.nn.sigmoid(x)

def _layernorm(x, axis=-1, eps=1e-05):
    m = jnp.mean(x, axis=axis, keepdims=True)
    v = jnp.var(x, axis=axis, keepdims=True)
    return (x - m) / jnp.sqrt(v + eps)

def _scatter_add(tgt, idx, src, axis=0):
    return tgt.at[idx].add(src)

def _segment_sum(src, seg, n):
    return jax.ops.segment_sum(src, seg, n)
kernel_name = 'mk_gnn_resnorm_d4_gnn_r8_44db38'

def setup_inputs(seed: int=0):
    np.random.seed(seed)
    _w = jnp.asarray

    def _rec_inputs():
        import jax
        import jax.numpy as jnp
        _gk = jax.random.key(seed)
        x = -0.0003713 + 1 * jax.random.normal(jax.random.fold_in(_gk, 1), (6250, 128), jnp.float32)
        src = jax.random.randint(jax.random.fold_in(_gk, 2), (100000,), 0, 6250, jnp.int32)
        dst = jnp.minimum((6250 * jax.random.uniform(jax.random.fold_in(_gk, 3), (100000,)) ** 2.0).astype(jnp.int32), 49999)
        _o = jnp.argsort(dst, stable=True)
        src = src[_o]
        dst = dst[_o]
        edge_attr_128 = -6.47781e-05 + 0.999943 * jax.random.normal(jax.random.fold_in(_gk, 12), (100000, 128), jnp.float32)
        edge_type_3 = jax.random.randint(jax.random.fold_in(_gk, 14), (100000,), 0, 3, jnp.int32)
        edge_weight = jax.random.uniform(jax.random.fold_in(_gk, 15), (100000,), jnp.float32, 0.0, 1)
        return (x, src, dst, edge_attr_128, edge_type_3, edge_weight)
    x, src, dst, edge_attr_128, edge_type_3, edge_weight = _rec_inputs()

    def _L0_gnn_setup():
        import jax, jax.numpy as jnp
        import numpy as np
        N, E, G, DIM = (12500, 200000, 64, 128)
        BN_EPS = 1e-05

        def _bn(h, gamma, beta):
            mu = jnp.mean(h, axis=0)
            var = jnp.var(h, axis=0)
            return (h - mu) * jax.lax.rsqrt(var + BN_EPS) * gamma + beta
        key = jax.random.key(seed)
        ks = jax.random.split(key, 20)
        inp = {'x': jax.random.normal(ks[0], (N, DIM), jnp.float32), 'edge_attr': jax.random.normal(ks[1], (E, DIM), jnp.float32), 'u': jax.random.normal(ks[2], (G, DIM), jnp.float32), 'edge_index': jax.random.randint(ks[3], (2, E), 0, N, jnp.int32), 'batch': jnp.sort(jax.random.randint(ks[4], (N,), 0, G, jnp.int32))}

        def xavier(k, shape):
            fan_in, fan_out = (shape[1], shape[0])
            lim = jnp.sqrt(6.0 / (fan_in + fan_out))
            return jax.random.uniform(k, shape, jnp.float32, -lim, lim)
        inp['W0'] = xavier(ks[5], (DIM, 3 * DIM))
        inp['b0'] = jnp.zeros((DIM,), jnp.float32)
        inp['W1'] = xavier(ks[6], (DIM, DIM))
        inp['b1'] = jnp.zeros((DIM,), jnp.float32)
        inp['W2'] = xavier(ks[7], (DIM, DIM))
        inp['b2'] = jnp.zeros((DIM,), jnp.float32)
        for i in range(3):
            inp[f'g{i}'] = jnp.ones((DIM,), jnp.float32)
            inp[f'bt{i}'] = jnp.zeros((DIM,), jnp.float32)
        return inp
    _L0_gnn_all = _L0_gnn_setup()
    _L0_gnn_in = {k: v for k, v in _L0_gnn_all.items() if k in ('u', 'W0', 'b0', 'W1', 'b1', 'W2', 'b2', 'g0', 'bt0', 'g1', 'bt1', 'g2', 'bt2')}
    del _L0_gnn_all

    def _L1_gnn_setup():
        import jax, jax.numpy as jnp
        import numpy as np
        NUM_NODES = 1250
        key = jax.random.key(seed)
        k1, k2, k3, k4 = jax.random.split(key, 4)
        x = jax.random.normal(k1, (NUM_NODES, 128), dtype=jnp.float32)
        edge_index = jax.random.randint(k2, (2, 80000), 0, NUM_NODES, dtype=jnp.int64)
        W = jax.random.normal(k3, (128, 128), dtype=jnp.float32) * (1.0 / np.sqrt(128))
        b = jax.random.normal(k4, (128,), dtype=jnp.float32) * 0.01
        return {'x': x, 'edge_index': edge_index, 'W': W, 'b': b}
    _L1_gnn_all = _L1_gnn_setup()
    _L1_gnn_in = {k: v for k, v in _L1_gnn_all.items() if k in ('W', 'b')}
    del _L1_gnn_all

    def _L2_gnn_setup():
        import jax, jax.numpy as jnp
        import numpy as np
        HIDDEN = 128
        N_NODES = 6250
        N_EDGES = 75000
        EPS = 1e-05
        key = jax.random.key(seed)
        ks = jax.random.split(key, 10)
        x = jax.random.normal(ks[0], (N_NODES, HIDDEN), dtype=jnp.float32)
        edge_index = jax.random.randint(ks[1], (2, N_EDGES), 0, N_NODES, dtype=jnp.int64)
        edge_type = jax.random.randint(ks[2], (N_EDGES,), 0, 3, dtype=jnp.int64)
        s = 0.02
        Wmsg = jax.random.normal(ks[3], (3, 2 * HIDDEN, HIDDEN), dtype=jnp.float32) * s
        bmsg = jnp.zeros((3, HIDDEN), dtype=jnp.float32)
        Wupd = jax.random.normal(ks[4], (2 * HIDDEN, HIDDEN), dtype=jnp.float32) * s
        bupd = jnp.zeros((HIDDEN,), dtype=jnp.float32)
        gamma = jnp.ones((HIDDEN,), dtype=jnp.float32)
        beta = jnp.zeros((HIDDEN,), dtype=jnp.float32)
        return {'x': x, 'edge_index': edge_index, 'edge_type': edge_type, 'Wmsg': Wmsg, 'bmsg': bmsg, 'Wupd': Wupd, 'bupd': bupd, 'gamma': gamma, 'beta': beta}
    _L2_gnn_all = _L2_gnn_setup()
    _L2_gnn_in = {k: v for k, v in _L2_gnn_all.items() if k in ('Wmsg', 'bmsg', 'Wupd', 'bupd', 'gamma', 'beta')}
    del _L2_gnn_all

    def _L3_gnn_setup():
        import jax, jax.numpy as jnp
        import numpy as np
        N_NODES = 12500
        N_EDGES = 400000
        IN_DIM = 128
        OUT_DIM = 128
        BN_EPS = 1e-05
        FILL_VALUE = 1.0
        key = jax.random.key(seed)
        k1, k2, k3, k4 = jax.random.split(key, 4)
        node_features = jax.random.normal(k1, (N_NODES, IN_DIM), dtype=jnp.float32)
        edge_index = jax.random.randint(k2, (2, N_EDGES), 0, N_NODES, dtype=jnp.int64)
        edge_weight = jax.random.uniform(k3, (N_EDGES,), dtype=jnp.float32)
        W = jax.random.normal(k4, (IN_DIM, OUT_DIM), dtype=jnp.float32) * np.sqrt(2.0 / (IN_DIM + OUT_DIM))
        b = jnp.zeros((OUT_DIM,), dtype=jnp.float32)
        gamma = jnp.ones((OUT_DIM,), dtype=jnp.float32)
        beta = jnp.zeros((OUT_DIM,), dtype=jnp.float32)
        return {'node_features': node_features, 'edge_index': edge_index, 'edge_weight': edge_weight, 'W': W, 'b': b, 'gamma': gamma, 'beta': beta}
    _L3_gnn_all = _L3_gnn_setup()
    _L3_gnn_in = {k: v for k, v in _L3_gnn_all.items() if k in ('W', 'b', 'gamma', 'beta')}
    del _L3_gnn_all
    return {'x': x, 'src': src, 'dst': dst, 'edge_attr_128': edge_attr_128, 'edge_type_3': edge_type_3, 'edge_weight': edge_weight, 'L0_gnn_u': _L0_gnn_in['u'], 'L0_gnn_W0': _L0_gnn_in['W0'], 'L0_gnn_b0': _L0_gnn_in['b0'], 'L0_gnn_W1': _L0_gnn_in['W1'], 'L0_gnn_b1': _L0_gnn_in['b1'], 'L0_gnn_W2': _L0_gnn_in['W2'], 'L0_gnn_b2': _L0_gnn_in['b2'], 'L0_gnn_g0': _L0_gnn_in['g0'], 'L0_gnn_bt0': _L0_gnn_in['bt0'], 'L0_gnn_g1': _L0_gnn_in['g1'], 'L0_gnn_bt1': _L0_gnn_in['bt1'], 'L0_gnn_g2': _L0_gnn_in['g2'], 'L0_gnn_bt2': _L0_gnn_in['bt2'], 'L1_gnn_W': _L1_gnn_in['W'], 'L1_gnn_b': _L1_gnn_in['b'], 'L2_gnn_Wmsg': _L2_gnn_in['Wmsg'], 'L2_gnn_bmsg': _L2_gnn_in['bmsg'], 'L2_gnn_Wupd': _L2_gnn_in['Wupd'], 'L2_gnn_bupd': _L2_gnn_in['bupd'], 'L2_gnn_gamma': _L2_gnn_in['gamma'], 'L2_gnn_beta': _L2_gnn_in['beta'], 'L3_gnn_W': _L3_gnn_in['W'], 'L3_gnn_b': _L3_gnn_in['b'], 'L3_gnn_gamma': _L3_gnn_in['gamma'], 'L3_gnn_beta': _L3_gnn_in['beta']}

def reference(x, src, dst, edge_attr_128, edge_type_3, edge_weight, L0_gnn_u, L0_gnn_W0, L0_gnn_b0, L0_gnn_W1, L0_gnn_b1, L0_gnn_W2, L0_gnn_b2, L0_gnn_g0, L0_gnn_bt0, L0_gnn_g1, L0_gnn_bt1, L0_gnn_g2, L0_gnn_bt2, L1_gnn_W, L1_gnn_b, L2_gnn_Wmsg, L2_gnn_bmsg, L2_gnn_Wupd, L2_gnn_bupd, L2_gnn_gamma, L2_gnn_beta, L3_gnn_W, L3_gnn_b, L3_gnn_gamma, L3_gnn_beta):
    import jax
    import jax.numpy as jnp

    def _L0_gnn_ref(x, edge_attr, u, W0, b0, W1, b1, W2, b2, g0, bt0, g1, bt1, g2, bt2, edge_index, batch):
        import jax, jax.numpy as jnp
        import numpy as np
        N, E, G, DIM = (12500, 200000, 64, 128)
        BN_EPS = 1e-05

        def _bn(h, gamma, beta):
            mu = jnp.mean(h, axis=0)
            var = jnp.var(h, axis=0)
            return (h - mu) * jax.lax.rsqrt(var + BN_EPS) * gamma + beta
        n = x.shape[0]
        src = edge_index[0]
        sums = jax.ops.segment_sum(edge_attr, src, num_segments=n)
        cnt = jax.ops.segment_sum(jnp.ones((edge_attr.shape[0],), edge_attr.dtype), src, num_segments=n)
        v_e = sums / jnp.maximum(cnt, 1.0)[:, None]
        out = jnp.concatenate([x, v_e, u[batch]], axis=1)
        for W, b, g, bt in ((W0, b0, g0, bt0), (W1, b1, g1, bt1), (W2, b2, g2, bt2)):
            out = jax.nn.relu(out @ W.T + b)
            out = _bn(out, g, bt)
        return out

    def _L1_gnn_ref(x, edge_index, W, b):
        import jax, jax.numpy as jnp
        import numpy as np
        NUM_NODES = 1250
        src, dst = (edge_index[0], edge_index[1])
        num_nodes = x.shape[0]
        aggregated = jax.ops.segment_sum(x[src], dst, num_segments=num_nodes)
        degree = jax.ops.segment_sum(jnp.ones_like(dst, dtype=x.dtype), dst, num_segments=num_nodes)
        degree = jnp.maximum(degree, 1.0)
        aggregated = aggregated / degree[:, None]
        out = jax.nn.relu(jnp.einsum('nd,od->no', aggregated + x, W) + b)
        return out

    def _L2_gnn_ref(x, edge_index, edge_type, Wmsg, bmsg, Wupd, bupd, gamma, beta):
        import jax, jax.numpy as jnp
        import numpy as np
        HIDDEN = 128
        N_NODES = 6250
        N_EDGES = 75000
        EPS = 1e-05
        src, dst = (edge_index[0], edge_index[1])
        N = x.shape[0]
        E = edge_type.shape[0]
        msg_input = jnp.concatenate([x[src], x[dst]], axis=-1)
        all_msgs = jnp.einsum('ec,tch->eth', msg_input, Wmsg) + bmsg
        messages = jnp.take_along_axis(all_msgs, edge_type[:, None, None], axis=1)[:, 0]
        agg = jax.ops.segment_sum(messages, dst, num_segments=N)
        count = jax.ops.segment_sum(jnp.ones((E, 1), dtype=x.dtype), dst, num_segments=N)
        agg = agg / jnp.maximum(count, 1.0)
        h = jnp.concatenate([x, agg], axis=-1) @ Wupd + bupd
        mu = jnp.mean(h, axis=-1, keepdims=True)
        var = jnp.var(h, axis=-1, keepdims=True)
        hn = (h - mu) / jnp.sqrt(var + EPS) * gamma + beta
        x_updated = jax.nn.gelu(hn, approximate=False)
        return x + x_updated

    def _L3_gnn_ref(node_features, edge_index, edge_weight, W, b, gamma, beta):
        import jax, jax.numpy as jnp
        import numpy as np
        N_NODES = 12500
        N_EDGES = 400000
        IN_DIM = 128
        OUT_DIM = 128
        BN_EPS = 1e-05
        FILL_VALUE = 1.0
        N = node_features.shape[0]
        dt = node_features.dtype
        loop = jnp.arange(N, dtype=edge_index.dtype)
        row = jnp.concatenate([edge_index[0], loop])
        col = jnp.concatenate([edge_index[1], loop])
        w = jnp.concatenate([edge_weight.astype(dt), jnp.full((N,), FILL_VALUE, dtype=dt)])
        deg = jax.ops.segment_sum(w, col, num_segments=N)
        dinv = jnp.where(deg > 0, jax.lax.rsqrt(deg), 0.0).astype(dt)
        norm = dinv[row] * w * dinv[col]
        x = node_features @ W
        msg = x[row] * norm[:, None]
        out = jax.ops.segment_sum(msg, col, num_segments=N) + b
        h = jax.nn.relu(out)
        mean = jnp.mean(h, axis=0)
        var = jnp.mean(jnp.square(h - mean), axis=0)
        h = (h - mean) * jax.lax.rsqrt(var + BN_EPS) * gamma + beta
        return h
    edge_index = jnp.stack([src, dst])
    batch0 = jnp.zeros((6250,), jnp.int32)
    x = _layernorm(x + _L0_gnn_ref(x, edge_attr_128, L0_gnn_u, L0_gnn_W0, L0_gnn_b0, L0_gnn_W1, L0_gnn_b1, L0_gnn_W2, L0_gnn_b2, L0_gnn_g0, L0_gnn_bt0, L0_gnn_g1, L0_gnn_bt1, L0_gnn_g2, L0_gnn_bt2, edge_index, batch0), axis=-1)
    x = _layernorm(x + _L1_gnn_ref(x, edge_index, L1_gnn_W, L1_gnn_b), axis=-1)
    x = _layernorm(x + _L2_gnn_ref(x, edge_index, edge_type_3, L2_gnn_Wmsg, L2_gnn_bmsg, L2_gnn_Wupd, L2_gnn_bupd, L2_gnn_gamma, L2_gnn_beta), axis=-1)
    x = _layernorm(x + _L3_gnn_ref(x, edge_index, edge_weight, L3_gnn_W, L3_gnn_b, L3_gnn_gamma, L3_gnn_beta), axis=-1)
    return x

_drawn_inputs = setup_inputs


def setup_inputs(seed=0):
    import zlib

    import numpy as np

    out = dict(_drawn_inputs(seed))
    spreads = {'L0_gnn_b0': (0.0, 0.1),
     'L0_gnn_b1': (0.0, 0.1),
     'L0_gnn_b2': (0.0, 0.1),
     'L0_gnn_g0': (1.0, 0.2),
     'L0_gnn_bt0': (0.0, 0.1),
     'L0_gnn_g1': (1.0, 0.2),
     'L0_gnn_bt1': (0.0, 0.1),
     'L0_gnn_g2': (1.0, 0.2),
     'L0_gnn_bt2': (0.0, 0.1),
     'L2_gnn_bmsg': (0.0, 0.298),
     'L2_gnn_bupd': (0.0, 0.1),
     'L2_gnn_gamma': (1.0, 0.2),
     'L2_gnn_beta': (0.0, 0.1),
     'L3_gnn_b': (0.0, 0.1),
     'L3_gnn_gamma': (1.0, 0.2),
     'L3_gnn_beta': (0.0, 0.1)}
    factors = {'L1_gnn_b': 6.772}
    for name, (base, spread) in spreads.items():
        noise = np.random.default_rng([zlib.crc32(name.encode()), seed]).standard_normal(out[name].shape)
        drawn = base * np.exp(spread * noise) if base else spread * noise
        out[name] = jnp.asarray(drawn.astype(out[name].dtype))
    for name, factor in factors.items():
        out[name] = (out[name] * factor).astype(out[name].dtype)
    return out
```

```python
from contextlib import ExitStack

import concourse.bass as bass
from concourse import mybir

ALU = mybir.AluOpType
ACT = mybir.ActivationFunctionType
AX_X = mybir.AxisListType.X
F32 = mybir.dt.float32
BF16 = mybir.dt.bfloat16
I32 = mybir.dt.int32
U32 = mybir.dt.uint32
U8 = mybir.dt.uint8
DVE = mybir.EngineType.DVE

P = 128
N = 6250
E = 100000
D = 128
TYPES = 3
GROUPS = -(-N // P)
LAST = N - (GROUPS - 1) * P
STEP = 7
STEPS = GROUPS // STEP
SHIFT = 7
NO_NODE = 63 * P

BATCH = 10
SRING = 3
MAIN = 780
TAIL_LANES = 80
TAIL = 2
COLS = MAIN + TAIL
ROUNDS = MAIN // (BATCH * SRING)
assert P * MAIN + TAIL_LANES * TAIL == E and ROUNDS * BATCH * SRING == MAIN

CH = 8
RING = 4
CHUNKS = 832
BATCHES = CHUNKS // CH
RROUNDS = BATCHES // RING
assert (E + GROUPS * (P - 1)) // P <= CHUNKS and RROUNDS * RING * CH == CHUNKS

ROW = D + 2
ONE, LANE1 = D, D + 1
PAY = 8
P_SRC, P_SRCT, P_LANE1, P_ONE, P_TYPE, P_W = 0, 1, 2, 3, 4, 7
EXTRA = PAY - P_ONE
AW = D + EXTRA
HALF = STEP * P // 2
ZCH = 32
EPS = 1e-5
NEAR = 3
WIDE_BANKS = (2, 3, 4, 5, 6, 7, 5)
BN_COLS = 250
NBN = N // BN_COLS


def first_of(i):
    return isinstance(i, int) and i == 0


class Chain:

    def __init__(self, eng, sem):
        self.eng, self.sem, self.n, self.at = eng, sem, 0, None

    def mark(self, ins):
        self.n += 1
        ins.then_inc(self.sem, 1)
        return self.n if self.at is None else self.at + (self.n - self.start)

    def wait(self, value):
        self.eng.wait_ge(self.sem, value)

    def link(self, ins):
        self.wait(self.mark(ins))

    def enter(self, i, per):
        self.start, self.per, self.at = self.n, per, i * per + self.n

    def leave(self, turns):
        assert self.n - self.start == self.per, (self.n - self.start, self.per)
        self.n = self.start + self.per * turns
        self.at = None


def gnn_kernel(nc, x, src, dst, edge_attr, edge_type, edge_weight, u, W0, b0, W1, b1, W2, b2,
               g0, bt0, g1, bt1, g2, bt2, L1W, L1b, Wmsg, bmsg, Wupd, bupd, gam2, bet2,
               W3, b3, gam3, bet3, out):
    with ExitStack() as ctx:
        def sb(name, shape, dt=F32):
            return ctx.enter_context(nc.sbuf_tensor(name, shape, dt))

        def sem(name):
            return ctx.enter_context(nc.semaphore(name))

        def dram(name, shape, dt=F32):
            return nc.dram_tensor(name, shape, dt).ap()

        slots_src = dram("slots_src", [P, CHUNKS, ROW])
        slots_dst = dram("slots_dst", [P, CHUNKS, PAY])
        sums_at_src = dram("sums_at_src", [BATCHES, CH], I32)
        sums_at_dst = dram("sums_at_dst", [BATCHES, CH], I32)
        x1_table = dram("x1_table", [P, GROUPS, D])
        msg_table = dram("msg_table", [P, GROUPS, TYPES * D])
        z_table = dram("z_table", [P, GROUPS, D])

        X = sb("X", [P, GROUPS, D])
        A = sb("A", [P, GROUPS * D])
        masks_raw = sb("masks_raw", [P, 9600])
        lists_raw = sb("lists_raw", [P, 11 * COLS])
        pay_raw = sb("pay_raw", [P, CHUNKS * PAY])
        rows_raw = sb("rows_raw", [P, RING * CH * AW])
        zr = sb("zr", [P, STEP, D])
        zt = sb("zt", [P, STEP, D])
        idx_scatter = sb("idx_scatter", [P, SRING, BATCH], U32)
        idx_gather = sb("idx_gather", [P, RING, CH], U32)
        idx_tail = sb("idx_tail", [P, 2, TAIL], U32)
        pay_stage = sb("pay_stage", [P, SRING, BATCH * PAY])
        tail_rows = sb("tail_rows", [P, TAIL, ROW])
        at_src = sb("at_src", [1, CHUNKS], I32)
        at_dst = sb("at_dst", [1, CHUNKS], I32)

        masks = masks_raw[:, :].bitcast(U8)[:, 0:GROUPS * COLS].rearrange("p (b c) -> p b c", c=COLS)
        sums_flat = masks_raw[:, 0:GROUPS * AW]
        sums = sums_flat.rearrange("p (g w) -> p g w", w=AW)
        onehot = masks_raw[:, GROUPS * AW:GROUPS * AW + 2 * CH * P].rearrange(
            "p (s j n) -> p s j n", s=2, j=CH)
        assert GROUPS * AW + 2 * CH * P <= 9600 and GROUPS * COLS <= 4 * 9600

        def listed(k, dt=F32):
            v = lists_raw[:, k * COLS:(k + 1) * COLS]
            return v if dt == F32 else v.bitcast(dt)
        src_i, dst_i, type_i, w_f = listed(0, I32), listed(1, I32), listed(2, I32), listed(3)
        lane1_src, pos = listed(4), listed(5)
        tmp_i, tmp2_i = listed(6, I32), listed(7, I32)
        group_b = lists_raw[:, 8 * COLS:8 * COLS + COLS // 2].bitcast(BF16)
        slot_src, slot_dst = listed(9), listed(10)
        B = lists_raw[:, 0:GROUPS * D]
        At = A[:, :].rearrange("p (g d) -> p g d", d=D)
        Bt = B.rearrange("p (g d) -> p g d", d=D)

        pay = pay_raw[:, 0:COLS * PAY].rearrange("p (c w) -> p c w", w=PAY)
        ordered = pay_raw[:, :].rearrange("p (k w) -> p k w", w=PAY)
        zeros = rows_raw[:, 0:ZCH * ROW]
        edge_rows = rows_raw[:, 0:SRING * BATCH * ROW].rearrange("p (s c w) -> p s c w", s=SRING, c=BATCH)
        slot_rows = rows_raw[:, 0:RING * CH * ROW].rearrange("p (s c w) -> p s c w", s=RING, c=CH)
        node_rows = rows_raw[:, :].rearrange("p (s c w) -> p s c w", s=RING, c=CH)
        msgs = rows_raw[:, 0:STEP * TYPES * D].rearrange("p (j f) -> p j f", j=STEP)

        lane_ids = sb("lane_ids", [P, P])
        group_ids = sb("group_ids", [P, GROUPS])
        chunk_ids = sb("chunk_ids", [BATCHES, CH])
        ident = sb("ident", [P, P])
        before = sb("before", [P, P])
        ones = sb("ones", [P, P])
        eps_col = sb("eps_col", [P, 1])
        cnt = sb("cnt", [P, GROUPS])
        small = sb("small", [P, 6, GROUPS])
        small_i = sb("small_i", [P, GROUPS], I32)
        start_at = sb("start_at", [P, GROUPS])
        below = sb("below", [BATCHES, CH, GROUPS])
        tile_of = sb("tile_of", [BATCHES, CH])
        at_cols = sb("at_cols", [BATCHES, 2, CH], I32)
        stats = sb("stats", [P, GROUPS, 6])
        mv = sb("mv", [P, 2, GROUPS])
        sd = sb("sd", [P, GROUPS])
        rstd = sb("rstd", [P, GROUPS])
        nmr = sb("nmr", [P, GROUPS])
        rcnt = sb("rcnt", [P, GROUPS])
        ctype = sb("ctype", [P, TYPES, GROUPS])
        dinv = sb("dinv", [P, GROUPS])
        deg = sb("deg", [P, 3, GROUPS])
        wraw = zt[:, 0:6, :]
        wT = sb("wT", [P, 6, D])
        wcat = sb("wcat", [P, 8, D])
        w3 = sb("w3", [P, D])
        cols = sb("cols", [P, 10])
        brows = sb("brows", [1, 5 * D])
        bc_src = sb("bc_src", [1, 5, D])
        bc = sb("bc", [P, 5, D])
        bias0 = sb("bias0", [P, 1])
        bn_st = sb("bn_st", [P, NBN, 6])
        bn_mv = sb("bn_mv", [P, 2])
        bn_c = sb("bn_c", [P, 3, 4])
        rowv = sb("rowv", [P, 5, D])

        ps = ctx.enter_context(nc.psum_tensor("ps", [P, 8, 512], F32))

        def bank(b, n=512):
            return ps[:, b, 0:n]

        keys_in, lists_in, x_in, w_in, tail_in = (sem(s) for s in (
            "keys_in", "lists_in", "x_in", "w_in", "tail_in"))
        zero_ready, zero_done, consts, gp_ones = (sem(s) for s in (
            "zero_ready", "zero_done", "consts", "gp_ones"))
        chain_sem = sem("vector_chain")
        pad_ready, masks_made, counted, counts_summed = (sem(s) for s in (
            "pad_ready", "masks_made", "counted", "counts_summed"))
        cols_ready, at_out, at_in = sem("cols_ready"), sem("at_out"), sem("at_in")
        slots_ready, pay_ready = sem("slots_ready"), sem("pay_ready")
        prep_in, prep_t, prep_out, bc_done, bc_copied, bias0_done, bias0_out = (sem(s) for s in (
            "prep_in", "prep_t", "prep_out", "bc_done", "bc_copied", "bias0_done", "bias0_out"))
        edge_rows_in = [sem(f"edge_rows_in{r}") for r in range(SRING)]
        staged_a, staged_b, staged_tail = sem("staged_a"), sem("staged_b"), sem("staged_tail")
        issued = sem("issued")
        scattered_a = [sem(f"scattered_a{r}") for r in range(SRING)]
        scattered_b = [sem(f"scattered_b{r}") for r in range(SRING)]
        tail_a, tail_b = sem("tail_a"), sem("tail_b")
        slot_rows_in = [sem(f"slot_rows_in{r}") for r in range(RING)]
        gathered = [sem(f"gathered{r}") for r in range(RING)]
        ordered_in = sem("ordered_in")
        sums_zero = sem("sums_zero")
        onehot_ready, products, added = sem("onehot_ready"), sem("products"), sem("added")
        idx_ready, extras_ready = sem("idx_ready"), sem("extras_ready")
        st = {s: {k: sem(f"{s}_{k}") for k in "ztcmr"} for s in
              ("mlp0", "mlp1", "mlp2", "x1", "f1", "g2", "h2", "f2", "g3", "f3")}
        bn_in = sem("bn_in")
        mv_done, sd_done = sem("mv_done"), sem("sd_done")
        bnsd_in, bnsd_out = sem("bnsd_in"), sem("bnsd_out")
        x1_ready, x1_out, msg_out, z_out, y_ready, y_out = (sem(s) for s in (
            "x1_ready", "x1_out", "msg_out", "z_out", "y_ready", "y_out"))
        counted_dst, bn_applied, stats_done, x_normed, sums_zero2 = (sem(s) for s in (
            "counted_dst", "bn_applied", "stats_done", "x_normed", "sums_zero2"))
        xt_done, xt_copied, upd_copied = sem("xt_done"), sem("xt_copied"), sem("upd_copied")
        norm_ready, gelu_done = sem("norm_ready"), sem("gelu_done")
        deg_ready, deg_sd = sem("deg_ready"), sem("deg_sd")
        sum_h, sq_ready, sum_sq, dev_ready = (sem(s) for s in ("sum_h", "sq_ready", "sum_sq", "dev_ready"))
        raw_ready, relu_done = sem("raw_ready"), sem("relu_done")
        rowsd_in, rowsd_out = sem("rowsd_in"), sem("rowsd_out")

        block = ctx.enter_context(nc.Block())

        def tslot(j, base=0):
            return ps[:, base + j // 4, (j % 4) * D:(j % 4 + 1) * D]

        def tslots(base=0):
            return ps[:, base:base + 2, :].rearrange("p b n -> p (b n)")[:, 0:STEP * D]

        def grouped(v):
            return v.rearrange("p (j d) -> p j d", d=D)

        zt_flat = zt[:, :, :].rearrange("p j d -> p (j d)")

        def product(s, j, width):
            return ps[:, 4 * s + j // 2, (j % 2) * AW:(j % 2) * AW + width]

        def last_edges(a):
            return a[P * MAIN:E].rearrange("(p c) -> p c", p=TAIL_LANES)

        def main_edges(a):
            return a[0:P * MAIN].rearrange("(p c) -> p c", p=P)

        attr_main = edge_attr[0:P * MAIN, :].rearrange("(p c) d -> p c d", p=P)
        attr_tail = edge_attr[P * MAIN:E, :].rearrange("(p c) d -> p c d", p=TAIL_LANES)

        def col(v):
            return v.rearrange("(d a) -> d a", a=1)

        def row(v):
            return v.rearrange("(a d) -> a d", a=1)

        def by_group(v):
            return (v[0:(GROUPS - 1) * P, :].rearrange("(g p) d -> p g d", p=P),
                    v[(GROUPS - 1) * P:N, :])

        @block.sync
        def _(sp):
            sp.dma_start(src_i[:, 0:MAIN], main_edges(src)).then_inc(keys_in, 16)
            sp.wait_ge(pad_ready, 1)
            sp.dma_start(src_i[0:TAIL_LANES, MAIN:COLS], last_edges(src)).then_inc(keys_in, 16)
            for dst_t, s in ((dst_i, dst), (type_i, edge_type), (w_f, edge_weight)):
                sp.dma_start(dst_t[:, 0:MAIN], main_edges(s)).then_inc(lists_in, 16)
                sp.dma_start(dst_t[0:TAIL_LANES, MAIN:COLS], last_edges(s)).then_inc(lists_in, 16)
            full, last = by_group(x)
            sp.dma_start(X[:, 0:GROUPS - 1, :], full).then_inc(x_in, 16)
            sp.dma_start(X[0:LAST, GROUPS - 1, :], last).then_inc(x_in, 16)
            sp.dma_start(wraw[:, 0:3, :], W0.rearrange("o (k i) -> o k i", k=3)).then_inc(w_in, 16)
            for k, w in ((3, W1), (4, W2), (5, L1W)):
                sp.dma_start(wraw[:, k, :], w).then_inc(w_in, 16)
            for t in range(TYPES):
                for h in range(2):
                    sp.dma_start(wcat[:, TYPES * h + t, :], Wmsg[t, h * D:(h + 1) * D, :]).then_inc(w_in, 16)
            sp.dma_start(wcat[:, 6:8, :], Wupd.rearrange("(h i) o -> i h o", h=2)).then_inc(w_in, 16)
            sp.dma_start(w3[:, :], W3).then_inc(w_in, 16)
            sp.dma_start(cols[:, 0:1], u[0:1, :].rearrange("a d -> d a")).then_inc(w_in, 16)
            for k, v in enumerate((b0, b1, b2, g0, bt0, g1, bt1, g2, bt2)):
                sp.dma_start(cols[:, k + 1:k + 2], col(v)).then_inc(w_in, 16)
            sp.dma_start(brows[0:1, 0:D], row(L1b)).then_inc(w_in, 16)
            sp.dma_start(brows[0:1, D:4 * D], bmsg.rearrange("t d -> (t d)").rearrange(
                "(a d) -> a d", a=1)).then_inc(w_in, 16)
            sp.dma_start(brows[0:1, 4 * D:5 * D], row(bupd)).then_inc(w_in, 16)
            for k, v in enumerate((gam2, bet2, b3, gam3, bet3)):
                sp.dma_start(bc_src[0:1, k, :], row(v)).then_inc(w_in, 16)
            sp.dma_start(tail_rows[0:TAIL_LANES, :, 0:D], attr_tail).then_inc(tail_in, 16)
            sp.wait_ge(zero_ready, 1)
            zero_rows = zeros.rearrange("p (c w) -> p c w", w=ROW)
            for k in range(CHUNKS // ZCH):
                sp.dma_start(slots_src[:, k * ZCH:(k + 1) * ZCH, :], zero_rows).then_inc(zero_done, 16)
            half = CHUNKS * PAY // 2
            for k in range(2):
                sp.dma_start(slots_dst.rearrange("p c w -> p (c w)")[:, k * half:(k + 1) * half],
                             zeros[:, 0:half]).then_inc(zero_done, 16)
            sp.wait_ge(gp_ones, 1)
            def load_edge_rows(i, r):
                at = i * (SRING * BATCH) + r * BATCH
                sp.dma_start(edge_rows[:, r, :, 0:D], attr_main[:, bass.ds(at, BATCH), :]).then_inc(
                    edge_rows_in[r], 16)
            for r in range(SRING):
                load_edge_rows(0, r)
            with sp.Fori(1, ROUNDS) as i:
                for r in range(SRING):
                    sp.wait_ge(scattered_a[r], i * (16 * BATCH))
                    load_edge_rows(i, r)
            for k, (table, flat) in enumerate(((sums_at_src, at_src), (sums_at_dst, at_dst))):
                sp.wait_ge(cols_ready, k + 1)
                sp.dma_start(table, at_cols[:, k, :]).then_inc(at_out, 16)
                sp.wait_ge(at_out, 16 * (k + 1))
                sp.dma_start(flat[0:1, :], table.rearrange("b c -> (b c)").rearrange(
                    "(a k) -> a k", a=1)).then_inc(at_in, 16)
            for r in range(SRING):
                sp.wait_ge(scattered_a[r], 16 * BATCH * ROUNDS)
            sp.wait_ge(tail_a, 16 * TAIL)
            with sp.Fori(0, RROUNDS) as i:
                for r in range(RING):
                    sp.wait_ge(products, i * RING + (r + 1))
                    sp.dma_start(slot_rows[:, r, :, :],
                                 slots_src[:, bass.ds(i * (RING * CH) + r * CH, CH), :]).then_inc(
                        slot_rows_in[r], 16)
            for r in range(SRING):
                sp.wait_ge(scattered_b[r], 16 * BATCH * ROUNDS)
            sp.wait_ge(tail_b, 16 * TAIL)
            sp.dma_start(ordered, slots_dst).then_inc(ordered_in, 16)
            sp.wait_ge(x1_ready, GROUPS)
            sp.dma_start(x1_table, X[:, :, :]).then_inc(x1_out, 16)
            with sp.Fori(0, STEPS) as i:
                sp.wait_ge(st["g2"]["r"], i * STEP + (STEP + NEAR))
                sp.dma_start(msg_table[:, bass.ds(i * STEP, STEP), :], msgs).then_inc(msg_out, 16)
            with sp.Fori(0, STEPS) as i:
                sp.wait_ge(st["g3"]["r"], i + 1)
                sp.dma_start(z_table[:, bass.ds(i * STEP, STEP), :],
                             At[:, bass.ds(i * STEP, STEP), :]).then_inc(z_out, 16)
            sp.wait_ge(y_ready, GROUPS)
            full, last = by_group(out)
            sp.dma_start(full, X[:, 0:GROUPS - 1, :]).then_inc(y_out, 16)
            sp.dma_start(last, X[0:LAST, GROUPS - 1, :]).then_inc(y_out, 16)
            sp.wait_ge(y_out, 32)

        @block.gpsimd
        def _(pool):
            pool.memset(zeros, 0.0).then_inc(zero_ready, 1)
            pool.iota(group_ids[:, :], [[1, GROUPS]], base=0, channel_multiplier=0,
                      allow_small_or_imprecise_dtypes=True).then_inc(consts, 1)
            pool.iota(lane_ids[:, :], [[1, P]], base=1, channel_multiplier=0,
                      allow_small_or_imprecise_dtypes=True).then_inc(consts, 1)
            pool.iota(chunk_ids[:, :], [[1, CH]], base=0, channel_multiplier=CH,
                      allow_small_or_imprecise_dtypes=True).then_inc(consts, 1)
            pool.memset(ones[:, :], 1.0).then_inc(consts, 1)
            pool.memset(eps_col[:, :], EPS).then_inc(consts, 1)
            pool.wait_ge(consts, 5)
            pool.affine_select(out=ident[:, :], in_=ones[:, :], pattern=[[-1, P]], base=0,
                               channel_multiplier=1, compare_op=ALU.is_equal, fill=0.0).then_inc(consts, 1)
            pool.affine_select(out=before[:, :], in_=ones[:, :], pattern=[[1, P]], base=0,
                               channel_multiplier=-1, compare_op=ALU.is_gt, fill=0.0).then_inc(consts, 1)
            pool.wait_ge(zero_done, 16 * (CHUNKS // ZCH + 2))
            pool.memset(edge_rows[:, :, :, ONE:ONE + 1], 1.0).then_inc(gp_ones, 1)
            flat_src = slots_src.rearrange("p c w -> (p c) w")
            flat_dst = slots_dst.rearrange("p c w -> (p c) w")
            with pool.Fori(0, ROUNDS) as i:
                for r in range(SRING):
                    pool.wait_ge(staged_a, i * SRING + (r + 1))
                    pool.sem_inc(issued, 1)
                    pool.wait_ge(edge_rows_in[r], i * 16 + 16)
                    pool.sem_inc(issued, 1)
                    for c in range(BATCH):
                        pool.indirect_dma_start(
                            flat_src, bass.IndirectOffsetOnAxis(idx_scatter[:, r, c:c + 1], 0),
                            edge_rows[:, r, c, :], None).then_inc(scattered_a[r], 16)
            pool.wait_ge(staged_tail, 1)
            for c in range(TAIL):
                pool.indirect_dma_start(
                    flat_src, bass.IndirectOffsetOnAxis(idx_tail[0:TAIL_LANES, 0, c:c + 1], 0),
                    tail_rows[0:TAIL_LANES, c, :], None).then_inc(tail_a, 16)
            def scatter_payloads(i, r):
                at = i * (SRING * BATCH) + r * BATCH
                pool.tensor_copy(idx_scatter[:, r, :], slot_dst[:, bass.ds(at, BATCH)])
                pool.tensor_copy(pay_stage[:, r, :],
                                 pay_raw[:, bass.ds(at * PAY, BATCH * PAY)]).then_inc(staged_b, 1)
                pool.wait_ge(staged_b, i * SRING + (r + 1))
                pool.sem_inc(issued, 1)
                for c in range(BATCH):
                    pool.indirect_dma_start(
                        flat_dst, bass.IndirectOffsetOnAxis(idx_scatter[:, r, c:c + 1], 0),
                        pay_stage[:, r, c * PAY:(c + 1) * PAY], None).then_inc(scattered_b[r], 16)

            for r in range(SRING):
                pool.wait_ge(scattered_a[r], 16 * BATCH * ROUNDS)
                pool.sem_inc(issued, 1)
                scatter_payloads(0, r)
            with pool.Fori(1, ROUNDS) as i:
                for r in range(SRING):
                    pool.wait_ge(scattered_b[r], i * (16 * BATCH))
                    pool.sem_inc(issued, 1)
                    scatter_payloads(i, r)
            for c in range(TAIL):
                pool.indirect_dma_start(
                    flat_dst, bass.IndirectOffsetOnAxis(idx_tail[0:TAIL_LANES, 1, c:c + 1], 0),
                    pay[0:TAIL_LANES, MAIN + c, :], None).then_inc(tail_b, 16)

            def gather(table, layer):
                with pool.Fori(0, RROUNDS) as i:
                    for r in range(RING):
                        pool.wait_ge(idx_ready, i * RING + ((layer - 1) * BATCHES + r + 1))
                        pool.sem_inc(issued, 1)
                        for c in range(CH):
                            pool.indirect_dma_start(
                                node_rows[:, r, c, 0:D], None, table,
                                bass.IndirectOffsetOnAxis(idx_gather[:, r, c:c + 1], 0)).then_inc(
                                gathered[r], 16)

            pool.wait_ge(x1_out, 16)
            gather(x1_table.rearrange("p g d -> (p g) d"), 1)
            pool.wait_ge(st["f1"]["z"], GROUPS)
            pool.memset(sums_flat, 0.0).then_inc(sums_zero2, 1)
            pool.wait_ge(msg_out, 16 * STEPS)
            gather(msg_table.rearrange("p g (t d) -> (p g t) d", t=TYPES), 2)
            pool.wait_ge(st["f2"]["z"], GROUPS)
            pool.memset(sums_flat, 0.0).then_inc(sums_zero2, 1)
            pool.wait_ge(z_out, 16 * STEPS)
            gather(z_table.rearrange("p g d -> (p g) d"), 3)

        W_LOADS = 3 + 1 + 2 * TYPES + 1 + 1 + 10 + 3 + 5

        @block.scalar
        def _(act):
            act.wait_ge(x_in, 32)
            with act.Fori(0, STEPS) as i:
                for j in range(STEP):
                    act.wait_ge(masks_made, i * STEP + (j + 1))
                    mask = masks[:, bass.ds(i * STEP + j, 1), :].rearrange("p a c -> p (a c)")
                    act.activation(mask, mask, ACT.Copy, accum_out=cnt[:, bass.ds(i * STEP + j, 1)]).then_inc(counted, 1)
            act.wait_ge(w_in, 16 * W_LOADS)
            for k in range(6):
                act.wait_ge(prep_t, k + 1)
                act.copy(wT[:, k, :], bank(6, D)).then_inc(prep_out, 1)
            act.wait_ge(bc_done, 1)
            act.copy(bc[:, 0:4, :].rearrange("p k d -> p (k d)"), bank(6)).then_inc(bc_copied, 1)
            act.wait_ge(bc_done, 2)
            act.copy(bc[:, 4, :], bank(6, D)).then_inc(bc_copied, 1)
            act.wait_ge(bias0_done, 1)
            act.activation(bias0[:, :], ps[:, 6, 0:1], ACT.Identity, bias=cols[:, 1:2]).then_inc(bias0_out, 1)
            with act.Fori(0, STEPS) as i:
                for j in range(STEP):
                    g = i * STEP + j
                    act.copy(zr[:, j, :], X[:, bass.ds(g, 1), :].rearrange("p a d -> p (a d)")).then_inc(
                        prep_in, 1)
                    act.wait_ge(xt_done, g + 1)
                    act.copy(A[:, bass.ds(g * D, D)], bank(6, D)).then_inc(xt_copied, 1)

            def stage_a(i, r):
                at = i * (SRING * BATCH) + r * BATCH
                act.copy(idx_scatter[:, r, :], slot_src[:, bass.ds(at, BATCH)])
                act.copy(edge_rows[:, r, :, LANE1:LANE1 + 1].rearrange("p c a -> p (c a)"),
                         lane1_src[:, bass.ds(at, BATCH)]).then_inc(staged_a, 1)

            act.wait_ge(slots_ready, 1)
            act.wait_ge(gp_ones, 1)
            for r in range(SRING):
                stage_a(0, r)
            with act.Fori(1, ROUNDS) as i:
                for r in range(SRING):
                    act.wait_ge(scattered_a[r], i * (16 * BATCH))
                    stage_a(i, r)
            act.wait_ge(tail_in, 16)
            act.wait_ge(pay_ready, 1)
            act.copy(idx_tail[:, 0, :], slot_src[:, MAIN:COLS])
            act.copy(idx_tail[:, 1, :], slot_dst[:, MAIN:COLS])
            act.copy(tail_rows[:, :, ONE:ONE + 1].rearrange("p c a -> p (c a)"), ones[:, 0:TAIL])
            act.copy(tail_rows[:, :, LANE1:LANE1 + 1].rearrange("p c a -> p (c a)"),
                     lane1_src[:, MAIN:COLS]).then_inc(staged_tail, 1)

            def copy_t(stage, i):
                act.wait_ge(st[stage]["t"], i + 1)
                act.copy(zt_flat, tslots()).then_inc(st[stage]["c"], 1)

            def relu_cols(stage, i, bias):
                for h in range(2):
                    act.wait_ge(st[stage]["m"], i * 2 + (h + 1))
                    act.activation(A[:, bass.ds(i * (2 * HALF) + h * HALF, HALF)], bank(2 + h, HALF),
                                   ACT.Relu, bias=bias).then_inc(st[stage]["r"], 1)

            def bn_sqrt(k):
                act.wait_ge(bnsd_in, k + 1)
                act.activation(bn_c[:, k, 0:1], bn_mv[:, 1:2], ACT.Sqrt, bias=eps_col[:, :]).then_inc(
                    bnsd_out, 1)

            copy_t("mlp0", 0)
            with act.Fori(0, STEPS - 1) as i:
                relu_cols("mlp0", i, bias0[:, :])
                copy_t("mlp0", i + 1)
            relu_cols("mlp0", STEPS - 1, bias0[:, :])
            bn_sqrt(0)
            for k, stage in ((1, "mlp1"), (2, "mlp2")):
                with act.Fori(0, STEPS) as i:
                    relu_cols(stage, i, cols[:, k + 1:k + 2])
                bn_sqrt(k)

            def affine_cols(i):
                for j in range(STEP):
                    act.activation(zr[:, j, :], A[:, bass.ds((i * STEP + j) * D, D)], ACT.Identity,
                                   bias=bn_c[:, 2, 3:4], scale=bn_c[:, 2, 2:3]).then_inc(st["x1"]["z"], 1)

            act.wait_ge(bn_in, 1)
            affine_cols(0)
            with act.Fori(0, STEPS - 1) as i:
                act.wait_ge(st["x1"]["t"], i + 1)
                affine_cols(i + 1)

            def ln_sqrt(k):
                act.wait_ge(mv_done, k)
                act.activation(sd[:, :], mv[:, 1, :], ACT.Sqrt,
                               bias=eps_col[:, :]).then_inc(sd_done, 1)

            def stage_gather(layer, i, r):
                b = i * RING + r
                act.wait_ge(products, b + (layer * BATCHES + 1))
                word = P_SRCT if layer == 2 else P_SRC
                act.copy(idx_gather[:, r, :], ordered[:, bass.ds(b * CH, CH), word:word + 1].rearrange(
                    "p c a -> p (c a)")).then_inc(idx_ready, 1)
                if layer == 1:
                    act.copy(node_rows[:, r, :, D:AW],
                             ordered[:, bass.ds(b * CH, CH), P_ONE:PAY]).then_inc(extras_ready, 1)

            def stage_rest(layer):
                with act.Fori(1, RROUNDS) as i:
                    for r in range(RING):
                        stage_gather(layer, i, r)

            def copy_all(stage, per=1):
                copy_t(stage, 0)
                with act.Fori(0, STEPS - 1) as i:
                    act.wait_ge(st[stage]["m"], i * per + per)
                    copy_t(stage, i + 1)

            ln_sqrt(1)
            act.wait_ge(ordered_in, 16)
            for r in range(RING):
                stage_gather(1, 0, r)
            stage_rest(1)
            act.wait_ge(deg_ready, 1)
            act.activation(deg[:, 2, :], deg[:, 1, :], ACT.Sqrt).then_inc(deg_sd, 1)
            copy_all("f1")
            ln_sqrt(2)
            copy_all("g2", STEP)
            for r in range(RING):
                stage_gather(2, 0, r)
            copy_t("h2", 0)

            def copy_upd(i):
                for j in range(STEP):
                    act.wait_ge(st["h2"]["m"], i * STEP + (j + 1))
                    act.copy(Bt[:, bass.ds(i * STEP + j, 1), :].rearrange("p a d -> p (a d)"),
                             ps[:, WIDE_BANKS[j], TYPES * D:]).then_inc(upd_copied, 1)

            with act.Fori(0, STEPS - 1) as i:
                copy_upd(i)
                copy_t("h2", i + 1)
            copy_upd(STEPS - 1)
            stage_rest(2)
            copy_all("f2")
            ln_sqrt(3)
            with act.Fori(0, STEPS) as i:
                act.wait_ge(norm_ready, i + 1)
                v = B[:, bass.ds(i * (STEP * D), STEP * D)]
                act.activation(v, v, ACT.Gelu).then_inc(gelu_done, 1)
            ln_sqrt(4)
            copy_all("g3")
            for r in range(RING):
                stage_gather(3, 0, r)
            stage_rest(3)
            with act.Fori(0, STEPS) as i:
                act.wait_ge(raw_ready, i + 1)
                v = B[:, bass.ds(i * (STEP * D), STEP * D)]
                act.activation(v, v, ACT.Relu).then_inc(relu_done, 1)
            with act.Fori(0, STEPS) as i:
                act.wait_ge(dev_ready, i + 1)
                act.activation(A[:, bass.ds(i * (STEP * D), STEP * D)],
                               B[:, bass.ds(i * (STEP * D), STEP * D)], ACT.Square).then_inc(sq_ready, 1)
            act.wait_ge(rowsd_in, 1)
            act.activation(rowv[:, 2, :], rowv[:, 1, :], ACT.Sqrt, bias=eps_col[:, :]).then_inc(rowsd_out, 1)
            ln_sqrt(5)

        @block.tensor
        def _(pe):
            def count_sums(k):
                pe.matmul(ps[:, 7, 0:GROUPS], before[:, :], cnt[:, :], start=True, stop=True)
                pe.matmul(ps[:, 7, 2 * GROUPS:3 * GROUPS], ones[:, :], cnt[:, :], start=True,
                          stop=True).then_inc(counts_summed, 1)

            pe.sem_inc(products, RING)
            pe.wait_ge(consts, 7)
            pe.wait_ge(counted, GROUPS)
            count_sums(0)
            pe.wait_ge(w_in, 16 * W_LOADS)
            for k in range(6):
                if k:
                    pe.wait_ge(prep_out, k)
                pe.transpose(bank(6, D), wraw[:, k, :], ident[:, :]).then_inc(prep_t, 1)
            pe.wait_ge(prep_out, 6)
            pe.matmul(bank(6), ones[0:1, :], bc_src[0:1, 0:4, :].rearrange("a k d -> a (k d)"),
                      start=True, stop=True).then_inc(bc_done, 1)
            pe.wait_ge(bc_copied, 1)
            pe.matmul(bank(6, D), ones[0:1, :], bc_src[0:1, 4, :], start=True, stop=True).then_inc(bc_done, 1)
            pe.wait_ge(bc_copied, 2)
            pe.matmul(ps[:, 6, 0:1], wT[:, 2, :], cols[:, 0:1], start=True, stop=True).then_inc(bias0_done, 1)
            pe.wait_ge(bias0_out, 1)
            with pe.Fori(0, STEPS) as i:
                for j in range(STEP):
                    pe.wait_ge(prep_in, i * STEP + (j + 1))
                    pe.transpose(bank(6, D), zr[:, j, :], ident[:, :]).then_inc(xt_done, 1)
            pe.wait_ge(counted_dst, GROUPS)
            count_sums(1)

            def reduce(q):
                width = ONE + 1 if q == 0 else AW if q == 1 else D
                rows = slot_rows if q == 0 else node_rows
                with pe.Fori(0, RROUNDS) as i:
                    for r in range(RING):
                        b = i * RING + r
                        pe.wait_ge(onehot_ready, b + (q * BATCHES + 1))
                        pe.wait_ge(added, b * CH + (CH + q * CHUNKS))
                        if q == 1:
                            pe.wait_ge(extras_ready, b + 1)
                        if q == 0:
                            pe.wait_ge(slot_rows_in[r], i * 16 + 16)
                        else:
                            pe.wait_ge(gathered[r], i * (16 * CH) + ((q - 1) * RROUNDS + 1) * (16 * CH))
                        for j in range(CH):
                            ins = pe.matmul(product(r % 2, j, width), onehot[:, r % 2, j, :],
                                            rows[:, r, j, 0:width], start=True, stop=True)
                        ins.then_inc(products, 1)

            def turn(stage, i):
                for j in range(STEP):
                    pe.wait_ge(st[stage]["z"], i * STEP + (j + 1))
                    ins = pe.transpose(tslot(j), zr[:, j, :], ident[:, :])
                ins.then_inc(st[stage]["t"], 1)

            reduce(0)
            def mlp0(i):
                for h in range(2):
                    pe.matmul(bank(2 + h, HALF), wT[:, 0, :],
                              A[:, bass.ds(i * (2 * HALF) + h * HALF, HALF)], start=True, stop=False)
                    pe.matmul(bank(2 + h, HALF), wT[:, 1, :],
                              zt_flat[:, h * HALF:(h + 1) * HALF],
                              start=False, stop=True).then_inc(st["mlp0"]["m"], 1)

            turn("mlp0", 0)
            with pe.Fori(0, STEPS - 1) as i:
                pe.wait_ge(st["mlp0"]["c"], i + 1)
                turn("mlp0", i + 1)
                mlp0(i)
            pe.wait_ge(st["mlp0"]["c"], STEPS)
            mlp0(STEPS - 1)
            for k, stage in ((1, "mlp1"), (2, "mlp2")):
                def sublayer(i):
                    for h in range(2):
                        pe.matmul(bank(2 + h, HALF), wT[:, 2 + k, :],
                                  A[:, bass.ds(i * (2 * HALF) + h * HALF, HALF)],
                                  start=True, stop=True).then_inc(st[stage]["m"], 1)
                pe.wait_ge(bn_applied, k)
                sublayer(0)
                with pe.Fori(1, STEPS) as i:
                    pe.wait_ge(st[stage]["r"], i * 2)
                    sublayer(i)
            turn("x1", 0)
            with pe.Fori(1, STEPS) as i:
                pe.wait_ge(st["x1"]["r"], i)
                turn("x1", i)
            reduce(1)

            def dense(stage, w, bias, i):
                pe.wait_ge(st[stage]["c"], i + 1)
                for j in range(STEP):
                    ins = pe.matmul(tslot(j, 2), zt[:, j, :], w, start=True, stop=bias is None)
                    if bias is not None:
                        ins = pe.matmul(tslot(j, 2), ones[0:1, :], bias, start=False, stop=True)
                ins.then_inc(st[stage]["m"], 1)

            def dense_all(stage, w, bias=None):
                turn(stage, 0)
                with pe.Fori(0, STEPS - 1) as i:
                    pe.wait_ge(st[stage]["c"], i + 1)
                    turn(stage, i + 1)
                    dense(stage, w, bias, i)
                pe.wait_ge(st[stage]["r"], STEPS - 1)
                dense(stage, w, bias, STEPS - 1)

            def wide_all(stage, w, bias):
                def wide(i):
                    pe.wait_ge(st[stage]["c"], i + 1)
                    for j in range(STEP):
                        g1 = i * STEP + (j + 1)
                        pe.wait_ge(st[stage]["r"], g1)
                        n = w.shape[1]
                        ins = pe.matmul(bank(WIDE_BANKS[j], n), zt[:, j, :], w, start=True, stop=bias is None)
                        if bias is not None:
                            ins = pe.matmul(bank(WIDE_BANKS[j], n), ones[0:1, :], bias, start=False, stop=True)
                        ins.then_inc(st[stage]["m"], 1)

                turn(stage, 0)
                with pe.Fori(0, STEPS - 1) as i:
                    pe.wait_ge(st[stage]["c"], i + 1)
                    turn(stage, i + 1)
                    wide(i)
                wide(STEPS - 1)

            dense_all("f1", wT[:, 5, :], brows[0:1, 0:D])
            wide_all("g2", wcat[:, 0:TYPES, :].rearrange("p k d -> p (k d)"), None)
            wide_all("h2", wcat[:, TYPES:2 * TYPES + 1, :].rearrange("p k d -> p (k d)"),
                     brows[0:1, D:5 * D])
            reduce(2)
            dense_all("f2", wcat[:, 7, :])
            dense_all("g3", w3[:, :])
            reduce(3)

            def over_nodes(b, v):
                per = bank(b).shape[1]
                for k in range((GROUPS - 1) * D // per):
                    pe.matmul(bank(b), ones[:, :], v[:, k * per:(k + 1) * per], start=(k == 0), stop=False,
                              skip_group_check=True)
                return pe.matmul(bank(b, D), ones[0:LAST, :], v[0:LAST, (GROUPS - 1) * D:GROUPS * D],
                                 start=False, stop=True, skip_group_check=True)

            pe.wait_ge(relu_done, STEPS)
            over_nodes(0, B).then_inc(sum_h, 1)
            pe.wait_ge(sq_ready, STEPS)
            over_nodes(1, A).then_inc(sum_sq, 1)

        @block.vector
        def _(dve):
            chain = Chain(dve, chain_sem)
            mark, link, wait = chain.mark, chain.link, chain.wait

            def tile(v, g):
                return v[:, bass.ds(g, 1), :].rearrange("p a d -> p (a d)")

            dve.memset(src_i[:, MAIN:COLS], NO_NODE)
            dve.memset(dst_i[:, MAIN:COLS], NO_NODE)
            dve.memset(type_i[:, MAIN:COLS], 0)
            dve.memset(w_f[:, MAIN:COLS], 0.0)
            dve.memset(X[:, GROUPS - 1, :], 0.0).then_inc(pad_ready, 1)

            def split_key(key, lane1):
                mark(dve.tensor_scalar(tmp_i, key, SHIFT, None, ALU.arith_shift_right))
                link(dve.tensor_scalar(tmp2_i, key, P - 1, None, ALU.bitwise_and))
                mark(dve.tensor_copy(group_b, tmp_i))
                link(dve.tensor_scalar(lane1, tmp2_i, 1.0, None, ALU.add))

            def start_slots(k):
                link(dve.tensor_scalar(small[:, 0, :], ps[:, 7, 2 * GROUPS:3 * GROUPS], P - 1.0, None, ALU.add))
                link(dve.tensor_copy(small_i[:, :], small[:, 0, :]))
                link(dve.tensor_scalar(small_i[:, :], small_i[:, :], SHIFT, None, ALU.arith_shift_right))
                link(dve.tensor_copy(small[:, 1, :], small_i[:, :]))
                link(dve.tensor_tensor_scan(small[:, 2, :], small[:, 1, :], small[:, 1, :], 0.0,
                                            ALU.add, ALU.bypass))
                link(dve.tensor_tensor(small[:, 3, :], small[:, 2, :], small[:, 1, :], ALU.subtract))
                link(dve.scalar_tensor_tensor(out=small[:, 4, :], in0=small[:, 3, :], scalar=float(P),
                                              in1=ps[:, 7, 0:GROUPS], op0=ALU.mult, op1=ALU.add))
                link(dve.tensor_scalar(start_at[:, :], small[:, 4, :], -1.0, None, ALU.add))
                link(dve.tensor_tensor(below[:, :, :],
                                       small[0:BATCHES, 2:3, :].broadcast_to([BATCHES, CH, GROUPS]),
                                       chunk_ids[:, :, None].broadcast_to([BATCHES, CH, GROUPS]), ALU.is_le))
                link(dve.tensor_reduce(tile_of[:, :], below[:, :, :], AX_X, ALU.add))
                dve.tensor_scalar(at_cols[:, k, :], tile_of[:, :], GROUPS - 1.0, float(AW), ALU.min,
                                  ALU.mult).then_inc(cols_ready, 1)

            def rank(slot):
                link(dve.memset(pos, 0.0))
                scans = []
                for g in range(GROUPS + 1):
                    if g < GROUPS:
                        running = ps[:, 2 * (g % 3):2 * (g % 3) + 2, :].rearrange("p b n -> p (b n)")[:, 0:COLS]
                        scans.append((running, mark(dve.tensor_tensor_scan(
                            running, masks[:, g, :], masks[:, g, :], start_at[:, g:g + 1],
                            ALU.add, ALU.bypass))))
                    if g:
                        running, scanned = scans[g - 1]
                        wait(last if g > 1 else scanned)
                        last = mark(dve.copy_predicated(pos, masks[:, g - 1, :], running))
                wait(last)
                link(dve.tensor_copy(tmp_i, pos))
                link(dve.tensor_scalar(tmp2_i, tmp_i, P - 1, None, ALU.bitwise_and))
                link(dve.tensor_scalar(tmp_i, tmp_i, SHIFT, None, ALU.arith_shift_right))
                return dve.scalar_tensor_tensor(out=slot, in0=tmp2_i, scalar=float(CHUNKS), in1=tmp_i,
                                                op0=ALU.mult, op1=ALU.add)

            dve.wait_ge(keys_in, 32)
            dve.wait_ge(consts, 7)
            split_key(src_i, lane1_src)
            with dve.Fori(0, STEPS) as i:
                for j in range(STEP):
                    g = i * STEP + j
                    dve.tensor_scalar(tile(masks, g), group_b, group_ids[:, bass.ds(g, 1)], None,
                                      ALU.is_equal).then_inc(masks_made, 1)
            link(dve.scalar_tensor_tensor(out=pay[:, :, P_SRC], in0=tmp2_i, scalar=float(GROUPS), in1=tmp_i,
                                          op0=ALU.mult, op1=ALU.add))
            dve.wait_ge(counts_summed, 1)
            start_slots(0)
            link(rank(slot_src))
            dve.sem_inc(slots_ready, 1)
            dve.wait_ge(lists_in, 96)
            split_key(dst_i, pay[:, :, P_LANE1])
            with dve.Fori(0, STEPS) as i:
                for j in range(STEP):
                    g = i * STEP + j
                    dve.tensor_scalar(tile(masks, g), group_b, group_ids[:, bass.ds(g, 1)], 0.0,
                                      ALU.is_equal, ALU.add,
                                      accum_out=cnt[:, bass.ds(g, 1)]).then_inc(counted_dst, 1)
            dve.wait_ge(counts_summed, 2)
            start_slots(1)
            link(rank(slot_dst))
            dve.scalar_tensor_tensor(out=pay[:, :, P_SRCT], in0=pay[:, :, P_SRC], scalar=float(TYPES),
                                     in1=type_i, op0=ALU.mult, op1=ALU.add)
            dve.memset(pay[:, :, P_ONE], 1.0)
            for t in range(TYPES):
                dve.tensor_scalar(pay[:, :, P_TYPE + t], type_i, float(t), None, ALU.is_equal)
            dve.tensor_copy(pay[:, :, P_W], w_f).then_inc(pay_ready, 1)

            def one_hots(q, i, r):
                b = i * RING + r
                s = r % 2
                dve.wait_ge(products, b + (q * BATCHES + RING - 1))
                if q == 0:
                    dve.wait_ge(slot_rows_in[r % RING], i * 16 + (r // RING + 1) * 16)
                    lane1 = slot_rows[:, r % RING, :, LANE1:LANE1 + 1]
                else:
                    lane1 = ordered[:, bass.ds(b * CH, CH), P_LANE1:P_LANE1 + 1]
                if q < 3:
                    dve.tensor_tensor(onehot[:, s, :, :], lane_ids[:, None, :].broadcast_to([P, CH, P]),
                                      lane1.broadcast_to([P, CH, P]), ALU.is_equal).then_inc(onehot_ready, 1)
                    return
                for j in range(CH):
                    edge = ordered[:, bass.ds(b * CH + j, 1), :].rearrange("p a w -> p (a w)")
                    ins = dve.tensor_scalar(onehot[:, s, j, :], lane_ids[:, :], edge[:, P_LANE1:P_LANE1 + 1],
                                            edge[:, P_W:P_W + 1], ALU.is_equal, ALU.mult)
                ins.then_inc(onehot_ready, 1)

            def add_sums(q, i, r):
                b = i * RING + r
                width = ONE + 1 if q == 0 else AW if q == 1 else D
                at = nc.values_load_multi_w_load_instructions(
                    (at_src if q == 0 else at_dst)[0:1, bass.ds(b * CH, CH)], engines=[DVE],
                    min_val=0, max_val=(GROUPS - 1) * AW)[1]
                dve.wait_ge(products, b + (q * BATCHES + RING + 1))
                for j in range(CH):
                    dve.wait_ge(added, b * CH + (2 * CH + q * CHUNKS + j))
                    to = sums_flat[:, bass.ds(at[j], width)]
                    dve.tensor_tensor(to, to, product(r % 2, j, width), ALU.add).then_inc(added, 1)

            def reduce(q):
                one_hots(q, 0, 0)
                with dve.Fori(0, RROUNDS - 1) as i:
                    for r in range(RING):
                        one_hots(q, i, r + 1)
                        add_sums(q, i, r)
                for r in range(RING):
                    if r < RING - 1:
                        one_hots(q, RROUNDS - 1, r + 1)
                    add_sums(q, RROUNDS - 1, r)
                dve.wait_ge(added, 2 * CH + (q + 1) * CHUNKS)

            def each_step(first, then):
                first(0)
                with dve.Fori(0, STEPS - 1) as i:
                    first(i + 1)
                    then(i)
                then(STEPS - 1)

            def step_of(v, i):
                return v[:, bass.ds(i * STEP, STEP), :]

            def group_stats(v, i):
                for j in range(STEP):
                    g = i * STEP + j
                    dve.bn_stats(tile(stats, g), tile(v, g)).then_inc(stats_done, 1)

            ln_count = [0]

            def layer_norm_scale():
                ln_count[0] += 1
                dve.wait_ge(stats_done, GROUPS * ln_count[0])
                mean_e, mean_o, var_e, var_o = (stats[:, :, k] for k in (1, 4, 2, 5))
                mark(dve.tensor_tensor(mv[:, 0, :], mean_e, mean_o, ALU.add))
                mark(dve.tensor_tensor(sd[:, :], mean_e, mean_o, ALU.subtract))
                link(dve.tensor_tensor(mv[:, 1, :], var_e, var_o, ALU.add))
                mark(dve.scalar_tensor_tensor(out=sd[:, :], in0=sd[:, :], scalar=0.25, in1=sd[:, :],
                                              op0=ALU.mult, op1=ALU.mult))
                link(dve.tensor_scalar(mv[:, 0, :], mv[:, 0, :], 0.5, None, ALU.mult))
                dve.scalar_tensor_tensor(out=mv[:, 1, :], in0=mv[:, 1, :], scalar=1.0 / D, in1=sd[:, :],
                                         op0=ALU.mult, op1=ALU.add).then_inc(mv_done, 1)
                dve.wait_ge(sd_done, ln_count[0])
                link(dve.reciprocal(rstd[:, :], sd[:, :]))
                link(dve.scalar_tensor_tensor(out=nmr[:, :], in0=mv[:, 0, :], scalar=-1.0,
                                              in1=rstd[:, :], op0=ALU.mult, op1=ALU.mult))

            def normalised(to, v, g):
                return dve.tensor_scalar(to, tile(v, g), rstd[:, bass.ds(g, 1)], nmr[:, bass.ds(g, 1)],
                                         ALU.mult, ALU.add)

            dve.sem_inc(added, 2 * CH)
            link(dve.memset(sums_flat, 0.0))
            dve.wait_ge(at_in, 32)
            reduce(0)
            link(dve.tensor_scalar(sd[:, :], sums[:, :, ONE], 1.0, None, ALU.max))
            link(dve.reciprocal(rcnt[:, :], sd[:, :]))

            def edge_means(i):
                for j in range(STEP):
                    g = i * STEP + j
                    dve.tensor_scalar(zr[:, j, :], tile(sums, g)[:, 0:D], rcnt[:, bass.ds(g, 1)], None,
                                      ALU.mult).then_inc(st["mlp0"]["z"], 1)

            edge_means(0)
            with dve.Fori(1, STEPS) as i:
                dve.wait_ge(st["mlp0"]["t"], i)
                edge_means(i)
            dve.wait_ge(st["mlp0"]["z"], GROUPS)
            dve.memset(sums_flat, 0.0).then_inc(sums_zero, 1)
            for k, stage in enumerate(("mlp0", "mlp1", "mlp2")):
                dve.wait_ge(st[stage]["r"], 2 * STEPS)
                for n in range(NBN):
                    last = mark(dve.bn_stats(bn_st[:, n, :], A[:, n * BN_COLS:(n + 1) * BN_COLS]))
                wait(last)
                dve.bn_aggr(bn_mv[:, :], bn_st[:, :, :].rearrange("p n s -> p (n s)")).then_inc(bnsd_in, 1)
                dve.wait_ge(bnsd_out, k + 1)
                dve.wait_ge(bnsd_in, k + 1)
                c = bn_c[:, k, :]
                link(dve.reciprocal(c[:, 1:2], c[:, 0:1]))
                link(dve.tensor_tensor(c[:, 2:3], c[:, 1:2], cols[:, 4 + 2 * k:5 + 2 * k], ALU.mult))
                link(dve.tensor_tensor(c[:, 1:2], bn_mv[:, 0:1], c[:, 2:3], ALU.mult))
                ins = dve.tensor_tensor(c[:, 3:4], cols[:, 5 + 2 * k:6 + 2 * k], c[:, 1:2], ALU.subtract)
                if k == 2:
                    ins.then_inc(bn_in, 1)
                else:
                    link(ins)
                    dve.tensor_scalar(A[:, :], A[:, :], c[:, 2:3], c[:, 3:4], ALU.mult, ALU.add).then_inc(
                        bn_applied, 1)

            with dve.Fori(0, STEPS) as i:
                dve.wait_ge(st["x1"]["t"], i + 1)
                dve.tensor_tensor(step_of(X, i), step_of(X, i), grouped(tslots()), ALU.add).then_inc(
                    st["x1"]["r"], 1)
                dve.wait_ge(st["x1"]["r"], i + 1)
                group_stats(X, i)
            layer_norm_scale()
            with dve.Fori(0, STEPS) as i:
                for j in range(STEP):
                    g = i * STEP + j
                    normalised(tile(X, g), X, g).then_inc(x1_ready, 1)
            dve.wait_ge(x1_ready, GROUPS)

            dve.wait_ge(ordered_in, 16)
            dve.wait_ge(sums_zero, 1)
            reduce(1)
            mark(dve.tensor_scalar(sd[:, :], sums[:, :, D], 1.0, None, ALU.max))
            link(dve.tensor_scalar(deg[:, 0, :], sums[:, :, AW - 1], 1.0, None, ALU.add))
            mark(dve.tensor_scalar(deg[:, 1, :], deg[:, 0, :], 1e-30, None, ALU.max))
            link(dve.reciprocal(rcnt[:, :], sd[:, :]))
            dve.sem_inc(deg_ready, 1)
            for t in range(TYPES):
                mark(dve.tensor_tensor(ctype[:, t, :], sums[:, :, D + 1 + t], rcnt[:, :], ALU.mult))

            def f1_operands(i):
                if not first_of(i):
                    dve.wait_ge(st["f1"]["t"], i)
                for j in range(STEP):
                    g = i * STEP + j
                    dve.scalar_tensor_tensor(out=zr[:, j, :], in0=tile(sums, g)[:, 0:D],
                                             scalar=rcnt[:, bass.ds(g, 1)], in1=tile(X, g),
                                             op0=ALU.mult, op1=ALU.add).then_inc(st["f1"]["z"], 1)

            def f1_results(i):
                dve.wait_ge(st["f1"]["m"], i + 1)
                dve.scalar_tensor_tensor(out=step_of(X, i), in0=grouped(tslots(2)), scalar=0.0,
                                         in1=step_of(X, i), op0=ALU.max, op1=ALU.add).then_inc(
                    st["f1"]["r"], 1)
                dve.wait_ge(st["f1"]["r"], i + 1)
                group_stats(X, i)

            each_step(f1_operands, f1_results)
            layer_norm_scale()
            dve.wait_ge(deg_sd, 1)
            link(dve.reciprocal(dinv[:, :], deg[:, 2, :]))
            link(dve.scalar_tensor_tensor(out=dinv[:, :], in0=deg[:, 0, :], scalar=0.0, in1=dinv[:, :],
                                          op0=ALU.is_gt, op1=ALU.mult))

            def normalised_operands(stage):
                def operands(i):
                    if not first_of(i):
                        dve.wait_ge(st[stage]["t"], i)
                    for j in range(STEP):
                        g = i * STEP + j
                        normalised(zr[:, j, :], X, g).then_inc(st[stage]["z"], 1)
                    for j in range(STEP):
                        g = i * STEP + j
                        dve.wait_ge(st[stage]["z"], g + 1)
                        normalised(tile(X, g), X, g).then_inc(x_normed, 1)
                return operands

            def g2_results(i):
                if not first_of(i):
                    dve.wait_ge(msg_out, i * 16)
                for j in range(STEP):
                    dve.wait_ge(st["g2"]["m"], i * STEP + (j + 1))
                    dve.tensor_copy(msgs[:, j, :], bank(WIDE_BANKS[j], TYPES * D)).then_inc(st["g2"]["r"], 1)

            dve.sem_inc(st["g2"]["r"], NEAR)
            operands = normalised_operands("g2")
            operands(0)
            operands(1)
            g2_results(0)
            with dve.Fori(1, STEPS - 1) as i:
                operands(i + 1)
                g2_results(i)
            g2_results(STEPS - 1)
            dve.wait_ge(x_normed, GROUPS)

            dve.sem_inc(st["h2"]["r"], NEAR)

            def h2_operands(i):
                if not first_of(i):
                    dve.wait_ge(st["h2"]["t"], i)
                for j in range(STEP):
                    g = i * STEP + j
                    dve.tensor_copy(zr[:, j, :], tile(X, g)).then_inc(st["h2"]["z"], 1)

            def h2_results(i):
                for js in (range(0, 3), range(3, 6), range(6, 7)):
                    marks = {}
                    for t in range(TYPES):
                        for j in js:
                            g = i * STEP + j
                            part = ps[:, WIDE_BANKS[j], t * D:(t + 1) * D]
                            share = ctype[:, t, bass.ds(g, 1)]
                            if t == 0:
                                dve.wait_ge(upd_copied, g + 1)
                                marks[j] = mark(dve.tensor_scalar(tile(At, g), part, share, None, ALU.mult))
                            else:
                                wait(marks[j])
                                ins = dve.scalar_tensor_tensor(out=tile(At, g), in0=part, scalar=share,
                                                               in1=tile(At, g), op0=ALU.mult, op1=ALU.add)
                                if t == 1:
                                    marks[j] = mark(ins)
                                else:
                                    ins.then_inc(st["h2"]["r"], 1)

            h2_operands(0)
            with dve.Fori(0, STEPS - 1) as i:
                chain.enter(i, 2 * STEP)
                h2_operands(i + 1)
                h2_results(i)
                chain.leave(STEPS - 1)
            h2_results(STEPS - 1)
            dve.wait_ge(st["h2"]["r"], NEAR + GROUPS)
            dve.wait_ge(sums_zero2, 1)
            reduce(2)

            def f2_operands(i):
                if not first_of(i):
                    dve.wait_ge(st["f2"]["t"], i)
                for j in range(STEP):
                    g = i * STEP + j
                    dve.scalar_tensor_tensor(out=zr[:, j, :], in0=tile(sums, g)[:, 0:D],
                                             scalar=rcnt[:, bass.ds(g, 1)], in1=tile(At, g),
                                             op0=ALU.mult, op1=ALU.add).then_inc(st["f2"]["z"], 1)

            def f2_results(i):
                dve.wait_ge(st["f2"]["m"], i + 1)
                dve.tensor_tensor(step_of(Bt, i), grouped(tslots(2)), step_of(Bt, i), ALU.add).then_inc(
                    st["f2"]["r"], 1)
                dve.wait_ge(st["f2"]["r"], i + 1)
                group_stats(Bt, i)

            each_step(f2_operands, f2_results)
            layer_norm_scale()

            def bcast(k):
                return bc[:, k:k + 1, :].broadcast_to([P, STEP, D])

            def norm_affine(i):
                for j in range(STEP):
                    g = i * STEP + j
                    last = mark(normalised(tile(Bt, g), Bt, g))
                wait(last)
                link(dve.tensor_tensor(step_of(Bt, i), step_of(Bt, i), bcast(0), ALU.mult))
                dve.tensor_tensor(step_of(Bt, i), step_of(Bt, i), bcast(1), ALU.add).then_inc(norm_ready, 1)

            def add_gelu(i):
                dve.wait_ge(gelu_done, i + 1)
                link(dve.scalar_tensor_tensor(out=step_of(X, i), in0=step_of(X, i), scalar=2.0,
                                              in1=step_of(Bt, i), op0=ALU.mult, op1=ALU.add))
                group_stats(X, i)

            norm_affine(0)
            with dve.Fori(0, STEPS - 1) as i:
                chain.enter(i, STEP + 2)
                norm_affine(i + 1)
                add_gelu(i)
                chain.leave(STEPS - 1)
            add_gelu(STEPS - 1)
            layer_norm_scale()

            def g3_results(i):
                dve.wait_ge(st["g3"]["m"], i + 1)
                for j in range(STEP):
                    g = i * STEP + j
                    ins = dve.tensor_scalar(tile(At, g), tslot(j, 2), dinv[:, bass.ds(g, 1)], None, ALU.mult)
                ins.then_inc(st["g3"]["r"], 1)

            each_step(normalised_operands("g3"), g3_results)
            dve.wait_ge(x_normed, 2 * GROUPS)
            dve.wait_ge(st["g3"]["r"], STEPS)
            link(dve.tensor_tensor(X[:, :, :], X[:, :, :], bc[:, 4:5, :].broadcast_to([P, GROUPS, D]), ALU.add))
            dve.wait_ge(sums_zero2, 2)
            reduce(3)
            with dve.Fori(0, STEPS) as i:
                chain.enter(i, STEP + 1)
                link(dve.tensor_tensor(step_of(Bt, i), step_of(sums, i)[:, :, 0:D], step_of(At, i), ALU.add))
                for j in range(STEP):
                    g = i * STEP + j
                    last = mark(dve.scalar_tensor_tensor(out=tile(Bt, g), in0=tile(Bt, g),
                                                         scalar=dinv[:, bass.ds(g, 1)], in1=bc[:, 2, :],
                                                         op0=ALU.mult, op1=ALU.add))
                wait(last)
                chain.leave(STEPS)
                dve.sem_inc(raw_ready, 1)

            def over_banks(b, to):
                link(dve.tensor_reduce(to, bank(b).rearrange("p (k d) -> p d k", k=4), AX_X, ALU.add))
                link(dve.tensor_scalar(to, to, 1.0 / N, None, ALU.mult))

            dve.wait_ge(sum_h, 1)
            over_banks(0, rowv[:, 0, :])
            with dve.Fori(0, STEPS) as i:
                dve.tensor_tensor(step_of(Bt, i), step_of(Bt, i), rowv[:, 0:1, :].broadcast_to([P, STEP, D]),
                                  ALU.subtract).then_inc(dev_ready, 1)
            dve.wait_ge(sum_sq, 1)
            over_banks(1, rowv[:, 1, :])
            dve.sem_inc(rowsd_in, 1)
            dve.wait_ge(rowsd_out, 1)
            link(dve.reciprocal(rowv[:, 3, :], rowv[:, 2, :]))
            link(dve.tensor_tensor(rowv[:, 4, :], rowv[:, 3, :], bc[:, 3, :], ALU.mult))
            with dve.Fori(0, STEPS) as i:
                chain.enter(i, 2)
                link(dve.tensor_tensor(step_of(Bt, i), step_of(Bt, i),
                                       rowv[:, 4:5, :].broadcast_to([P, STEP, D]), ALU.mult))
                link(dve.tensor_tensor(step_of(X, i), step_of(X, i), step_of(Bt, i), ALU.add))
                group_stats(X, i)
                chain.leave(STEPS)
            layer_norm_scale()
            with dve.Fori(0, STEPS) as i:
                for j in range(STEP):
                    g = i * STEP + j
                    normalised(tile(X, g), X, g).then_inc(y_ready, 1)


_INS = ["x", "src", "dst", "edge_attr_128", "edge_type_3", "edge_weight",
        "L0_gnn_u", "L0_gnn_W0", "L0_gnn_b0", "L0_gnn_W1", "L0_gnn_b1", "L0_gnn_W2", "L0_gnn_b2",
        "L0_gnn_g0", "L0_gnn_bt0", "L0_gnn_g1", "L0_gnn_bt1", "L0_gnn_g2", "L0_gnn_bt2",
        "L1_gnn_W", "L1_gnn_b", "L2_gnn_Wmsg", "L2_gnn_bmsg", "L2_gnn_Wupd", "L2_gnn_bupd",
        "L2_gnn_gamma", "L2_gnn_beta", "L3_gnn_W", "L3_gnn_b", "L3_gnn_gamma", "L3_gnn_beta"]


def kernel(**inputs):
    import numpy as _np
    import concourse.bacc as _bacc
    from concourse import mybir as _mybir
    from concourse.bass_utils import run_bass_kernel_spmd as _run

    nc = _bacc.Bacc("TRN2", target_bir_lowering=False, num_devices=1)
    arrays, args = {}, []
    for name in _INS:
        a = _np.ascontiguousarray(inputs[name])
        arrays[f"in_{name}"] = a
        args.append(nc.dram_tensor(f"in_{name}", a.shape, _mybir.dt.from_np(a.dtype), kind="ExternalInput").ap())
    args.append(nc.dram_tensor("out_nodes", (N, D), _mybir.dt.float32, kind="ExternalOutput").ap())
    gnn_kernel(nc, *args)
    r = _run(nc, [arrays], core_ids=[0])
    return r.results[0]["out_nodes"]
```

```python
from contextlib import ExitStack

import concourse.bass as bass
from concourse import mybir

ALU = mybir.AluOpType
ACT = mybir.ActivationFunctionType
AX_X = mybir.AxisListType.X
F32 = mybir.dt.float32
BF16 = mybir.dt.bfloat16
I32 = mybir.dt.int32
U32 = mybir.dt.uint32
U8 = mybir.dt.uint8
DVE = mybir.EngineType.DVE

P = 128
N = 6250
E = 100000
D = 128
TYPES = 3
GROUPS = -(-N // P)
LAST = N - (GROUPS - 1) * P
STEP = 7
STEPS = GROUPS // STEP
SHIFT = 7
NO_NODE = 63 * P

BATCH = 10
SRING = 3
FIRST_ROUNDS = 4
MAIN = 780
TAIL_LANES = 80
TAIL = 2
COLS = MAIN + TAIL
ROUNDS = MAIN // (BATCH * SRING)
assert P * MAIN + TAIL_LANES * TAIL == E and ROUNDS * BATCH * SRING == MAIN

CH = 8
RING = 4
CHUNKS = 832
BATCHES = CHUNKS // CH
RROUNDS = BATCHES // RING
assert (E + GROUPS * (P - 1)) // P <= CHUNKS and RROUNDS * RING * CH == CHUNKS

ROW = D + 2
ONE, LANE1 = D, D + 1
PAY = 8
P_SRC, P_SRCT, P_LANE1, P_ONE, P_TYPE, P_W = 0, 1, 2, 3, 4, 7
EXTRA = PAY - P_ONE
AW = D + EXTRA
HALF = STEP * P // 2
FULL = -(-E // P)
COUNT_SPLIT = 4
EPS = 1e-5
NEAR = 3
WIDE_BANKS = (2, 3, 4, 5, 6, 7, 5)
OWN_SETS = (GROUPS - 1) // 2
BN_COLS = 250
NBN = N // BN_COLS


def first_of(i):
    return isinstance(i, int) and i == 0


class Chain:

    def __init__(self, eng, sem):
        self.eng, self.sem, self.n, self.at = eng, sem, 0, None

    def mark(self, ins):
        self.n += 1
        ins.then_inc(self.sem, 1)
        return self.n if self.at is None else self.at + (self.n - self.start)

    def last(self):
        return self.n if self.at is None else self.at + (self.n - self.start)

    def wait(self, value):
        self.eng.wait_ge(self.sem, value)

    def link(self, ins):
        self.wait(self.mark(ins))

    def enter(self, i, per):
        self.start, self.per, self.at = self.n, per, i * per + self.n

    def leave(self, turns):
        assert self.n - self.start == self.per, (self.n - self.start, self.per)
        self.n = self.start + self.per * turns
        self.at = None


def gnn_kernel(nc, x, src, dst, edge_attr, edge_type, edge_weight, u, W0, b0, W1, b1, W2, b2,
               g0, bt0, g1, bt1, g2, bt2, L1W, L1b, Wmsg, bmsg, Wupd, bupd, gam2, bet2,
               W3, b3, gam3, bet3, out):
    with ExitStack() as ctx:
        def sb(name, shape, dt=F32):
            return ctx.enter_context(nc.sbuf_tensor(name, shape, dt))

        def sem(name):
            return ctx.enter_context(nc.semaphore(name))

        def dram(name, shape, dt=F32):
            return nc.dram_tensor(name, shape, dt).ap()

        slots_src = dram("slots_src", [P, CHUNKS, ROW])
        slots_dst = dram("slots_dst", [P, CHUNKS, PAY])
        sums_at_src = dram("sums_at_src", [BATCHES, CH], I32)
        sums_at_dst = dram("sums_at_dst", [BATCHES, CH], I32)
        x1_table = dram("x1_table", [P, GROUPS, D])
        msg_table = dram("msg_table", [P, GROUPS, TYPES * D])
        z_table = dram("z_table", [P, GROUPS, D])

        X = sb("X", [P, GROUPS, D])
        A = sb("A", [P, GROUPS * D])
        masks_raw = sb("masks_raw", [P, 9600])
        lists_raw = sb("lists_raw", [P, 11 * COLS])
        pay_raw = sb("pay_raw", [P, CHUNKS * PAY])
        rows_raw = sb("rows_raw", [P, RING * CH * AW])
        zr = sb("zr", [P, STEP, D])
        zt = sb("zt", [P, STEP, D])
        idx_scatter = sb("idx_scatter", [P, SRING, BATCH], U32)
        idx_gather = sb("idx_gather", [P, RING, CH], U32)
        idx_tail = sb("idx_tail", [P, 2, TAIL], U32)
        pay_stage = sb("pay_stage", [P, SRING, BATCH * PAY])
        tail_rows = sb("tail_rows", [P, TAIL, ROW])
        at_src = sb("at_src", [1, CHUNKS], I32)
        at_dst = sb("at_dst", [1, CHUNKS], I32)

        masks = masks_raw[:, :].bitcast(U8)[:, 0:GROUPS * COLS].rearrange("p (b c) -> p b c", c=COLS)
        sums_flat = masks_raw[:, 0:GROUPS * AW]
        sums = sums_flat.rearrange("p (g w) -> p g w", w=AW)
        onehot = masks_raw[:, GROUPS * AW:GROUPS * AW + 2 * CH * P].rearrange(
            "p (s j n) -> p s j n", s=2, j=CH)
        assert GROUPS * AW + 2 * CH * P <= 9600 and GROUPS * COLS <= 4 * 9600

        def listed(k, dt=F32):
            v = lists_raw[:, k * COLS:(k + 1) * COLS]
            return v if dt == F32 else v.bitcast(dt)
        src_i, dst_i, type_i, w_f = listed(0, I32), listed(1, I32), listed(2, I32), listed(3)
        lane1_src, pos = listed(4), listed(5)
        tmp_i, tmp2_i = listed(6, I32), listed(7, I32)
        group_b = lists_raw[:, 8 * COLS:8 * COLS + COLS // 2].bitcast(BF16)
        slot_src, slot_dst = listed(9), listed(10)
        B = lists_raw[:, 0:GROUPS * D]
        At = A[:, :].rearrange("p (g d) -> p g d", d=D)
        Bt = B.rearrange("p (g d) -> p g d", d=D)

        pay = pay_raw[:, 0:COLS * PAY].rearrange("p (c w) -> p c w", w=PAY)
        ordered = pay_raw[:, :].rearrange("p (k w) -> p k w", w=PAY)
        zeros = rows_raw[:, 0:CHUNKS * PAY // 2]
        edge_rows = rows_raw[:, 0:SRING * BATCH * ROW].rearrange("p (s c w) -> p s c w", s=SRING, c=BATCH)
        slot_rows = rows_raw[:, 0:RING * CH * ROW].rearrange("p (s c w) -> p s c w", s=RING, c=CH)
        node_rows = rows_raw[:, :].rearrange("p (s c w) -> p s c w", s=RING, c=CH)
        msgs = rows_raw[:, 0:STEP * TYPES * D].rearrange("p (j f) -> p j f", j=STEP)

        lane_ids = sb("lane_ids", [P, P])
        group_ids = sb("group_ids", [P, GROUPS])
        chunk_ids = sb("chunk_ids", [BATCHES, CH])
        ident = sb("ident", [P, P])
        before = sb("before", [P, P])
        ones = sb("ones", [P, P])
        eps_col = sb("eps_col", [P, 1])
        cnt = sb("cnt", [P, GROUPS])
        small = sb("small", [P, 6, GROUPS])
        small_i = sb("small_i", [P, GROUPS], I32)
        start_at = sb("start_at", [P, GROUPS])
        below = sb("below", [BATCHES, CH, GROUPS])
        tile_of = sb("tile_of", [BATCHES, CH])
        at_cols = sb("at_cols", [BATCHES, 2, CH], I32)
        stats = sb("stats", [P, GROUPS, 6])
        mv = sb("mv", [P, 2, GROUPS])
        sd = sb("sd", [P, GROUPS])
        rstd = sb("rstd", [P, GROUPS])
        nmr = sb("nmr", [P, GROUPS])
        rcnt = sb("rcnt", [P, GROUPS])
        ctype = sb("ctype", [P, TYPES, GROUPS])
        dinv = sb("dinv", [P, GROUPS])
        deg = sb("deg", [P, 3, GROUPS])
        wraw = zt[:, 0:6, :]
        wT = sb("wT", [P, 6, D])
        wcat = sb("wcat", [P, 8, D])
        w3 = sb("w3", [P, D])
        cols = sb("cols", [P, 10])
        l1b_row = sb("l1b_row", [1, D])
        bc_src = A[0:1, 0:9 * D]
        bc = sb("bc", [P, 9, D])
        zero_row = sb("zero_row", [P, ROW])
        last_chunk = sb("last_chunk", [P, STEPS, STEP + 1], I32)
        bias0 = sb("bias0", [P, 1])
        bn_st = sb("bn_st", [P, NBN, 6])
        bn_mv = sb("bn_mv", [P, 2])
        bn_c = sb("bn_c", [P, 3, 4])
        rowv = sb("rowv", [P, 5, D])

        ps = ctx.enter_context(nc.psum_tensor("ps", [P, 8, 512], F32))

        def bank(b, n=512):
            return ps[:, b, 0:n]

        keys_in, lists_in, x_in, w_in, tail_in = (sem(s) for s in (
            "keys_in", "lists_in", "x_in", "w_in", "tail_in"))
        zero_ready, zero_done, consts, gp_ones = (sem(s) for s in (
            "zero_ready", "zero_done", "consts", "gp_ones"))
        chain_sem = sem("vector_chain")
        pad_ready, masks_made, counted, counts_summed = (sem(s) for s in (
            "pad_ready", "masks_made", "counted", "counts_summed"))
        cols_ready, at_out, at_in = sem("cols_ready"), sem("at_out"), sem("at_in")
        slots_ready, pay_ready = sem("slots_ready"), sem("pay_ready")
        prep_in, prep_t, prep_out, bc_done, bc_copied, bias0_done, bias0_out = (sem(s) for s in (
            "prep_in", "prep_t", "prep_out", "bc_done", "bc_copied", "bias0_done", "bias0_out"))
        edge_rows_in = [sem(f"edge_rows_in{r}") for r in range(SRING)]
        staged_a, staged_b, staged_tail = sem("staged_a"), sem("staged_b"), sem("staged_tail")
        issued = sem("issued")
        scattered_a = [sem(f"scattered_a{r}") for r in range(SRING)]
        scattered_b = [sem(f"scattered_b{r}") for r in range(SRING)]
        tail_a, tail_b = sem("tail_a"), sem("tail_b")
        slot_rows_in = [sem(f"slot_rows_in{r}") for r in range(RING)]
        gathered = [sem(f"gathered{r}") for r in range(RING)]
        first_in, ordered_in, last_zero = sem("first_in"), sem("ordered_in"), sem("last_zero")
        sums_zero = sem("sums_zero")
        onehot_ready, products, added = sem("onehot_ready"), sem("products"), sem("added")
        idx_ready, extras_ready = sem("idx_ready"), sem("extras_ready")
        st = {s: {k: sem(f"{s}_{k}") for k in "ztcmr"} for s in
              ("mlp0", "mlp1", "mlp2", "x1", "f1", "g2", "h2", "f2", "g3", "f3")}
        bn_in = sem("bn_in")
        mv_done, sd_done = sem("mv_done"), sem("sd_done")
        bnsd_in, bnsd_out = sem("bnsd_in"), sem("bnsd_out")
        x1_ready, x1_out, msg_out, z_out, y_ready, y_out = (sem(s) for s in (
            "x1_ready", "x1_out", "msg_out", "z_out", "y_ready", "y_out"))
        counted_dve, bn_applied, stats_done, x_normed, sums_zero2 = (sem(s) for s in (
            "counted_dve", "bn_applied", "stats_done", "x_normed", "sums_zero2"))
        xt_done, xt_copied = sem("xt_done"), sem("xt_copied")
        norm_ready, gelu_done = sem("norm_ready"), sem("gelu_done")
        deg_ready, deg_sd = sem("deg_ready"), sem("deg_sd")
        sum_h, sq_ready, sum_sq, dev_ready = (sem(s) for s in ("sum_h", "sq_ready", "sum_sq", "dev_ready"))
        scale_ready, b_normed = sem("scale_ready"), sem("b_normed")
        raw_ready, relu_done = sem("raw_ready"), sem("relu_done")
        rowsd_in, rowsd_out = sem("rowsd_in"), sem("rowsd_out")

        block = ctx.enter_context(nc.Block())

        def tslot(j, base=0):
            return ps[:, base + j // 4, (j % 4) * D:(j % 4 + 1) * D]

        def tslots(base=0):
            return ps[:, base:base + 2, :].rearrange("p b n -> p (b n)")[:, 0:STEP * D]

        def grouped(v):
            return v.rearrange("p (j d) -> p j d", d=D)

        zt_flat = zt[:, :, :].rearrange("p j d -> p (j d)")

        def product(s, j, width):
            if width == D:
                return ps[:, 2 * s + j // 4, (j % 4) * D:(j % 4 + 1) * D]
            return ps[:, 4 * s + j // 2, (j % 2) * AW:(j % 2) * AW + width]

        def last_edges(a):
            return a[P * MAIN:E].rearrange("(p c) -> p c", p=TAIL_LANES)

        def main_edges(a):
            return a[0:P * MAIN].rearrange("(p c) -> p c", p=P)

        attr_main = edge_attr[0:P * MAIN, :].rearrange("(p c) d -> p c d", p=P)
        attr_tail = edge_attr[P * MAIN:E, :].rearrange("(p c) d -> p c d", p=TAIL_LANES)

        def col(v):
            return v.rearrange("(d a) -> d a", a=1)

        def row(v):
            return v.rearrange("(a d) -> a d", a=1)

        def by_group(v):
            return (v[0:(GROUPS - 1) * P, :].rearrange("(g p) d -> p g d", p=P),
                    v[(GROUPS - 1) * P:N, :])

        @block.sync
        def _(sp):
            sp.dma_start(src_i[:, 0:MAIN], main_edges(src)).then_inc(keys_in, 16)
            sp.wait_ge(pad_ready, 1)
            sp.dma_start(src_i[0:TAIL_LANES, MAIN:COLS], last_edges(src)).then_inc(keys_in, 16)
            for dst_t, s in ((dst_i, dst), (type_i, edge_type), (w_f, edge_weight)):
                sp.dma_start(dst_t[:, 0:MAIN], main_edges(s)).then_inc(lists_in, 16)
                sp.dma_start(dst_t[0:TAIL_LANES, MAIN:COLS], last_edges(s)).then_inc(lists_in, 16)
            full, last = by_group(x)
            sp.dma_start(X[:, 0:GROUPS - 1, :], full).then_inc(x_in, 16)
            sp.dma_start(X[0:LAST, GROUPS - 1, :], last).then_inc(x_in, 16)
            sp.dma_start(wraw[:, 0:3, :], W0.rearrange("o (k i) -> o k i", k=3)).then_inc(w_in, 16)
            for k, w in ((3, W1), (4, W2), (5, L1W)):
                sp.dma_start(wraw[:, k, :], w).then_inc(w_in, 16)
            for t in range(TYPES):
                for h in range(2):
                    sp.dma_start(wcat[:, TYPES * h + t, :], Wmsg[t, h * D:(h + 1) * D, :]).then_inc(w_in, 16)
            sp.dma_start(wcat[:, 6:8, :], Wupd.rearrange("(h i) o -> i h o", h=2)).then_inc(w_in, 16)
            sp.dma_start(w3[:, :], W3).then_inc(w_in, 16)
            sp.dma_start(cols[:, 0:1], u[0:1, :].rearrange("a d -> d a")).then_inc(w_in, 16)
            for k, v in enumerate((b0, b1, b2, g0, bt0, g1, bt1, g2, bt2)):
                sp.dma_start(cols[:, k + 1:k + 2], col(v)).then_inc(w_in, 16)
            sp.dma_start(l1b_row[0:1, :], row(L1b)).then_inc(w_in, 16)
            for k, v in enumerate((gam2, bet2, b3, gam3, bet3, bmsg[0], bmsg[1], bmsg[2], bupd)):
                sp.dma_start(bc_src[0:1, k * D:(k + 1) * D], row(v)).then_inc(w_in, 16)
            sp.dma_start(tail_rows[0:TAIL_LANES, :, 0:D], attr_tail).then_inc(tail_in, 16)
            sp.wait_ge(zero_ready, 2)
            half = CHUNKS * PAY // 2
            for k in range(2):
                sp.dma_start(slots_dst.rearrange("p c w -> p (c w)")[:, k * half:(k + 1) * half],
                             zeros[:, 0:half]).then_inc(zero_done, 16)
            half = (CHUNKS - FULL) // 2
            for k in range(2):
                sp.dma_start(slots_src[:, FULL + k * half:FULL + (k + 1) * half, :],
                             zeros[:, 0:half * ROW].rearrange("p (c w) -> p c w", w=ROW)).then_inc(zero_done, 16)
            sp.wait_ge(cols_ready, 1)
            sp.wait_ge(zero_done, 16 * 4)
            with sp.Fori(0, STEPS) as i:
                at = nc.values_load_multi_w_load_instructions(
                    last_chunk[0:1, bass.ds(i, 1), 0:STEP].rearrange("p a j -> p (a j)"),
                    engines=[mybir.EngineType.SP], min_val=0, max_val=CHUNKS - 1,
                    skip_runtime_bounds_check_because="a group ends at or before the last chunk")[1]
                for j in range(STEP):
                    sp.dma_start(slots_src[:, bass.ds(at[j], 1), :].rearrange("p a w -> p (a w)"),
                                 zero_row[:, :]).then_inc(last_zero, 16)
            sp.wait_ge(gp_ones, 1)
            def load_edge_rows(i, r):
                at = i * (SRING * BATCH) + r * BATCH
                sp.dma_start(edge_rows[:, r, :, 0:D], attr_main[:, bass.ds(at, BATCH), :]).then_inc(
                    edge_rows_in[r], 16)
            for r in range(SRING):
                load_edge_rows(0, r)
            with sp.Fori(1, ROUNDS) as i:
                for r in range(SRING):
                    sp.wait_ge(scattered_a[r], i * (16 * BATCH))
                    load_edge_rows(i, r)
            for k, (table, flat) in enumerate(((sums_at_src, at_src), (sums_at_dst, at_dst))):
                sp.wait_ge(cols_ready, k + 1)
                sp.dma_start(table, at_cols[:, k, :]).then_inc(at_out, 16)
                sp.wait_ge(at_out, 16 * (k + 1))
                sp.dma_start(flat[0:1, :], table.rearrange("b c -> (b c)").rearrange(
                    "(a k) -> a k", a=1)).then_inc(at_in, 16)
            for r in range(SRING):
                sp.wait_ge(scattered_a[r], 16 * BATCH * ROUNDS)
            sp.wait_ge(tail_a, 16 * TAIL)
            with sp.Fori(0, RROUNDS) as i:
                for r in range(RING):
                    sp.wait_ge(products, i * RING + (r + 1))
                    sp.dma_start(slot_rows[:, r, :, :],
                                 slots_src[:, bass.ds(i * (RING * CH) + r * CH, CH), :]).then_inc(
                        slot_rows_in[r], 16)
            for r in range(SRING):
                sp.wait_ge(scattered_b[r], 16 * BATCH * ROUNDS)
            sp.wait_ge(tail_b, 16 * TAIL)
            first = RING * CH
            sp.dma_start(ordered[:, 0:first, :], slots_dst[:, 0:first, :]).then_inc(first_in, 16)
            sp.dma_start(ordered[:, first:CHUNKS, :], slots_dst[:, first:CHUNKS, :]).then_inc(ordered_in, 16)
            sp.wait_ge(x1_ready, GROUPS)
            sp.dma_start(x1_table, X[:, :, :]).then_inc(x1_out, 16)
            with sp.Fori(0, STEPS) as i:
                sp.wait_ge(st["g2"]["r"], i * STEP + (STEP + NEAR))
                sp.dma_start(msg_table[:, bass.ds(i * STEP, STEP), :], msgs).then_inc(msg_out, 16)
            with sp.Fori(0, STEPS) as i:
                sp.wait_ge(st["g3"]["r"], i + 1)
                sp.dma_start(z_table[:, bass.ds(i * STEP, STEP), :],
                             At[:, bass.ds(i * STEP, STEP), :]).then_inc(z_out, 16)
            sp.wait_ge(y_ready, GROUPS)
            full, last = by_group(out)
            sp.dma_start(full, X[:, 0:GROUPS - 1, :]).then_inc(y_out, 16)
            sp.dma_start(last, X[0:LAST, GROUPS - 1, :]).then_inc(y_out, 16)
            sp.wait_ge(y_out, 32)

        @block.gpsimd
        def _(pool):
            pool.memset(zeros, 0.0).then_inc(zero_ready, 1)
            pool.memset(zero_row[:, :], 0.0).then_inc(zero_ready, 1)
            pool.iota(group_ids[:, :], [[1, GROUPS]], base=0, channel_multiplier=0,
                      allow_small_or_imprecise_dtypes=True).then_inc(consts, 1)
            pool.iota(lane_ids[:, :], [[1, P]], base=1, channel_multiplier=0,
                      allow_small_or_imprecise_dtypes=True).then_inc(consts, 1)
            pool.iota(chunk_ids[:, :], [[1, CH]], base=0, channel_multiplier=CH,
                      allow_small_or_imprecise_dtypes=True).then_inc(consts, 1)
            pool.memset(ones[:, :], 1.0).then_inc(consts, 1)
            pool.memset(eps_col[:, :], EPS).then_inc(consts, 1)
            pool.wait_ge(consts, 5)
            pool.affine_select(out=ident[:, :], in_=ones[:, :], pattern=[[-1, P]], base=0,
                               channel_multiplier=1, compare_op=ALU.is_equal, fill=0.0).then_inc(consts, 1)
            pool.affine_select(out=before[:, :], in_=ones[:, :], pattern=[[1, P]], base=0,
                               channel_multiplier=-1, compare_op=ALU.is_gt, fill=0.0).then_inc(consts, 1)
            pool.wait_ge(zero_done, 16 * 4)
            pool.memset(edge_rows[:, :, :, ONE:ONE + 1], 1.0).then_inc(gp_ones, 1)
            flat_src = slots_src.rearrange("p c w -> (p c) w")
            flat_dst = slots_dst.rearrange("p c w -> (p c) w")
            pool.wait_ge(last_zero, 16 * GROUPS)
            pool.sem_inc(issued, 1)
            with pool.Fori(0, ROUNDS) as i:
                for r in range(SRING):
                    pool.wait_ge(staged_a, i * SRING + (r + 1))
                    pool.sem_inc(issued, 1)
                    pool.wait_ge(edge_rows_in[r], i * 16 + 16)
                    pool.sem_inc(issued, 1)
                    for c in range(BATCH):
                        pool.indirect_dma_start(
                            flat_src, bass.IndirectOffsetOnAxis(idx_scatter[:, r, c:c + 1], 0),
                            edge_rows[:, r, c, :], None).then_inc(scattered_a[r], 16)
            pool.wait_ge(staged_tail, 1)
            for c in range(TAIL):
                pool.indirect_dma_start(
                    flat_src, bass.IndirectOffsetOnAxis(idx_tail[0:TAIL_LANES, 0, c:c + 1], 0),
                    tail_rows[0:TAIL_LANES, c, :], None).then_inc(tail_a, 16)
            def scatter_payloads(i, r):
                at = i * (SRING * BATCH) + r * BATCH
                pool.tensor_copy(idx_scatter[:, r, :], slot_dst[:, bass.ds(at, BATCH)])
                pool.tensor_copy(pay_stage[:, r, :],
                                 pay_raw[:, bass.ds(at * PAY, BATCH * PAY)]).then_inc(staged_b, 1)
                pool.wait_ge(staged_b, i * SRING + (r + 1))
                pool.sem_inc(issued, 1)
                for c in range(BATCH):
                    pool.indirect_dma_start(
                        flat_dst, bass.IndirectOffsetOnAxis(idx_scatter[:, r, c:c + 1], 0),
                        pay_stage[:, r, c * PAY:(c + 1) * PAY], None).then_inc(scattered_b[r], 16)

            for r in range(SRING):
                pool.wait_ge(scattered_a[r], 16 * BATCH * ROUNDS)
                pool.sem_inc(issued, 1)
                scatter_payloads(0, r)
            with pool.Fori(1, ROUNDS) as i:
                for r in range(SRING):
                    pool.wait_ge(scattered_b[r], i * (16 * BATCH))
                    pool.sem_inc(issued, 1)
                    scatter_payloads(i, r)
            for c in range(TAIL):
                pool.indirect_dma_start(
                    flat_dst, bass.IndirectOffsetOnAxis(idx_tail[0:TAIL_LANES, 1, c:c + 1], 0),
                    pay[0:TAIL_LANES, MAIN + c, :], None).then_inc(tail_b, 16)

            def gather(table, layer):
                with pool.Fori(0, RROUNDS) as i:
                    for r in range(RING):
                        pool.wait_ge(idx_ready, i * RING + ((layer - 1) * BATCHES + r + 1))
                        pool.sem_inc(issued, 1)
                        for c in range(CH):
                            pool.indirect_dma_start(
                                node_rows[:, r, c, 0:D], None, table,
                                bass.IndirectOffsetOnAxis(idx_gather[:, r, c:c + 1], 0)).then_inc(
                                gathered[r], 16)

            pool.wait_ge(x1_out, 16)
            gather(x1_table.rearrange("p g d -> (p g) d"), 1)
            pool.wait_ge(st["f1"]["z"], GROUPS)
            pool.memset(sums_flat, 0.0).then_inc(sums_zero2, 1)
            pool.wait_ge(msg_out, 16 * STEPS)
            gather(msg_table.rearrange("p g (t d) -> (p g t) d", t=TYPES), 2)
            pool.wait_ge(st["f2"]["z"], GROUPS)
            pool.memset(sums_flat, 0.0).then_inc(sums_zero2, 1)
            pool.wait_ge(z_out, 16 * STEPS)
            gather(z_table.rearrange("p g d -> (p g) d"), 3)

        W_LOADS = 1 + 3 + 2 * TYPES + 1 + 1 + 10 + 1 + 9

        @block.scalar
        def _(act):
            act.wait_ge(x_in, 32)
            with act.Fori(0, STEPS) as i:
                for j in range(COUNT_SPLIT, STEP):
                    act.wait_ge(masks_made, i * (STEP - COUNT_SPLIT) + (j + 1 - COUNT_SPLIT))
                    mask = masks[:, bass.ds(i * STEP + j, 1), :].rearrange("p a c -> p (a c)")
                    act.activation(mask, mask, ACT.Copy, accum_out=cnt[:, bass.ds(i * STEP + j, 1)]).then_inc(counted, 1)
            act.wait_ge(w_in, 16 * W_LOADS)
            for k in range(6):
                act.wait_ge(prep_t, k + 1)
                act.copy(wT[:, k, :], bank(6, D)).then_inc(prep_out, 1)
            for k in range(3):
                act.wait_ge(bc_done, k + 1)
                n = min(4, 9 - 4 * k)
                act.copy(bc[:, 4 * k:4 * k + n, :].rearrange("p k d -> p (k d)"), bank(6, n * D)).then_inc(
                    bc_copied, 1)
            act.wait_ge(bias0_done, 1)
            act.activation(bias0[:, :], ps[:, 6, 0:1], ACT.Identity, bias=cols[:, 1:2]).then_inc(bias0_out, 1)
            with act.Fori(0, STEPS) as i:
                for j in range(STEP):
                    g = i * STEP + j
                    act.copy(zr[:, j, :], X[:, bass.ds(g, 1), :].rearrange("p a d -> p (a d)")).then_inc(
                        prep_in, 1)
                    act.wait_ge(xt_done, g + 1)
                    act.copy(A[:, bass.ds(g * D, D)], bank(6, D)).then_inc(xt_copied, 1)

            def stage_a(i, r):
                at = i * (SRING * BATCH) + r * BATCH
                act.copy(idx_scatter[:, r, :], slot_src[:, bass.ds(at, BATCH)])
                act.copy(edge_rows[:, r, :, LANE1:LANE1 + 1].rearrange("p c a -> p (c a)"),
                         lane1_src[:, bass.ds(at, BATCH)]).then_inc(staged_a, 1)

            act.wait_ge(slots_ready, 1)
            act.wait_ge(gp_ones, 1)
            for r in range(SRING):
                stage_a(0, r)
            for part, ends in enumerate(((1, FIRST_ROUNDS), (FIRST_ROUNDS, ROUNDS))):
                act.wait_ge(slots_ready, part + 1)
                with act.Fori(*ends) as i:
                    for r in range(SRING):
                        act.wait_ge(scattered_a[r], i * (16 * BATCH))
                        stage_a(i, r)
            act.wait_ge(tail_in, 16)
            act.wait_ge(pay_ready, 1)
            act.copy(idx_tail[:, 0, :], slot_src[:, MAIN:COLS])
            act.copy(idx_tail[:, 1, :], slot_dst[:, MAIN:COLS])
            act.copy(tail_rows[:, :, ONE:ONE + 1].rearrange("p c a -> p (c a)"), ones[:, 0:TAIL])
            act.copy(tail_rows[:, :, LANE1:LANE1 + 1].rearrange("p c a -> p (c a)"),
                     lane1_src[:, MAIN:COLS]).then_inc(staged_tail, 1)

            def copy_t(stage, i):
                act.wait_ge(st[stage]["t"], i + 1)
                act.copy(zt_flat, tslots()).then_inc(st[stage]["c"], 1)

            def relu_cols(stage, i, bias):
                for h in range(2):
                    act.wait_ge(st[stage]["m"], i * 2 + (h + 1))
                    act.activation(A[:, bass.ds(i * (2 * HALF) + h * HALF, HALF)], bank(2 + h, HALF),
                                   ACT.Relu, bias=bias).then_inc(st[stage]["r"], 1)

            def bn_sqrt(k):
                act.wait_ge(bnsd_in, k + 1)
                act.activation(bn_c[:, k, 0:1], bn_mv[:, 1:2], ACT.Sqrt, bias=eps_col[:, :]).then_inc(
                    bnsd_out, 1)

            copy_t("mlp0", 0)
            with act.Fori(0, STEPS - 1) as i:
                relu_cols("mlp0", i, bias0[:, :])
                copy_t("mlp0", i + 1)
            relu_cols("mlp0", STEPS - 1, bias0[:, :])
            bn_sqrt(0)
            for k, stage in ((1, "mlp1"), (2, "mlp2")):
                with act.Fori(0, STEPS) as i:
                    relu_cols(stage, i, cols[:, k + 1:k + 2])
                bn_sqrt(k)

            def affine_cols(i):
                for j in range(STEP):
                    act.activation(zr[:, j, :], A[:, bass.ds((i * STEP + j) * D, D)], ACT.Identity,
                                   bias=bn_c[:, 2, 3:4], scale=bn_c[:, 2, 2:3]).then_inc(st["x1"]["z"], 1)

            act.wait_ge(bn_in, 1)
            affine_cols(0)
            with act.Fori(0, STEPS - 1) as i:
                act.wait_ge(st["x1"]["t"], i + 1)
                affine_cols(i + 1)

            def ln_sqrt(k):
                act.wait_ge(mv_done, k)
                act.activation(sd[:, :], mv[:, 1, :], ACT.Sqrt,
                               bias=eps_col[:, :]).then_inc(sd_done, 1)

            def stage_gather(layer, i, r):
                b = i * RING + r
                act.wait_ge(products, b + (layer * BATCHES + 1))
                word = P_SRCT if layer == 2 else P_SRC
                act.copy(idx_gather[:, r, :], ordered[:, bass.ds(b * CH, CH), word:word + 1].rearrange(
                    "p c a -> p (c a)")).then_inc(idx_ready, 1)
                if layer == 1:
                    act.copy(node_rows[:, r, :, D:AW],
                             ordered[:, bass.ds(b * CH, CH), P_ONE:PAY]).then_inc(extras_ready, 1)

            def stage_rest(layer):
                with act.Fori(1, RROUNDS) as i:
                    for r in range(RING):
                        stage_gather(layer, i, r)

            def copy_all(stage, per=1, then=None):
                copy_t(stage, 0)
                if then:
                    then(0)
                with act.Fori(0, STEPS - 1) as i:
                    act.wait_ge(st[stage]["m"], i * per + per)
                    copy_t(stage, i + 1)
                    if then:
                        then(i + 1)

            def normalise(v, i, ready, count, done):
                act.wait_ge(ready, i * count + count)
                for j in range(STEP):
                    g = i * STEP + j
                    t = v[:, bass.ds(g, 1), :].rearrange("p a d -> p (a d)")
                    act.activation(t, t, ACT.Identity, bias=nmr[:, bass.ds(g, 1)],
                                   scale=rstd[:, bass.ds(g, 1)]).then_inc(done, 1)

            ln_sqrt(1)
            act.wait_ge(first_in, 16)
            for r in range(RING):
                stage_gather(1, 0, r)
            act.wait_ge(ordered_in, 16)
            stage_rest(1)
            act.wait_ge(deg_ready, 1)
            act.activation(deg[:, 2, :], deg[:, 1, :], ACT.Sqrt).then_inc(deg_sd, 1)
            copy_all("f1")
            ln_sqrt(2)
            copy_all("g2", STEP, lambda i: normalise(X, i, st["g2"]["z"], STEP, x_normed))
            for r in range(RING):
                stage_gather(2, 0, r)
            def own_in(i, first, count=2):
                if not first_of(i):
                    act.wait_ge(st["h2"]["t"], i)
                for k in range(count):
                    ins = act.copy(zr[:, k, :], X[:, bass.ds(first + k, 1), :].rearrange("p a d -> p (a d)"))
                ins.then_inc(st["h2"]["z"], 1)

            def own_t(i, count=2):
                act.wait_ge(st["h2"]["t"], i + 1)
                if not first_of(i):
                    act.wait_ge(st["h2"]["m"], i)
                act.copy(zt_flat[:, 0:count * D], bank(4, count * D)).then_inc(st["h2"]["c"], 1)

            act.wait_ge(x_normed, GROUPS)
            own_in(0, 0, 1)
            own_t(0, 1)
            own_in(1, 1)
            with act.Fori(1, OWN_SETS) as i:
                stage_gather(2, i, 0)
                own_t(i)
                own_in(i + 1, i * 2 + 1)
                for r in range(1, RING):
                    stage_gather(2, i, r)
            stage_gather(2, OWN_SETS, 0)
            own_t(OWN_SETS)
            for r in range(1, RING):
                stage_gather(2, OWN_SETS, r)
            with act.Fori(OWN_SETS + 1, RROUNDS) as i:
                for r in range(RING):
                    stage_gather(2, i, r)
            copy_all("f2")
            ln_sqrt(3)
            def gelu(i):
                act.wait_ge(norm_ready, i + 1)
                v = B[:, bass.ds(i * (STEP * D), STEP * D)]
                act.activation(v, v, ACT.Gelu).then_inc(gelu_done, 1)

            def normalise_b(i):
                for j in range(STEP):
                    g = i * STEP + j
                    t = Bt[:, bass.ds(g, 1), :].rearrange("p a d -> p (a d)")
                    ins = act.activation(t, t, ACT.Identity, bias=nmr[:, bass.ds(g, 1)],
                                         scale=rstd[:, bass.ds(g, 1)])
                ins.then_inc(b_normed, 1)

            act.wait_ge(scale_ready, 1)
            normalise_b(0)
            with act.Fori(0, STEPS - 1) as i:
                normalise_b(i + 1)
                gelu(i)
            gelu(STEPS - 1)
            ln_sqrt(4)
            with act.Fori(0, STEPS) as i:
                normalise(X, i, st["g3"]["r"], 1, x_normed)
            for r in range(RING):
                stage_gather(3, 0, r)
            stage_rest(3)

            def relu_step(i):
                act.wait_ge(raw_ready, i + 1)
                v = B[:, bass.ds(i * (STEP * D), STEP * D)]
                act.activation(v, v, ACT.Relu).then_inc(relu_done, 1)

            copy_t("f3", 0)
            act.wait_ge(st["f3"]["m"], 1)
            copy_t("f3", 1)
            with act.Fori(1, STEPS - 1) as i:
                act.wait_ge(st["f3"]["m"], i + 1)
                copy_t("f3", i + 1)
                relu_step(i - 1)
            relu_step(STEPS - 2)
            relu_step(STEPS - 1)
            with act.Fori(0, STEPS) as i:
                act.wait_ge(dev_ready, i + 1)
                act.activation(A[:, bass.ds(i * (STEP * D), STEP * D)],
                               B[:, bass.ds(i * (STEP * D), STEP * D)], ACT.Square).then_inc(sq_ready, 1)
            act.wait_ge(rowsd_in, 1)
            act.activation(rowv[:, 2, :], rowv[:, 1, :], ACT.Sqrt, bias=eps_col[:, :]).then_inc(rowsd_out, 1)
            ln_sqrt(5)

        @block.tensor
        def _(pe):
            def count_sums(k):
                pe.matmul(ps[:, 7, 0:GROUPS], before[:, :], cnt[:, :], start=True, stop=True)
                pe.matmul(ps[:, 7, 2 * GROUPS:3 * GROUPS], ones[:, :], cnt[:, :], start=True,
                          stop=True).then_inc(counts_summed, 1)

            pe.sem_inc(products, RING)
            pe.wait_ge(consts, 7)
            pe.wait_ge(counted, STEPS * (STEP - COUNT_SPLIT))
            pe.wait_ge(counted_dve, STEPS * COUNT_SPLIT)
            count_sums(0)
            pe.wait_ge(w_in, 16 * W_LOADS)
            for k in range(6):
                if k:
                    pe.wait_ge(prep_out, k)
                pe.transpose(bank(6, D), wraw[:, k, :], ident[:, :]).then_inc(prep_t, 1)
            pe.wait_ge(prep_out, 6)
            for k in range(3):
                n = min(4, 9 - 4 * k) * D
                if k:
                    pe.wait_ge(bc_copied, k)
                pe.matmul(bank(6, n), ones[0:1, :], bc_src[0:1, 4 * k * D:4 * k * D + n],
                          start=True, stop=True).then_inc(bc_done, 1)
            pe.wait_ge(bc_copied, 3)
            pe.matmul(ps[:, 6, 0:1], wT[:, 2, :], cols[:, 0:1], start=True, stop=True).then_inc(bias0_done, 1)
            pe.wait_ge(bias0_out, 1)
            with pe.Fori(0, STEPS) as i:
                for j in range(STEP):
                    pe.wait_ge(prep_in, i * STEP + (j + 1))
                    pe.transpose(bank(6, D), zr[:, j, :], ident[:, :]).then_inc(xt_done, 1)
            pe.wait_ge(counted_dve, STEPS * COUNT_SPLIT + GROUPS)
            count_sums(1)

            def reduce(q):
                width = ONE + 1 if q == 0 else AW if q == 1 else D
                rows = slot_rows if q == 0 else node_rows
                def one_round(i, beside=None):
                    for r in range(RING):
                        b = i * RING + r
                        pe.wait_ge(onehot_ready, b + (q * BATCHES + 1))
                        pe.wait_ge(added, b * CH + (CH + q * CHUNKS))
                        if q == 1:
                            pe.wait_ge(extras_ready, b + 1)
                        if q == 0:
                            pe.wait_ge(slot_rows_in[r], i * 16 + 16)
                        else:
                            pe.wait_ge(gathered[r], i * (16 * CH) + ((q - 1) * RROUNDS + 1) * (16 * CH))
                        for j in range(CH):
                            ins = pe.matmul(product(r % 2, j, width), onehot[:, r % 2, j, :],
                                            rows[:, r, j, 0:width], start=True, stop=True)
                        ins.then_inc(products, 1)
                        if beside and r == 0:
                            own_turn(i + 1)
                        if beside and r == RING // 2:
                            own_wide(i + 1)

                if q == 2:
                    with pe.Fori(0, OWN_SETS) as i:
                        one_round(i, True)
                with pe.Fori(OWN_SETS if q == 2 else 0, RROUNDS) as i:
                    one_round(i)

            def own_turn(i, count=2):
                pe.wait_ge(st["h2"]["z"], i + 1)
                if not first_of(i):
                    pe.wait_ge(st["h2"]["c"], i)
                for k in range(count):
                    ins = pe.transpose(bank(4, count * D)[:, k * D:(k + 1) * D], zr[:, k, :], ident[:, :])
                ins.then_inc(st["h2"]["t"], 1)

            def own_wide(i, count=2):
                pe.wait_ge(st["h2"]["c"], i + 1)
                if not first_of(i):
                    pe.wait_ge(st["h2"]["r"], i)
                for k in range(count):
                    ins = pe.matmul(bank(5 + k), zt[:, k, :],
                                    wcat[:, TYPES:2 * TYPES + 1, :].rearrange("p k d -> p (k d)"),
                                    start=True, stop=True)
                ins.then_inc(st["h2"]["m"], 1)

            def turn(stage, i):
                for j in range(STEP):
                    pe.wait_ge(st[stage]["z"], i * STEP + (j + 1))
                    ins = pe.transpose(tslot(j), zr[:, j, :], ident[:, :])
                ins.then_inc(st[stage]["t"], 1)

            reduce(0)
            def mlp0(i):
                for h in range(2):
                    pe.matmul(bank(2 + h, HALF), wT[:, 0, :],
                              A[:, bass.ds(i * (2 * HALF) + h * HALF, HALF)], start=True, stop=False)
                    pe.matmul(bank(2 + h, HALF), wT[:, 1, :],
                              zt_flat[:, h * HALF:(h + 1) * HALF],
                              start=False, stop=True).then_inc(st["mlp0"]["m"], 1)

            turn("mlp0", 0)
            with pe.Fori(0, STEPS - 1) as i:
                pe.wait_ge(st["mlp0"]["c"], i + 1)
                turn("mlp0", i + 1)
                mlp0(i)
            pe.wait_ge(st["mlp0"]["c"], STEPS)
            mlp0(STEPS - 1)
            for k, stage in ((1, "mlp1"), (2, "mlp2")):
                def sublayer(i):
                    for h in range(2):
                        pe.matmul(bank(2 + h, HALF), wT[:, 2 + k, :],
                                  A[:, bass.ds(i * (2 * HALF) + h * HALF, HALF)],
                                  start=True, stop=True).then_inc(st[stage]["m"], 1)
                pe.wait_ge(bn_applied, k)
                sublayer(0)
                with pe.Fori(1, STEPS) as i:
                    pe.wait_ge(st[stage]["r"], i * 2)
                    sublayer(i)
            turn("x1", 0)
            with pe.Fori(1, STEPS) as i:
                pe.wait_ge(st["x1"]["r"], i)
                turn("x1", i)
            reduce(1)

            def dense(stage, w, bias, i):
                pe.wait_ge(st[stage]["c"], i + 1)
                for j in range(STEP):
                    ins = pe.matmul(tslot(j, 2), zt[:, j, :], w, start=True, stop=bias is None)
                    if bias is not None:
                        ins = pe.matmul(tslot(j, 2), ones[0:1, :], bias, start=False, stop=True)
                ins.then_inc(st[stage]["m"], 1)

            def dense_all(stage, w, bias=None):
                turn(stage, 0)
                pe.wait_ge(st[stage]["c"], 1)
                turn(stage, 1)
                dense(stage, w, bias, 0)
                with pe.Fori(1, STEPS - 1) as i:
                    pe.wait_ge(st[stage]["c"], i + 1)
                    turn(stage, i + 1)
                    pe.wait_ge(st[stage]["r"], i)
                    dense(stage, w, bias, i)
                pe.wait_ge(st[stage]["r"], STEPS - 1)
                dense(stage, w, bias, STEPS - 1)

            def wide_all(stage, w):
                def wide(i):
                    pe.wait_ge(st[stage]["c"], i + 1)
                    for j in range(STEP):
                        g1 = i * STEP + (j + 1)
                        pe.wait_ge(st[stage]["r"], g1)
                        n = w.shape[1]
                        pe.matmul(bank(WIDE_BANKS[j], n), zt[:, j, :], w, start=True, stop=True).then_inc(st[stage]["m"], 1)

                turn(stage, 0)
                with pe.Fori(0, STEPS - 1) as i:
                    pe.wait_ge(st[stage]["c"], i + 1)
                    turn(stage, i + 1)
                    wide(i)
                wide(STEPS - 1)

            dense_all("f1", wT[:, 5, :], l1b_row[0:1, :])
            wide_all("g2", wcat[:, 0:TYPES, :].rearrange("p k d -> p (k d)"))
            pe.wait_ge(st["g2"]["r"], NEAR + GROUPS)
            own_turn(0, 1)
            own_wide(0, 1)
            reduce(2)
            dense_all("f2", wcat[:, 7, :])
            reduce(3)
            dense_all("f3", w3[:, :])

            def over_nodes(b, v):
                per = bank(b).shape[1]
                for k in range((GROUPS - 1) * D // per):
                    pe.matmul(bank(b), ones[:, :], v[:, k * per:(k + 1) * per], start=(k == 0), stop=False,
                              skip_group_check=True)
                return pe.matmul(bank(b, D), ones[0:LAST, :], v[0:LAST, (GROUPS - 1) * D:GROUPS * D],
                                 start=False, stop=True, skip_group_check=True)

            pe.wait_ge(relu_done, STEPS)
            over_nodes(0, B).then_inc(sum_h, 1)
            pe.wait_ge(sq_ready, STEPS)
            over_nodes(1, A).then_inc(sum_sq, 1)

        @block.vector
        def _(dve):
            chain = Chain(dve, chain_sem)
            mark, link, wait = chain.mark, chain.link, chain.wait

            def tile(v, g):
                return v[:, bass.ds(g, 1), :].rearrange("p a d -> p (a d)")

            dve.memset(src_i[:, MAIN:COLS], NO_NODE)
            dve.memset(dst_i[:, MAIN:COLS], NO_NODE)
            dve.memset(type_i[:, MAIN:COLS], 0)
            dve.memset(w_f[:, MAIN:COLS], 0.0)
            dve.memset(X[:, GROUPS - 1, :], 0.0).then_inc(pad_ready, 1)

            def split_key(key, lane1):
                mark(dve.tensor_scalar(tmp_i, key, SHIFT, None, ALU.arith_shift_right))
                link(dve.tensor_scalar(tmp2_i, key, P - 1, None, ALU.bitwise_and))
                mark(dve.tensor_copy(group_b, tmp_i))
                link(dve.tensor_scalar(lane1, tmp2_i, 1.0, None, ALU.add))

            def start_slots(k):
                link(dve.tensor_scalar(small[:, 0, :], ps[:, 7, 2 * GROUPS:3 * GROUPS], P - 1.0, None, ALU.add))
                link(dve.tensor_copy(small_i[:, :], small[:, 0, :]))
                link(dve.tensor_scalar(small_i[:, :], small_i[:, :], SHIFT, None, ALU.arith_shift_right))
                link(dve.tensor_copy(small[:, 1, :], small_i[:, :]))
                link(dve.tensor_tensor_scan(small[:, 2, :], small[:, 1, :], small[:, 1, :], 0.0,
                                            ALU.add, ALU.bypass))
                link(dve.tensor_tensor(small[:, 3, :], small[:, 2, :], small[:, 1, :], ALU.subtract))
                link(dve.scalar_tensor_tensor(out=small[:, 4, :], in0=small[:, 3, :], scalar=float(P),
                                              in1=ps[:, 7, 0:GROUPS], op0=ALU.mult, op1=ALU.add))
                link(dve.tensor_scalar(start_at[:, :], small[:, 4, :], -1.0, None, ALU.add))
                link(dve.tensor_tensor(below[:, :, :],
                                       small[0:BATCHES, 2:3, :].broadcast_to([BATCHES, CH, GROUPS]),
                                       chunk_ids[:, :, None].broadcast_to([BATCHES, CH, GROUPS]), ALU.is_le))
                link(dve.tensor_reduce(tile_of[:, :], below[:, :, :], AX_X, ALU.add))
                if k == 0:
                    dve.tensor_scalar(last_chunk[:, :, 0:STEP],
                                      small[:, 2, :].rearrange("p (i j) -> p i j", j=STEP), -1.0, 0.0,
                                      ALU.add, ALU.max)
                dve.tensor_scalar(at_cols[:, k, :], tile_of[:, :], GROUPS - 1.0, float(AW), ALU.min,
                                  ALU.mult).then_inc(cols_ready, 1)

            def rank(slot, cuts):
                link(dve.memset(pos, 0.0))
                for c0, c1 in zip(cuts, cuts[1:]):
                    part = slice(c0, c1)
                    scans = []
                    for g in range(GROUPS + 1):
                        if g < GROUPS:
                            running = ps[:, 2 * (g % 3):2 * (g % 3) + 2, :].rearrange(
                                "p b n -> p (b n)")[:, 0:c1 - c0]
                            scans.append((running, mark(dve.tensor_tensor_scan(
                                running, masks[:, g, part], masks[:, g, part], start_at[:, g:g + 1],
                                ALU.add, ALU.bypass))))
                        if g:
                            running, scanned = scans[g - 1]
                            wait(last if g > 1 else scanned)
                            if c1 < COLS:
                                dve.tensor_copy(start_at[:, g - 1:g], running[:, c1 - c0 - 1:c1 - c0])
                            last = mark(dve.copy_predicated(pos[:, part], masks[:, g - 1, part], running))
                    wait(last)
                    link(dve.tensor_copy(tmp_i[:, part], pos[:, part]))
                    link(dve.tensor_scalar(tmp2_i[:, part], tmp_i[:, part], P - 1, None, ALU.bitwise_and))
                    link(dve.tensor_scalar(tmp_i[:, part], tmp_i[:, part], SHIFT, None, ALU.arith_shift_right))
                    dve.scalar_tensor_tensor(out=slot[:, part], in0=tmp2_i[:, part], scalar=float(CHUNKS),
                                             in1=tmp_i[:, part], op0=ALU.mult, op1=ALU.add).then_inc(
                        slots_ready, 1)

            def count_masks(i, js):
                for j in js:
                    g = i * STEP + j
                    dve.tensor_scalar(tile(masks, g), group_b, group_ids[:, bass.ds(g, 1)], 0.0,
                                      ALU.is_equal, ALU.add,
                                      accum_out=cnt[:, bass.ds(g, 1)]).then_inc(counted_dve, 1)

            dve.wait_ge(keys_in, 32)
            dve.wait_ge(consts, 7)
            split_key(src_i, lane1_src)
            with dve.Fori(0, STEPS) as i:
                count_masks(i, range(COUNT_SPLIT))
                for j in range(COUNT_SPLIT, STEP):
                    g = i * STEP + j
                    dve.tensor_scalar(tile(masks, g), group_b, group_ids[:, bass.ds(g, 1)], None,
                                      ALU.is_equal).then_inc(masks_made, 1)
            link(dve.scalar_tensor_tensor(out=pay[:, :, P_SRC], in0=tmp2_i, scalar=float(GROUPS), in1=tmp_i,
                                          op0=ALU.mult, op1=ALU.add))
            dve.wait_ge(counts_summed, 1)
            start_slots(0)
            rank(slot_src, (0, FIRST_ROUNDS * SRING * BATCH, COLS))
            dve.wait_ge(slots_ready, 2)
            dve.wait_ge(lists_in, 96)
            split_key(dst_i, pay[:, :, P_LANE1])
            with dve.Fori(0, STEPS) as i:
                count_masks(i, range(STEP))
            dve.wait_ge(counts_summed, 2)
            start_slots(1)
            rank(slot_dst, (0, COLS))
            dve.wait_ge(slots_ready, 3)
            dve.scalar_tensor_tensor(out=pay[:, :, P_SRCT], in0=pay[:, :, P_SRC], scalar=float(TYPES),
                                     in1=type_i, op0=ALU.mult, op1=ALU.add)
            dve.memset(pay[:, :, P_ONE], 1.0)
            for t in range(TYPES):
                dve.tensor_scalar(pay[:, :, P_TYPE + t], type_i, float(t), None, ALU.is_equal)
            dve.tensor_copy(pay[:, :, P_W], w_f).then_inc(pay_ready, 1)

            def own_terms(i, first, count=2):
                dve.wait_ge(st["h2"]["m"], i + 1)
                groups = [(5 + k, first + k) for k in range(count)]
                for t in range(TYPES):
                    for b, g in groups:
                        part = ps[:, b, t * D:(t + 1) * D]
                        share = ctype[:, t, bass.ds(g, 1)]
                        if t == 0:
                            ins = dve.tensor_scalar(tile(At, g), part, share, None, ALU.mult)
                        else:
                            ins = dve.scalar_tensor_tensor(out=tile(At, g), in0=part, scalar=share,
                                                           in1=tile(At, g), op0=ALU.mult, op1=ALU.add)
                        if t < TYPES - 1:
                            mark(ins)
                    if t < TYPES - 1:
                        for b, g in groups if t == 0 else ():
                            dve.tensor_tensor(tile(Bt, g), ps[:, b, TYPES * D:], bc[:, 8, :], ALU.add)
                        wait(chain.last())
                ins.then_inc(st["h2"]["r"], 1)

            def reduce(q):
                width = ONE + 1 if q == 0 else AW if q == 1 else D

                def one_hot(i, r, j):
                    s, to = r % 2, onehot[:, r % 2, j, :]
                    if j == 0:
                        dve.wait_ge(products, i * RING + (q * BATCHES + r + RING - 1))
                        if q == 0:
                            dve.wait_ge(slot_rows_in[r % RING], i * 16 + (r // RING + 1) * 16)
                    if q == 0:
                        ins = dve.tensor_scalar(to, lane_ids[:, :], slot_rows[:, r % RING, j, LANE1:LANE1 + 1],
                                                None, ALU.is_equal)
                    else:
                        edge = ordered[:, bass.ds(i * (RING * CH) + (r * CH + j), 1), :].rearrange(
                            "p a w -> p (a w)")
                        lane1, weight = edge[:, P_LANE1:P_LANE1 + 1], edge[:, P_W:P_W + 1]
                        if q < 3:
                            ins = dve.tensor_scalar(to, lane_ids[:, :], lane1, None, ALU.is_equal)
                        else:
                            ins = dve.tensor_scalar(to, lane_ids[:, :], lane1, weight, ALU.is_equal, ALU.mult)
                    if j == CH - 1:
                        ins.then_inc(onehot_ready, 1)

                def batch(i, r, ahead=True):
                    b = i * RING + r
                    at = nc.values_load_multi_w_load_instructions(
                        (at_src if q == 0 else at_dst)[0:1, bass.ds(b * CH, CH)], engines=[DVE],
                        min_val=0, max_val=(GROUPS - 1) * AW,
                        skip_runtime_bounds_check_because="the tables hold at most GROUPS - 1 times AW")[1]
                    dve.wait_ge(products, b + (q * BATCHES + RING + 1))
                    for j in range(CH):
                        dve.wait_ge(added, b * CH + (2 * CH + q * CHUNKS + j))
                        to = sums_flat[:, bass.ds(at[j], width)]
                        dve.tensor_tensor(to, to, product(r % 2, j, width), ALU.add).then_inc(added, 1)
                        if ahead:
                            one_hot(i, r + 2, j)

                for r in range(2):
                    for j in range(CH):
                        one_hot(0, r, j)

                def rounds(first, end, beside=False):
                    with dve.Fori(first, end) as i:
                        for r in range(RING):
                            batch(i, r)
                            if beside and r == 0:
                                chain.enter(i - first, 4)
                                own_terms(i, i * 2 - 1)
                                chain.leave(end - first)

                if q == 2:
                    rounds(0, 1)
                    rounds(1, OWN_SETS + 1, True)
                    assert OWN_SETS + 1 == RROUNDS - 1
                else:
                    rounds(0, RROUNDS - 1)
                for r in range(RING):
                    batch(RROUNDS - 1, r, r < RING - 2)
                dve.wait_ge(added, 2 * CH + (q + 1) * CHUNKS)

            def each_step(first, then, per=0):
                first(0)
                first(1)
                with dve.Fori(1, STEPS - 1) as i:
                    if per:
                        chain.enter(i - 1, per)
                    first(i + 1)
                    then(i - 1)
                    if per:
                        chain.leave(STEPS - 2)
                then(STEPS - 2)
                then(STEPS - 1)

            def step_of(v, i):
                return v[:, bass.ds(i * STEP, STEP), :]

            def group_stats(v, i):
                for j in range(STEP):
                    g = i * STEP + j
                    dve.bn_stats(tile(stats, g), tile(v, g)).then_inc(stats_done, 1)

            ln_count = [0]

            def layer_norm_scale():
                ln_count[0] += 1
                dve.wait_ge(stats_done, GROUPS * ln_count[0])
                mean_e, mean_o, var_e, var_o = (stats[:, :, k] for k in (1, 4, 2, 5))
                mark(dve.tensor_tensor(mv[:, 0, :], mean_e, mean_o, ALU.add))
                mark(dve.tensor_tensor(sd[:, :], mean_e, mean_o, ALU.subtract))
                link(dve.tensor_tensor(mv[:, 1, :], var_e, var_o, ALU.add))
                mark(dve.scalar_tensor_tensor(out=sd[:, :], in0=sd[:, :], scalar=0.25, in1=sd[:, :],
                                              op0=ALU.mult, op1=ALU.mult))
                link(dve.tensor_scalar(mv[:, 0, :], mv[:, 0, :], 0.5, None, ALU.mult))
                dve.scalar_tensor_tensor(out=mv[:, 1, :], in0=mv[:, 1, :], scalar=1.0 / D, in1=sd[:, :],
                                         op0=ALU.mult, op1=ALU.add).then_inc(mv_done, 1)
                dve.wait_ge(sd_done, ln_count[0])
                link(dve.reciprocal(rstd[:, :], sd[:, :]))
                link(dve.scalar_tensor_tensor(out=nmr[:, :], in0=mv[:, 0, :], scalar=-1.0,
                                              in1=rstd[:, :], op0=ALU.mult, op1=ALU.mult))

            def normalised(to, v, g):
                return dve.tensor_scalar(to, tile(v, g), rstd[:, bass.ds(g, 1)], nmr[:, bass.ds(g, 1)],
                                         ALU.mult, ALU.add)

            dve.sem_inc(added, 2 * CH)
            link(dve.memset(sums_flat, 0.0))
            dve.wait_ge(at_in, 32)
            reduce(0)
            link(dve.tensor_scalar(sd[:, :], sums[:, :, ONE], 1.0, None, ALU.max))
            link(dve.reciprocal(rcnt[:, :], sd[:, :]))

            def edge_means(i):
                for j in range(STEP):
                    g = i * STEP + j
                    dve.tensor_scalar(zr[:, j, :], tile(sums, g)[:, 0:D], rcnt[:, bass.ds(g, 1)], None,
                                      ALU.mult).then_inc(st["mlp0"]["z"], 1)

            edge_means(0)
            with dve.Fori(1, STEPS) as i:
                dve.wait_ge(st["mlp0"]["t"], i)
                edge_means(i)
            dve.wait_ge(st["mlp0"]["z"], GROUPS)
            dve.memset(sums_flat, 0.0).then_inc(sums_zero, 1)
            for k, stage in enumerate(("mlp0", "mlp1", "mlp2")):
                dve.wait_ge(st[stage]["r"], 2 * STEPS)
                for n in range(NBN):
                    last = mark(dve.bn_stats(bn_st[:, n, :], A[:, n * BN_COLS:(n + 1) * BN_COLS]))
                wait(last)
                dve.bn_aggr(bn_mv[:, :], bn_st[:, :, :].rearrange("p n s -> p (n s)")).then_inc(bnsd_in, 1)
                dve.wait_ge(bnsd_out, k + 1)
                dve.wait_ge(bnsd_in, k + 1)
                c = bn_c[:, k, :]
                link(dve.reciprocal(c[:, 1:2], c[:, 0:1]))
                link(dve.tensor_tensor(c[:, 2:3], c[:, 1:2], cols[:, 4 + 2 * k:5 + 2 * k], ALU.mult))
                link(dve.tensor_tensor(c[:, 1:2], bn_mv[:, 0:1], c[:, 2:3], ALU.mult))
                ins = dve.tensor_tensor(c[:, 3:4], cols[:, 5 + 2 * k:6 + 2 * k], c[:, 1:2], ALU.subtract)
                if k == 2:
                    ins.then_inc(bn_in, 1)
                else:
                    link(ins)
                    dve.tensor_scalar(A[:, :], A[:, :], c[:, 2:3], c[:, 3:4], ALU.mult, ALU.add).then_inc(
                        bn_applied, 1)

            with dve.Fori(0, STEPS) as i:
                dve.wait_ge(st["x1"]["t"], i + 1)
                dve.tensor_tensor(step_of(X, i), step_of(X, i), grouped(tslots()), ALU.add).then_inc(
                    st["x1"]["r"], 1)
                dve.wait_ge(st["x1"]["r"], i + 1)
                group_stats(X, i)
            layer_norm_scale()
            with dve.Fori(0, STEPS) as i:
                for j in range(STEP):
                    g = i * STEP + j
                    normalised(tile(X, g), X, g).then_inc(x1_ready, 1)
            dve.wait_ge(x1_ready, GROUPS)

            dve.wait_ge(first_in, 16)
            dve.wait_ge(ordered_in, 16)
            dve.wait_ge(sums_zero, 1)
            reduce(1)
            mark(dve.tensor_scalar(sd[:, :], sums[:, :, D], 1.0, None, ALU.max))
            link(dve.tensor_scalar(deg[:, 0, :], sums[:, :, AW - 1], 1.0, None, ALU.add))
            mark(dve.tensor_scalar(deg[:, 1, :], deg[:, 0, :], 1e-30, None, ALU.max))
            link(dve.reciprocal(rcnt[:, :], sd[:, :]))
            dve.sem_inc(deg_ready, 1)
            for t in range(TYPES):
                mark(dve.tensor_tensor(ctype[:, t, :], sums[:, :, D + 1 + t], rcnt[:, :], ALU.mult))

            def f1_operands(i):
                if not first_of(i):
                    dve.wait_ge(st["f1"]["t"], i)
                for j in range(STEP):
                    g = i * STEP + j
                    dve.scalar_tensor_tensor(out=zr[:, j, :], in0=tile(sums, g)[:, 0:D],
                                             scalar=rcnt[:, bass.ds(g, 1)], in1=tile(X, g),
                                             op0=ALU.mult, op1=ALU.add).then_inc(st["f1"]["z"], 1)

            def f1_results(i):
                dve.wait_ge(st["f1"]["m"], i + 1)
                dve.scalar_tensor_tensor(out=step_of(X, i), in0=grouped(tslots(2)), scalar=0.0,
                                         in1=step_of(X, i), op0=ALU.max, op1=ALU.add).then_inc(
                    st["f1"]["r"], 1)
                dve.wait_ge(st["f1"]["r"], i + 1)
                group_stats(X, i)

            each_step(f1_operands, f1_results)
            layer_norm_scale()
            dve.wait_ge(deg_sd, 1)
            link(dve.reciprocal(dinv[:, :], deg[:, 2, :]))
            link(dve.scalar_tensor_tensor(out=dinv[:, :], in0=deg[:, 0, :], scalar=0.0, in1=dinv[:, :],
                                          op0=ALU.is_gt, op1=ALU.mult))

            def normalised_operands(stage):
                def operands(i):
                    if not first_of(i):
                        dve.wait_ge(st[stage]["t"], i)
                    for j in range(STEP):
                        g = i * STEP + j
                        normalised(zr[:, j, :], X, g).then_inc(st[stage]["z"], 1)
                return operands

            def g2_results(i):
                if not first_of(i):
                    dve.wait_ge(msg_out, i * 16)
                for j in range(STEP):
                    dve.wait_ge(st["g2"]["m"], i * STEP + (j + 1))
                    dve.tensor_tensor(msgs[:, j, :], bank(WIDE_BANKS[j], TYPES * D),
                                      bc[:, 5:8, :].rearrange("p k d -> p (k d)"), ALU.add).then_inc(
                        st["g2"]["r"], 1)

            dve.sem_inc(st["g2"]["r"], NEAR)
            operands = normalised_operands("g2")
            operands(0)
            operands(1)
            g2_results(0)
            with dve.Fori(1, STEPS - 1) as i:
                operands(i + 1)
                g2_results(i)
            g2_results(STEPS - 1)
            dve.wait_ge(x_normed, GROUPS)

            own_terms(0, 0, 1)
            dve.wait_ge(sums_zero2, 1)
            reduce(2)
            dve.wait_ge(st["h2"]["r"], OWN_SETS + 1)

            def f2_operands(i):
                if not first_of(i):
                    dve.wait_ge(st["f2"]["t"], i)
                for j in range(STEP):
                    g = i * STEP + j
                    dve.scalar_tensor_tensor(out=zr[:, j, :], in0=tile(sums, g)[:, 0:D],
                                             scalar=rcnt[:, bass.ds(g, 1)], in1=tile(At, g),
                                             op0=ALU.mult, op1=ALU.add).then_inc(st["f2"]["z"], 1)

            def f2_results(i):
                dve.wait_ge(st["f2"]["m"], i + 1)
                dve.tensor_tensor(step_of(Bt, i), grouped(tslots(2)), step_of(Bt, i), ALU.add).then_inc(
                    st["f2"]["r"], 1)
                dve.wait_ge(st["f2"]["r"], i + 1)
                group_stats(Bt, i)

            each_step(f2_operands, f2_results)
            layer_norm_scale()
            dve.sem_inc(scale_ready, 1)

            def bcast(k):
                return bc[:, k:k + 1, :].broadcast_to([P, STEP, D])

            def norm_affine(i):
                dve.wait_ge(b_normed, i + 1)
                link(dve.tensor_tensor(step_of(Bt, i), step_of(Bt, i), bcast(0), ALU.mult))
                dve.tensor_tensor(step_of(Bt, i), step_of(Bt, i), bcast(1), ALU.add).then_inc(norm_ready, 1)

            def add_gelu(i):
                dve.wait_ge(gelu_done, i + 1)
                link(dve.scalar_tensor_tensor(out=step_of(X, i), in0=step_of(X, i), scalar=2.0,
                                              in1=step_of(Bt, i), op0=ALU.mult, op1=ALU.add))
                group_stats(X, i)

            norm_affine(0)
            with dve.Fori(0, STEPS - 1) as i:
                chain.enter(i, 2)
                norm_affine(i + 1)
                add_gelu(i)
                chain.leave(STEPS - 1)
            add_gelu(STEPS - 1)
            layer_norm_scale()

            mark(dve.tensor_tensor(small[:, 0, :], rstd[:, :], dinv[:, :], ALU.mult))
            link(dve.tensor_tensor(small[:, 1, :], nmr[:, :], dinv[:, :], ALU.mult))
            with dve.Fori(0, STEPS) as i:
                for j in range(STEP):
                    g = i * STEP + j
                    ins = dve.tensor_scalar(tile(At, g), tile(X, g), small[:, 0, bass.ds(g, 1)],
                                            small[:, 1, bass.ds(g, 1)], ALU.mult, ALU.add)
                ins.then_inc(st["g3"]["r"], 1)
            dve.wait_ge(x_normed, 2 * GROUPS)
            dve.wait_ge(st["g3"]["r"], STEPS)
            link(dve.tensor_tensor(X[:, :, :], X[:, :, :], bc[:, 4:5, :].broadcast_to([P, GROUPS, D]), ALU.add))
            dve.wait_ge(sums_zero2, 2)
            reduce(3)
            def f3_operands(i):
                if not first_of(i):
                    dve.wait_ge(st["f3"]["t"], i)
                dve.tensor_tensor(zr[:, :, :], step_of(sums, i)[:, :, 0:D], step_of(At, i), ALU.add).then_inc(
                    st["f3"]["z"], STEP)

            def f3_results(i):
                dve.wait_ge(st["f3"]["m"], i + 1)
                for j in range(STEP):
                    g = i * STEP + j
                    last = mark(dve.scalar_tensor_tensor(out=tile(Bt, g), in0=tslot(j, 2),
                                                         scalar=dinv[:, bass.ds(g, 1)], in1=bc[:, 2, :],
                                                         op0=ALU.mult, op1=ALU.add))
                wait(last)
                dve.sem_inc(st["f3"]["r"], 1)
                dve.sem_inc(raw_ready, 1)

            each_step(f3_operands, f3_results, STEP)

            def over_banks(b, to):
                link(dve.tensor_reduce(to, bank(b).rearrange("p (k d) -> p d k", k=4), AX_X, ALU.add))
                link(dve.tensor_scalar(to, to, 1.0 / N, None, ALU.mult))

            dve.wait_ge(sum_h, 1)
            over_banks(0, rowv[:, 0, :])
            with dve.Fori(0, STEPS) as i:
                dve.tensor_tensor(step_of(Bt, i), step_of(Bt, i), rowv[:, 0:1, :].broadcast_to([P, STEP, D]),
                                  ALU.subtract).then_inc(dev_ready, 1)
            dve.wait_ge(sum_sq, 1)
            over_banks(1, rowv[:, 1, :])
            dve.sem_inc(rowsd_in, 1)
            dve.wait_ge(rowsd_out, 1)
            link(dve.reciprocal(rowv[:, 3, :], rowv[:, 2, :]))
            link(dve.tensor_tensor(rowv[:, 4, :], rowv[:, 3, :], bc[:, 3, :], ALU.mult))
            with dve.Fori(0, STEPS) as i:
                chain.enter(i, 2)
                link(dve.tensor_tensor(step_of(Bt, i), step_of(Bt, i),
                                       rowv[:, 4:5, :].broadcast_to([P, STEP, D]), ALU.mult))
                link(dve.tensor_tensor(step_of(X, i), step_of(X, i), step_of(Bt, i), ALU.add))
                group_stats(X, i)
                chain.leave(STEPS)
            layer_norm_scale()
            with dve.Fori(0, STEPS) as i:
                for j in range(STEP):
                    g = i * STEP + j
                    normalised(tile(X, g), X, g).then_inc(y_ready, 1)


_INS = ["x", "src", "dst", "edge_attr_128", "edge_type_3", "edge_weight",
        "L0_gnn_u", "L0_gnn_W0", "L0_gnn_b0", "L0_gnn_W1", "L0_gnn_b1", "L0_gnn_W2", "L0_gnn_b2",
        "L0_gnn_g0", "L0_gnn_bt0", "L0_gnn_g1", "L0_gnn_bt1", "L0_gnn_g2", "L0_gnn_bt2",
        "L1_gnn_W", "L1_gnn_b", "L2_gnn_Wmsg", "L2_gnn_bmsg", "L2_gnn_Wupd", "L2_gnn_bupd",
        "L2_gnn_gamma", "L2_gnn_beta", "L3_gnn_W", "L3_gnn_b", "L3_gnn_gamma", "L3_gnn_beta"]


def kernel(**inputs):
    import numpy as _np
    import concourse.bacc as _bacc
    from concourse import mybir as _mybir
    from concourse.bass_utils import run_bass_kernel_spmd as _run

    nc = _bacc.Bacc("TRN2", target_bir_lowering=False, num_devices=1)
    arrays, args = {}, []
    for name in _INS:
        a = _np.ascontiguousarray(inputs[name])
        arrays[f"in_{name}"] = a
        args.append(nc.dram_tensor(f"in_{name}", a.shape, _mybir.dt.from_np(a.dtype), kind="ExternalInput").ap())
    args.append(nc.dram_tensor("out_nodes", (N, D), _mybir.dt.float32, kind="ExternalOutput").ap())
    gnn_kernel(nc, *args)
    r = _run(nc, [arrays], core_ids=[0])
    return r.results[0]["out_nodes"]
```

```python
from contextlib import ExitStack

import concourse.bass as bass
from concourse import mybir

ALU = mybir.AluOpType
ACT = mybir.ActivationFunctionType
AX_X = mybir.AxisListType.X
F32 = mybir.dt.float32
BF16 = mybir.dt.bfloat16
I32 = mybir.dt.int32
U32 = mybir.dt.uint32
U8 = mybir.dt.uint8
DVE = mybir.EngineType.DVE

P = 128
N = 6250
E = 100000
D = 128
TYPES = 3
GROUPS = -(-N // P)
LAST = N - (GROUPS - 1) * P
STEP = 7
STEPS = GROUPS // STEP
SHIFT = 7
NO_NODE = 63 * P

BATCH = 10
SRING = 3
FIRST_ROUNDS = 3
MAIN = 780
TAIL_LANES = 80
TAIL = 2
COLS = MAIN + TAIL
ROUNDS = MAIN // (BATCH * SRING)
PBATCH = 39
PRING = 2
PROUNDS = MAIN // (PBATCH * PRING)
assert P * MAIN + TAIL_LANES * TAIL == E
assert ROUNDS * BATCH * SRING == MAIN and PROUNDS * PBATCH * PRING == MAIN

CH = 8
RING = 4
CHUNKS = 832
BATCHES = CHUNKS // CH
RROUNDS = BATCHES // RING
assert (E + GROUPS * (P - 1)) // P <= CHUNKS and RROUNDS * RING * CH == CHUNKS

ROW = D + 2
ONE, LANE1 = D, D + 1
PAY = 8
P_SRC, P_SRCT, P_LANE1, P_ONE, P_TYPE, P_W = 0, 1, 2, 3, 4, 7
EXTRA = PAY - P_ONE
AW = D + EXTRA
HALF = STEP * P // 2
FULL = -(-E // P)
ZERO_CUT = 4
COUNT_SPLIT = 3
EPS = 1e-5
NEAR = 2
Z_CUT = 4
Y_CUT = 4
MSG_CUT = 4
VECTORS = 4 + TYPES
MV_COUNT = (1, STEPS, STEPS, 1, 1)
OWN_SETS = (GROUPS - 1) // 2
BN_COLS = 250
NBN = N // BN_COLS


def first_of(i):
    return isinstance(i, int) and i == 0


class Chain:

    def __init__(self, eng, sem):
        self.eng, self.sem, self.n, self.at = eng, sem, 0, None

    def mark(self, ins):
        self.n += 1
        ins.then_inc(self.sem, 1)
        return self.n if self.at is None else self.at + (self.n - self.start)

    def last(self):
        return self.n if self.at is None else self.at + (self.n - self.start)

    def wait(self, value):
        self.eng.wait_ge(self.sem, value)

    def link(self, ins):
        self.wait(self.mark(ins))

    def enter(self, i, per):
        self.start, self.per, self.at = self.n, per, i * per + self.n

    def leave(self, turns):
        assert self.n - self.start == self.per, (self.n - self.start, self.per)
        self.n = self.start + self.per * turns
        self.at = None


def gnn_kernel(nc, x, src, dst, edge_attr, edge_type, edge_weight, u, W0, b0, W1, b1, W2, b2,
               g0, bt0, g1, bt1, g2, bt2, L1W, L1b, Wmsg, bmsg, Wupd, bupd, gam2, bet2,
               W3, b3, gam3, bet3, out):
    with ExitStack() as ctx:
        def sb(name, shape, dt=F32):
            return ctx.enter_context(nc.sbuf_tensor(name, shape, dt))

        def sem(name):
            return ctx.enter_context(nc.semaphore(name))

        def dram(name, shape, dt=F32):
            return nc.dram_tensor(name, shape, dt).ap()

        slots_src = dram("slots_src", [P, CHUNKS, ROW])
        slots_dst = dram("slots_dst", [P, CHUNKS, PAY])
        sums_at_src = dram("sums_at_src", [BATCHES, CH], I32)
        sums_at_dst = dram("sums_at_dst", [BATCHES, CH], I32)
        x1_table = dram("x1_table", [P, GROUPS, D])
        msg_table = dram("msg_table", [P, GROUPS, TYPES * D])
        z_table = dram("z_table", [P, GROUPS, D])

        X = sb("X", [P, GROUPS, D])
        A = sb("A", [P, GROUPS * D])
        masks_raw = sb("masks_raw", [P, 9600])
        lists_raw = sb("lists_raw", [P, 11 * COLS])
        pay_raw = sb("pay_raw", [P, CHUNKS * PAY])
        rows_raw = sb("rows_raw", [P, RING * CH * AW])
        zr = sb("zr", [P, STEP, D])
        zt = sb("zt", [P, STEP, D])
        idx_scatter = sb("idx_scatter", [P, SRING, BATCH], U32)
        idx_gather = sb("idx_gather", [P, RING, CH], U32)
        idx_tail = sb("idx_tail", [P, 2, TAIL], U32)
        tail_rows = sb("tail_rows", [P, TAIL, ROW])
        at_src = sb("at_src", [1, CHUNKS], I32)
        at_dst = sb("at_dst", [1, CHUNKS], I32)

        masks = masks_raw[:, :].bitcast(U8)[:, 0:GROUPS * COLS].rearrange("p (b c) -> p b c", c=COLS)
        sums_flat = masks_raw[:, 0:GROUPS * AW]
        sums = sums_flat.rearrange("p (g w) -> p g w", w=AW)
        onehot = masks_raw[:, GROUPS * AW:GROUPS * AW + 2 * CH * P].rearrange(
            "p (s j n) -> p s j n", s=2, j=CH)
        assert GROUPS * AW + 2 * CH * P <= 9600 and GROUPS * COLS <= 4 * 9600

        def listed(k, dt=F32):
            v = lists_raw[:, k * COLS:(k + 1) * COLS]
            return v if dt == F32 else v.bitcast(dt)
        src_i, dst_i, type_i, w_f = listed(0, I32), listed(1, I32), listed(2, I32), listed(3)
        lane1_src, pos = listed(4), listed(5)
        tmp_i, tmp2_i = listed(6, I32), listed(7, I32)
        group_b = lists_raw[:, 8 * COLS:8 * COLS + COLS // 2].bitcast(BF16)
        slot_src, slot_dst = listed(9), listed(10)
        pay_stage = lists_raw[:, 0:PRING * PBATCH * PAY].rearrange("p (r f) -> p r f", r=PRING)
        idx_pay = listed(1, U32)[:, 0:PRING * PBATCH].rearrange("p (r c) -> p r c", r=PRING)
        assert PRING * PBATCH * PAY <= COLS
        B = lists_raw[:, 0:GROUPS * D]
        At = A[:, :].rearrange("p (g d) -> p g d", d=D)
        Bt = B.rearrange("p (g d) -> p g d", d=D)

        pay = pay_raw[:, 0:COLS * PAY].rearrange("p (c w) -> p c w", w=PAY)
        ordered = pay_raw[:, :].rearrange("p (k w) -> p k w", w=PAY)
        zeros = rows_raw[:, 0:CHUNKS * PAY // 2]
        edge_rows = rows_raw[:, 0:SRING * BATCH * ROW].rearrange("p (s c w) -> p s c w", s=SRING, c=BATCH)
        slot_rows = rows_raw[:, 0:RING * CH * ROW].rearrange("p (s c w) -> p s c w", s=RING, c=CH)
        node_rows = rows_raw[:, :].rearrange("p (s c w) -> p s c w", s=RING, c=CH)
        zr2 = A[:, 0:STEP * D].rearrange("p (j d) -> p j d", d=D)
        zt2 = A[:, STEP * D:2 * STEP * D].rearrange("p (j d) -> p j d", d=D)
        msgs = rows_raw[:, 0:STEP * TYPES * D].rearrange("p (j f) -> p j f", j=STEP)

        lane_ids = sb("lane_ids", [P, P])
        group_ids = sb("group_ids", [P, GROUPS])
        chunk_ids = sb("chunk_ids", [BATCHES, CH])
        ident = sb("ident", [P, P])
        before = sb("before", [P, P])
        ones = sb("ones", [P, P])
        eps_col = sb("eps_col", [P, 1])
        cnt = sb("cnt", [P, GROUPS])
        small = sb("small", [P, 6, GROUPS])
        small_i = sb("small_i", [P, GROUPS], I32)
        start_at = sb("start_at", [P, GROUPS])
        below = sb("below", [BATCHES, CH, GROUPS])
        tile_of = sb("tile_of", [BATCHES, CH])
        at_cols = sb("at_cols", [BATCHES, 2, CH], I32)
        stats = sb("stats", [P, GROUPS, 6])
        mv = sb("mv", [P, 2, GROUPS])
        sd = sb("sd", [P, GROUPS])
        rstd = sb("rstd", [P, GROUPS])
        nmr = sb("nmr", [P, GROUPS])
        rcnt = sb("rcnt", [P, GROUPS])
        ctype = sb("ctype", [P, TYPES, GROUPS])
        dinv = sb("dinv", [P, GROUPS])
        deg = sb("deg", [P, 3, GROUPS])
        wraw = zt[:, 0:6, :]
        wT = sb("wT", [P, 6, D])
        wcat = sb("wcat", [P, 8, D])
        w3 = sb("w3", [P, D])
        cols = sb("cols", [P, 13])
        bc_src = A[0:1, 0:VECTORS * D]
        bc = sb("bc", [P, VECTORS, D])
        zero_row = sb("zero_row", [P, ROW])
        last_chunk = sb("last_chunk", [P, STEPS, STEP + 1], I32)
        bias0 = sb("bias0", [P, 1])
        bn_st = sb("bn_st", [P, NBN, 6])
        bn_mv = sb("bn_mv", [P, 2])
        bn_c = sb("bn_c", [P, 4, 4])

        ps = ctx.enter_context(nc.psum_tensor("ps", [P, 8, 512], F32))

        def bank(b, n=512):
            return ps[:, b, 0:n]

        keys_in, lists_in, x_in, w_in, tail_in = (sem(s) for s in (
            "keys_in", "lists_in", "x_in", "w_in", "tail_in"))
        zero_ready, zero_done, consts, gp_ones = (sem(s) for s in (
            "zero_ready", "zero_done", "consts", "gp_ones"))
        chain_sem = sem("vector_chain")
        pad_ready, masks_made, counted, counts_summed = (sem(s) for s in (
            "pad_ready", "masks_made", "counted", "counts_summed"))
        cols_ready, at_out, at_in = sem("cols_ready"), sem("at_out"), sem("at_in")
        slots_ready, pay_ready = sem("slots_ready"), sem("pay_ready")
        prep_in, prep_t, prep_out, bc_done, bc_copied, bias0_done, bias0_out = (sem(s) for s in (
            "prep_in", "prep_t", "prep_out", "bc_done", "bc_copied", "bias0_done", "bias0_out"))
        edge_rows_in = [sem(f"edge_rows_in{r}") for r in range(SRING)]
        staged_a, staged_b, staged_tail = sem("staged_a"), sem("staged_b"), sem("staged_tail")
        issued = sem("issued")
        scattered_a = [sem(f"scattered_a{r}") for r in range(SRING)]
        scattered_b = [sem(f"scattered_b{r}") for r in range(PRING)]
        tail_a, tail_b = sem("tail_a"), sem("tail_b")
        slot_rows_in = [sem(f"slot_rows_in{r}") for r in range(RING)]
        gathered = [sem(f"gathered{r}") for r in range(RING)]
        first_in, ordered_in, last_zero = sem("first_in"), sem("ordered_in"), sem("last_zero")
        sums_zero = sem("sums_zero")
        onehot_ready, products, added = sem("onehot_ready"), sem("products"), sem("added")
        idx_ready, extras_ready = sem("idx_ready"), sem("extras_ready")
        st = {s: {k: sem(f"{s}_{k}") for k in "ztcmr"} for s in
              ("mlp0", "mlp1", "mlp2", "x1", "f1", "g2", "h2", "f2", "g3", "f3", "x3")}
        bn_in = sem("bn_in")
        mv_done, sd_done = sem("mv_done"), sem("sd_done")
        bnsd_in, bnsd_out = sem("bnsd_in"), sem("bnsd_out")
        x1_ready, x1_out, msg_out_a, msg_out_b, z_out, y_ready, y_out = (sem(s) for s in (
            "x1_ready", "x1_out", "msg_out_a", "msg_out_b", "z_out", "y_ready", "y_out"))
        counted_dve, bn_applied, stats_done, x_normed, sums_zero2 = (sem(s) for s in (
            "counted_dve", "bn_applied", "stats_done", "x_normed", "sums_zero2"))
        xt_done, xt_copied = sem("xt_done"), sem("xt_copied")
        norm_ready, gelu_done, f1_scaled = sem("norm_ready"), sem("gelu_done"), sem("f1_scaled")
        b_normed = sem("b_normed")
        f2_scaled, scaled_b = sem("f2_scaled"), sem("scaled_b")
        deg_ready, deg_sd = sem("deg_ready"), sem("deg_sd")
        loops_ready, y_ready2 = sem("loops_ready"), sem("y_ready2")
        y_scaled, z_scaled = sem("y_scaled"), sem("z_scaled")

        block = ctx.enter_context(nc.Block())

        def tslot(j, base=0):
            return ps[:, base + j // 4, (j % 4) * D:(j % 4 + 1) * D]

        def tslots(base=0):
            return ps[:, base:base + 2, :].rearrange("p b n -> p (b n)")[:, 0:STEP * D]

        def grouped(v):
            return v.rearrange("p (j d) -> p j d", d=D)

        zt_flat = zt[:, :, :].rearrange("p j d -> p (j d)")

        def product(s, j, width):
            if width == D:
                return ps[:, 2 * s + j // 4, (j % 4) * D:(j % 4 + 1) * D]
            return ps[:, 4 * s + j // 2, (j % 2) * AW:(j % 2) * AW + width]

        def last_edges(a):
            return a[P * MAIN:E].rearrange("(p c) -> p c", p=TAIL_LANES)

        def main_edges(a):
            return a[0:P * MAIN].rearrange("(p c) -> p c", p=P)

        attr_main = edge_attr[0:P * MAIN, :].rearrange("(p c) d -> p c d", p=P)
        attr_tail = edge_attr[P * MAIN:E, :].rearrange("(p c) d -> p c d", p=TAIL_LANES)

        def col(v):
            return v.rearrange("(d a) -> d a", a=1)

        def row(v):
            return v.rearrange("(a d) -> a d", a=1)

        def by_group(v):
            return (v[0:(GROUPS - 1) * P, :].rearrange("(g p) d -> p g d", p=P),
                    v[(GROUPS - 1) * P:N, :])

        def zero_last_chunks(eng, kind, j0, j1):
            eng.wait_ge(cols_ready, 1)
            eng.wait_ge(zero_done, 16 * 4)
            with eng.Fori(0, STEPS) as i:
                at = nc.values_load_multi_w_load_instructions(
                    last_chunk[0:1, bass.ds(i, 1), j0:j1].rearrange("p a j -> p (a j)"),
                    engines=[kind], min_val=0, max_val=CHUNKS - 1,
                    skip_runtime_bounds_check_because="a group ends at or before the last chunk")[1]
                for j in range(j1 - j0):
                    eng.dma_start(slots_src[:, bass.ds(at[j], 1), :].rearrange("p a w -> p (a w)"),
                                  zero_row[:, :]).then_inc(last_zero, 16)

        @block.sync
        def _(sp):
            sp.dma_start(src_i[:, 0:MAIN], main_edges(src)).then_inc(keys_in, 16)
            sp.wait_ge(pad_ready, 1)
            sp.dma_start(src_i[0:TAIL_LANES, MAIN:COLS], last_edges(src)).then_inc(keys_in, 16)
            for dst_t, s in ((dst_i, dst), (type_i, edge_type), (w_f, edge_weight)):
                sp.dma_start(dst_t[:, 0:MAIN], main_edges(s)).then_inc(lists_in, 16)
                sp.dma_start(dst_t[0:TAIL_LANES, MAIN:COLS], last_edges(s)).then_inc(lists_in, 16)
            full, last = by_group(x)
            sp.dma_start(X[:, 0:GROUPS - 1, :], full).then_inc(x_in, 16)
            sp.dma_start(X[0:LAST, GROUPS - 1, :], last).then_inc(x_in, 16)
            sp.dma_start(wraw[:, 0:3, :], W0.rearrange("o (k i) -> o k i", k=3)).then_inc(w_in, 16)
            for k, w in ((3, W1), (4, W2), (5, L1W)):
                sp.dma_start(wraw[:, k, :], w).then_inc(w_in, 16)
            for t in range(TYPES):
                for h in range(2):
                    sp.dma_start(wcat[:, TYPES * h + t, :], Wmsg[t, h * D:(h + 1) * D, :]).then_inc(w_in, 16)
            sp.dma_start(wcat[:, 6:8, :], Wupd.rearrange("(h i) o -> i h o", h=2)).then_inc(w_in, 16)
            sp.dma_start(w3[:, :], W3).then_inc(w_in, 16)
            sp.dma_start(cols[:, 0:1], u[0:1, :].rearrange("a d -> d a")).then_inc(w_in, 16)
            for k, v in enumerate((b0, b1, b2, g0, bt0, g1, bt1, g2, bt2, gam3, bet3, b3)):
                sp.dma_start(cols[:, k + 1:k + 2], col(v)).then_inc(w_in, 16)
            for k, v in enumerate((gam2, bet2, bmsg[0], bmsg[1], bmsg[2], bupd, L1b)):
                sp.dma_start(bc_src[0:1, k * D:(k + 1) * D], row(v)).then_inc(w_in, 16)
            sp.dma_start(tail_rows[0:TAIL_LANES, :, 0:D], attr_tail).then_inc(tail_in, 16)
            sp.wait_ge(zero_ready, 2)
            half = CHUNKS * PAY // 2
            for k in range(2):
                sp.dma_start(slots_dst.rearrange("p c w -> p (c w)")[:, k * half:(k + 1) * half],
                             zeros[:, 0:half]).then_inc(zero_done, 16)
            half = (CHUNKS - FULL) // 2
            for k in range(2):
                sp.dma_start(slots_src[:, FULL + k * half:FULL + (k + 1) * half, :],
                             zeros[:, 0:half * ROW].rearrange("p (c w) -> p c w", w=ROW)).then_inc(zero_done, 16)
            sp.wait_ge(gp_ones, 1)

            def load_edge_rows(i, r):
                at = i * (SRING * BATCH) + r * BATCH
                sp.dma_start(edge_rows[:, r, :, 0:D], attr_main[:, bass.ds(at, BATCH), :]).then_inc(
                    edge_rows_in[r], 16)
            for r in range(SRING):
                load_edge_rows(0, r)
            zero_last_chunks(sp, mybir.EngineType.SP, 0, ZERO_CUT)
            with sp.Fori(1, ROUNDS) as i:
                for r in range(SRING):
                    sp.wait_ge(scattered_a[r], i * (16 * BATCH))
                    load_edge_rows(i, r)
            for k, (table, flat) in enumerate(((sums_at_src, at_src), (sums_at_dst, at_dst))):
                sp.wait_ge(cols_ready, k + 1)
                sp.dma_start(table, at_cols[:, k, :]).then_inc(at_out, 16)
                sp.wait_ge(at_out, 16 * (k + 1))
                sp.dma_start(flat[0:1, :], table.rearrange("b c -> (b c)").rearrange(
                    "(a k) -> a k", a=1)).then_inc(at_in, 16)
            for r in range(SRING):
                sp.wait_ge(scattered_a[r], 16 * BATCH * ROUNDS)
            sp.wait_ge(tail_a, 16 * TAIL)
            with sp.Fori(0, RROUNDS) as i:
                for r in range(RING):
                    sp.wait_ge(products, i * RING + (r + 1))
                    sp.dma_start(slot_rows[:, r, :, :],
                                 slots_src[:, bass.ds(i * (RING * CH) + r * CH, CH), :]).then_inc(
                        slot_rows_in[r], 16)
            sp.wait_ge(x1_ready, GROUPS)
            sp.dma_start(x1_table, X[:, :, :]).then_inc(x1_out, 16)
            for r in range(PRING):
                sp.wait_ge(scattered_b[r], 16 * PBATCH * PROUNDS)
            sp.wait_ge(tail_b, 16 * TAIL)
            first = RING * CH
            sp.dma_start(ordered[:, 0:first, :], slots_dst[:, 0:first, :]).then_inc(first_in, 16)
            sp.dma_start(ordered[:, first:CHUNKS, :], slots_dst[:, first:CHUNKS, :]).then_inc(ordered_in, 16)
            with sp.Fori(0, STEPS) as i:
                for j0, j1, done in ((0, MSG_CUT, msg_out_a), (MSG_CUT, STEP, msg_out_b)):
                    sp.wait_ge(st["g2"]["r"], i * STEP + (j1 + NEAR))
                    sp.dma_start(msg_table[:, bass.ds(i * STEP + j0, j1 - j0), :],
                                 msgs[:, j0:j1, :]).then_inc(done, 16)
            with sp.Fori(0, STEPS) as i:
                sp.wait_ge(st["g3"]["r"], i + 1)
                sp.wait_ge(st["g3"]["z"], i + 1)
                sp.dma_start(z_table[:, bass.ds(i * STEP, STEP), :],
                             At[:, bass.ds(i * STEP, STEP), :]).then_inc(z_out, 16)
            full, last = by_group(out)
            with sp.Fori(0, STEPS - 1) as i:
                sp.wait_ge(y_ready, i * Y_CUT + Y_CUT)
                sp.wait_ge(y_ready2, i * (STEP - Y_CUT) + (STEP - Y_CUT))
                sp.dma_start(full[:, bass.ds(i * STEP, STEP), :],
                             X[:, bass.ds(i * STEP, STEP), :]).then_inc(y_out, 16)
            sp.wait_ge(y_ready, STEPS * Y_CUT)
            sp.wait_ge(y_ready2, STEPS * (STEP - Y_CUT))
            sp.dma_start(full[:, GROUPS - STEP:GROUPS - 1, :], X[:, GROUPS - STEP:GROUPS - 1, :]).then_inc(y_out, 16)
            sp.dma_start(last, X[0:LAST, GROUPS - 1, :]).then_inc(y_out, 16)
            sp.wait_ge(y_out, 16 * (STEPS + 1))

        @block.gpsimd
        def _(pool):
            pool.memset(zeros, 0.0).then_inc(zero_ready, 1)
            pool.memset(zero_row[:, :], 0.0).then_inc(zero_ready, 1)
            pool.iota(group_ids[:, :], [[1, GROUPS]], base=0, channel_multiplier=0,
                      allow_small_or_imprecise_dtypes=True).then_inc(consts, 1)
            pool.iota(lane_ids[:, :], [[1, P]], base=1, channel_multiplier=0,
                      allow_small_or_imprecise_dtypes=True).then_inc(consts, 1)
            pool.iota(chunk_ids[:, :], [[1, CH]], base=0, channel_multiplier=CH,
                      allow_small_or_imprecise_dtypes=True).then_inc(consts, 1)
            pool.memset(ones[:, :], 1.0).then_inc(consts, 1)
            pool.memset(eps_col[:, :], EPS).then_inc(consts, 1)
            pool.wait_ge(consts, 5)
            pool.affine_select(out=ident[:, :], in_=ones[:, :], pattern=[[-1, P]], base=0,
                               channel_multiplier=1, compare_op=ALU.is_equal, fill=0.0).then_inc(consts, 1)
            pool.affine_select(out=before[:, :], in_=ones[:, :], pattern=[[1, P]], base=0,
                               channel_multiplier=-1, compare_op=ALU.is_gt, fill=0.0).then_inc(consts, 1)
            pool.wait_ge(zero_done, 16 * 4)
            pool.memset(edge_rows[:, :, :, ONE:ONE + 1], 1.0).then_inc(gp_ones, 1)
            flat_src = slots_src.rearrange("p c w -> (p c) w")
            flat_dst = slots_dst.rearrange("p c w -> (p c) w")
            pool.wait_ge(last_zero, 16 * GROUPS)
            pool.sem_inc(issued, 1)
            with pool.Fori(0, ROUNDS) as i:
                for r in range(SRING):
                    pool.wait_ge(staged_a, i * SRING + (r + 1))
                    pool.sem_inc(issued, 1)
                    pool.wait_ge(edge_rows_in[r], i * 16 + 16)
                    pool.sem_inc(issued, 1)
                    for c in range(BATCH):
                        pool.indirect_dma_start(
                            flat_src, bass.IndirectOffsetOnAxis(idx_scatter[:, r, c:c + 1], 0),
                            edge_rows[:, r, c, :], None).then_inc(scattered_a[r], 16)
            pool.wait_ge(staged_tail, 1)
            for c in range(TAIL):
                pool.indirect_dma_start(
                    flat_src, bass.IndirectOffsetOnAxis(idx_tail[0:TAIL_LANES, 0, c:c + 1], 0),
                    tail_rows[0:TAIL_LANES, c, :], None).then_inc(tail_a, 16)
            def scatter_payloads(i, r):
                at = i * (PRING * PBATCH) + r * PBATCH
                pool.tensor_copy(idx_pay[:, r, :], slot_dst[:, bass.ds(at, PBATCH)])
                pool.tensor_copy(pay_stage[:, r, :],
                                 pay_raw[:, bass.ds(at * PAY, PBATCH * PAY)]).then_inc(staged_b, 1)
                pool.wait_ge(staged_b, i * PRING + (r + 1))
                pool.sem_inc(issued, 1)
                for c in range(PBATCH):
                    pool.indirect_dma_start(
                        flat_dst, bass.IndirectOffsetOnAxis(idx_pay[:, r, c:c + 1], 0),
                        pay_stage[:, r, c * PAY:(c + 1) * PAY], None).then_inc(scattered_b[r], 16)

            for r in range(PRING):
                scatter_payloads(0, r)
            with pool.Fori(1, PROUNDS) as i:
                for r in range(PRING):
                    pool.wait_ge(scattered_b[r], i * (16 * PBATCH))
                    pool.sem_inc(issued, 1)
                    scatter_payloads(i, r)
            for c in range(TAIL):
                pool.indirect_dma_start(
                    flat_dst, bass.IndirectOffsetOnAxis(idx_tail[0:TAIL_LANES, 1, c:c + 1], 0),
                    pay[0:TAIL_LANES, MAIN + c, :], None).then_inc(tail_b, 16)

            def gather(table, layer):
                with pool.Fori(0, RROUNDS) as i:
                    for r in range(RING):
                        pool.wait_ge(idx_ready, i * RING + ((layer - 1) * BATCHES + r + 1))
                        pool.sem_inc(issued, 1)
                        for c in range(CH):
                            pool.indirect_dma_start(
                                node_rows[:, r, c, 0:D], None, table,
                                bass.IndirectOffsetOnAxis(idx_gather[:, r, c:c + 1], 0)).then_inc(
                                gathered[r], 16)

            pool.wait_ge(x1_out, 16)
            gather(x1_table.rearrange("p g d -> (p g) d"), 1)
            pool.wait_ge(st["f1"]["z"], GROUPS)
            pool.memset(sums_flat, 0.0).then_inc(sums_zero2, 1)
            pool.wait_ge(msg_out_a, 16 * STEPS)
            pool.wait_ge(msg_out_b, 16 * STEPS)
            gather(msg_table.rearrange("p g (t d) -> (p g t) d", t=TYPES), 2)
            for i in range(STEPS):
                t = Bt[:, i * STEP:(i + 1) * STEP, :]
                pool.wait_ge(b_normed, (i + 1) * STEP)
                pool.tensor_tensor(t, t, bc[:, 0:1, :].broadcast_to([P, STEP, D]), ALU.mult).then_inc(scaled_b, 1)
                pool.wait_ge(scaled_b, i + 1)
                pool.tensor_tensor(t, t, bc[:, 1:2, :].broadcast_to([P, STEP, D]), ALU.add).then_inc(
                    norm_ready, 1)
            pool.wait_ge(st["f2"]["z"], GROUPS)
            pool.memset(sums_flat, 0.0).then_inc(sums_zero2, 1)
            pool.wait_ge(z_out, 16 * STEPS)
            gather(z_table.rearrange("p g d -> (p g) d"), 3)

        W_LOADS = 1 + 3 + 2 * TYPES + 1 + 1 + 13 + VECTORS

        @block.scalar
        def _(act):
            with act.Fori(0, STEPS) as i:
                for j in range(COUNT_SPLIT, STEP):
                    act.wait_ge(masks_made, i * (STEP - COUNT_SPLIT) + (j + 1 - COUNT_SPLIT))
                    mask = masks[:, bass.ds(i * STEP + j, 1), :].rearrange("p a c -> p (a c)")
                    act.activation(mask, mask, ACT.Copy,
                                   accum_out=cnt[:, bass.ds(i * STEP + j, 1)]).then_inc(counted, 1)
            zero_last_chunks(act, mybir.EngineType.Activation, ZERO_CUT, STEP)
            def stage_a(i, r):
                at = i * (SRING * BATCH) + r * BATCH
                act.copy(idx_scatter[:, r, :], slot_src[:, bass.ds(at, BATCH)])
                act.copy(edge_rows[:, r, :, LANE1:LANE1 + 1].rearrange("p c a -> p (c a)"),
                         lane1_src[:, bass.ds(at, BATCH)]).then_inc(staged_a, 1)

            act.wait_ge(slots_ready, 1)
            act.wait_ge(gp_ones, 1)
            for r in range(SRING):
                stage_a(0, r)
            act.wait_ge(w_in, 16 * W_LOADS)
            for k in range(6):
                act.wait_ge(prep_t, k + 1)
                act.copy(wT[:, k, :], bank(6, D)).then_inc(prep_out, 1)
            for k in range(2):
                act.wait_ge(bc_done, k + 1)
                n = min(4, VECTORS - 4 * k)
                act.copy(bc[:, 4 * k:4 * k + n, :].rearrange("p k d -> p (k d)"), bank(6, n * D)).then_inc(
                    bc_copied, 1)
            act.wait_ge(bias0_done, 1)
            act.activation(bias0[:, :], ps[:, 6, 0:1], ACT.Identity, bias=cols[:, 1:2]).then_inc(bias0_out, 1)
            for part, ends in enumerate(((1, FIRST_ROUNDS), (FIRST_ROUNDS, ROUNDS))):
                act.wait_ge(slots_ready, part + 1)
                with act.Fori(*ends) as i:
                    for r in range(SRING):
                        act.wait_ge(scattered_a[r], i * (16 * BATCH))
                        stage_a(i, r)
            act.wait_ge(tail_in, 16)
            act.wait_ge(pay_ready, 1)
            act.copy(idx_tail[:, 0, :], slot_src[:, MAIN:COLS])
            act.copy(idx_tail[:, 1, :], slot_dst[:, MAIN:COLS])
            act.copy(tail_rows[:, :, ONE:ONE + 1].rearrange("p c a -> p (c a)"), ones[:, 0:TAIL])
            act.copy(tail_rows[:, :, LANE1:LANE1 + 1].rearrange("p c a -> p (c a)"),
                     lane1_src[:, MAIN:COLS]).then_inc(staged_tail, 1)

            act.wait_ge(x_in, 32)
            with act.Fori(0, STEPS) as i:
                for j in range(STEP):
                    g = i * STEP + j
                    act.copy(zr[:, j, :], X[:, bass.ds(g, 1), :].rearrange("p a d -> p (a d)")).then_inc(
                        prep_in, 1)
                    act.wait_ge(xt_done, g + 1)
                    act.copy(A[:, bass.ds(g * D, D)], bank(6, D)).then_inc(xt_copied, 1)

            def copy_t(stage, i):
                act.wait_ge(st[stage]["t"], i + 1)
                act.copy(zt_flat, tslots()).then_inc(st[stage]["c"], 1)

            def relu_cols(stage, i, bias):
                for h in range(2):
                    act.wait_ge(st[stage]["m"], i * 2 + (h + 1))
                    act.activation(A[:, bass.ds(i * (2 * HALF) + h * HALF, HALF)], bank(2 + h, HALF),
                                   ACT.Relu, bias=bias).then_inc(st[stage]["r"], 1)

            def bn_sqrt(k):
                act.wait_ge(bnsd_in, k + 1)
                act.activation(bn_c[:, k, 0:1], bn_mv[:, 1:2], ACT.Sqrt, bias=eps_col[:, :]).then_inc(
                    bnsd_out, 1)

            copy_t("mlp0", 0)
            with act.Fori(0, STEPS - 1) as i:
                relu_cols("mlp0", i, bias0[:, :])
                copy_t("mlp0", i + 1)
            relu_cols("mlp0", STEPS - 1, bias0[:, :])
            bn_sqrt(0)
            for k, stage in ((1, "mlp1"), (2, "mlp2")):
                with act.Fori(0, STEPS) as i:
                    relu_cols(stage, i, cols[:, k + 1:k + 2])
                bn_sqrt(k)

            def affine_all(stage, k):
                def affine_cols(i):
                    for j in range(STEP):
                        act.activation(zr[:, j, :], A[:, bass.ds((i * STEP + j) * D, D)], ACT.Identity,
                                       bias=bn_c[:, k, 3:4], scale=bn_c[:, k, 2:3]).then_inc(st[stage]["z"], 1)

                act.wait_ge(bn_in, k - 1)
                affine_cols(0)
                with act.Fori(0, STEPS - 1) as i:
                    act.wait_ge(st[stage]["t"], i + 1)
                    affine_cols(i + 1)

            affine_all("x1", 2)

            def ln_sqrt(k, i=None):
                part = slice(None) if i is None else bass.ds(i * STEP, STEP)
                value = sum(MV_COUNT[:k - 1]) + 1
                act.wait_ge(mv_done, value if i is None else i + value)
                act.activation(sd[:, part], mv[:, 1, part], ACT.Sqrt,
                               bias=eps_col[:, :]).then_inc(sd_done, 1)

            def stage_gather(layer, i, r):
                b = i * RING + r
                act.wait_ge(products, b + (layer * BATCHES + 1))
                word = P_SRCT if layer == 2 else P_SRC
                act.copy(idx_gather[:, r, :], ordered[:, bass.ds(b * CH, CH), word:word + 1].rearrange(
                    "p c a -> p (c a)")).then_inc(idx_ready, 1)
                if layer == 1:
                    act.copy(node_rows[:, r, :, D:AW],
                             ordered[:, bass.ds(b * CH, CH), P_ONE:PAY]).then_inc(extras_ready, 1)

            def stage_rest(layer):
                with act.Fori(1, RROUNDS) as i:
                    for r in range(RING):
                        stage_gather(layer, i, r)

            def normalise(v, i, ready, count, done):
                act.wait_ge(ready, i * count + count)
                for j in range(STEP):
                    g = i * STEP + j
                    t = v[:, bass.ds(g, 1), :].rearrange("p a d -> p (a d)")
                    act.activation(t, t, ACT.Identity, bias=nmr[:, bass.ds(g, 1)],
                                   scale=rstd[:, bass.ds(g, 1)]).then_inc(done, 1)

            ln_sqrt(1)
            act.wait_ge(first_in, 16)
            for r in range(RING):
                stage_gather(1, 0, r)
            act.wait_ge(ordered_in, 16)
            stage_rest(1)
            act.wait_ge(deg_ready, 1)
            act.activation(deg[:, 2, :], deg[:, 1, :], ACT.Sqrt).then_inc(deg_sd, 1)

            def g2_copy(i):
                act.wait_ge(st["g2"]["t"], i + 1)
                if not first_of(i):
                    act.wait_ge(st["g2"]["m"], i * STEP)
                act.copy(zt2[:, :, :].rearrange("p j d -> p (j d)"), tslots(4)).then_inc(st["g2"]["c"], 1)

            def g2_operands(i):
                act.wait_ge(f1_scaled, i + 1)
                for j in range(STEP):
                    g = i * STEP + j
                    act.activation(zr2[:, j, :], X[:, bass.ds(g, 1), :].rearrange("p a d -> p (a d)"),
                                   ACT.Identity, bias=nmr[:, bass.ds(g, 1)],
                                   scale=rstd[:, bass.ds(g, 1)]).then_inc(st["g2"]["z"], 1)

            copy_t("f1", 0)
            act.wait_ge(st["f1"]["m"], 1)
            copy_t("f1", 1)
            ln_sqrt(2, 0)
            g2_operands(0)
            act.wait_ge(st["f1"]["m"], 2)
            copy_t("f1", 2)
            ln_sqrt(2, 1)
            with act.Fori(2, STEPS - 1) as i:
                g2_copy(i - 2)
                g2_operands(i - 1)
                act.wait_ge(st["f1"]["m"], i + 1)
                copy_t("f1", i + 1)
                ln_sqrt(2, i)
            g2_copy(STEPS - 3)
            g2_operands(STEPS - 2)
            ln_sqrt(2, STEPS - 1)
            g2_copy(STEPS - 2)
            g2_operands(STEPS - 1)
            g2_copy(STEPS - 1)
            for r in range(RING):
                stage_gather(2, 0, r)
            def own_in(i, first, count=2):
                if not first_of(i):
                    act.wait_ge(st["h2"]["t"], i)
                for k in range(count):
                    ins = act.copy(zr[:, k, :], X[:, bass.ds(first + k, 1), :].rearrange("p a d -> p (a d)"))
                ins.then_inc(st["h2"]["z"], 1)

            def own_t(i, count=2):
                act.wait_ge(st["h2"]["t"], i + 1)
                if not first_of(i):
                    act.wait_ge(st["h2"]["m"], i)
                act.copy(zt_flat[:, 0:count * D], bank(4, count * D)).then_inc(st["h2"]["c"], 1)

            with act.Fori(0, STEPS) as i:
                normalise(X, i, st["g2"]["z"], STEP, x_normed)
            act.wait_ge(x_normed, GROUPS)
            own_in(0, 0, 1)
            own_t(0, 1)
            own_in(1, 1)
            with act.Fori(1, OWN_SETS) as i:
                stage_gather(2, i, 0)
                own_t(i)
                own_in(i + 1, i * 2 + 1)
                for r in range(1, RING):
                    stage_gather(2, i, r)
            stage_gather(2, OWN_SETS, 0)
            own_t(OWN_SETS)
            for r in range(1, RING):
                stage_gather(2, OWN_SETS, r)
            with act.Fori(OWN_SETS + 1, RROUNDS) as i:
                for r in range(RING):
                    stage_gather(2, i, r)
            copy_t("f2", 0)
            act.wait_ge(st["f2"]["m"], 1)
            copy_t("f2", 1)
            ln_sqrt(3, 0)
            with act.Fori(1, STEPS - 1) as i:
                act.wait_ge(st["f2"]["m"], i + 1)
                copy_t("f2", i + 1)
                normalise(Bt, i - 1, f2_scaled, 1, b_normed)
                ln_sqrt(3, i)
            normalise(Bt, STEPS - 2, f2_scaled, 1, b_normed)
            ln_sqrt(3, STEPS - 1)
            normalise(Bt, STEPS - 1, f2_scaled, 1, b_normed)
            def gelu(i):
                act.wait_ge(norm_ready, i + 1)
                v = B[:, bass.ds(i * (STEP * D), STEP * D)]
                act.activation(v, v, ACT.Gelu).then_inc(gelu_done, 1)

            with act.Fori(0, STEPS) as i:
                gelu(i)
            ln_sqrt(4)
            for r in range(RING):
                stage_gather(3, 0, r)
            act.wait_ge(z_scaled, 1)
            with act.Fori(0, STEPS) as i:
                for j in range(Z_CUT, STEP):
                    g = i * STEP + j
                    ins = act.activation(At[:, bass.ds(g, 1), :].rearrange("p a d -> p (a d)"),
                                         X[:, bass.ds(g, 1), :].rearrange("p a d -> p (a d)"), ACT.Identity,
                                         bias=small[:, 1, bass.ds(g, 1)], scale=small[:, 0, bass.ds(g, 1)])
                ins.then_inc(st["g3"]["z"], 1)
            act.wait_ge(z_out, 16 * STEPS)
            with act.Fori(0, STEPS) as i:
                normalise(X, i, st["g3"]["r"], 1, x_normed)
            stage_rest(3)
            with act.Fori(0, STEPS) as i:
                for j in range(STEP):
                    g = i * STEP + j
                    t = At[:, bass.ds(g, 1), :].rearrange("p a d -> p (a d)")
                    act.activation(t, t, ACT.Copy, scale=dinv[:, bass.ds(g, 1)]).then_inc(loops_ready, 1)

            copy_t("f3", 0)
            with act.Fori(0, STEPS - 1) as i:
                relu_cols("f3", i, cols[:, 12:13])
                copy_t("f3", i + 1)
            relu_cols("f3", STEPS - 1, cols[:, 12:13])
            bn_sqrt(3)
            affine_all("x3", 3)
            ln_sqrt(5)
            act.wait_ge(y_scaled, 1)
            with act.Fori(0, STEPS) as i:
                for j in range(Y_CUT, STEP):
                    g = i * STEP + j
                    t = X[:, bass.ds(g, 1), :].rearrange("p a d -> p (a d)")
                    act.activation(t, t, ACT.Identity, bias=nmr[:, bass.ds(g, 1)],
                                   scale=rstd[:, bass.ds(g, 1)]).then_inc(y_ready2, 1)

        @block.tensor
        def _(pe):
            def count_sums(k):
                pe.matmul(ps[:, 7, 0:GROUPS], before[:, :], cnt[:, :], start=True, stop=True)
                pe.matmul(ps[:, 7, 2 * GROUPS:3 * GROUPS], ones[:, :], cnt[:, :], start=True,
                          stop=True).then_inc(counts_summed, 1)

            pe.sem_inc(products, RING)
            pe.wait_ge(consts, 7)
            pe.wait_ge(counted, STEPS * (STEP - COUNT_SPLIT))
            pe.wait_ge(counted_dve, STEPS * COUNT_SPLIT)
            count_sums(0)
            pe.wait_ge(w_in, 16 * W_LOADS)
            for k in range(6):
                if k:
                    pe.wait_ge(prep_out, k)
                pe.transpose(bank(6, D), wraw[:, k, :], ident[:, :]).then_inc(prep_t, 1)
            pe.wait_ge(prep_out, 6)
            for k in range(2):
                n = min(4, VECTORS - 4 * k) * D
                if k:
                    pe.wait_ge(bc_copied, k)
                pe.matmul(bank(6, n), ones[0:1, :], bc_src[0:1, 4 * k * D:4 * k * D + n],
                          start=True, stop=True).then_inc(bc_done, 1)
            pe.wait_ge(bc_copied, 2)
            pe.matmul(ps[:, 6, 0:1], wT[:, 2, :], cols[:, 0:1], start=True, stop=True).then_inc(bias0_done, 1)
            pe.wait_ge(bias0_out, 1)
            pe.wait_ge(counted_dve, STEPS * COUNT_SPLIT + GROUPS)
            count_sums(1)
            with pe.Fori(0, STEPS) as i:
                for j in range(STEP):
                    pe.wait_ge(prep_in, i * STEP + (j + 1))
                    pe.transpose(bank(6, D), zr[:, j, :], ident[:, :]).then_inc(xt_done, 1)
            pe.wait_ge(xt_copied, GROUPS)

            def reduce(q):
                width = ONE + 1 if q == 0 else AW if q == 1 else D
                rows = slot_rows if q == 0 else node_rows
                def one_round(i, beside=None):
                    for r in range(RING):
                        b = i * RING + r
                        pe.wait_ge(onehot_ready, b + (q * BATCHES + 1))
                        pe.wait_ge(added, b * CH + (CH + q * CHUNKS))
                        if q == 1:
                            pe.wait_ge(extras_ready, b + 1)
                        if q == 0:
                            pe.wait_ge(slot_rows_in[r], i * 16 + 16)
                        else:
                            pe.wait_ge(gathered[r], i * (16 * CH) + ((q - 1) * RROUNDS + 1) * (16 * CH))
                        for j in range(CH):
                            ins = pe.matmul(product(r % 2, j, width), onehot[:, r % 2, j, :],
                                            rows[:, r, j, 0:width], start=True, stop=True)
                        ins.then_inc(products, 1)
                        if beside and r == 0:
                            own_turn(i + 1)
                        if beside and r == RING // 2:
                            own_wide(i + 1)

                if q == 2:
                    with pe.Fori(0, OWN_SETS) as i:
                        one_round(i, True)
                with pe.Fori(OWN_SETS if q == 2 else 0, RROUNDS) as i:
                    one_round(i)

            def own_turn(i, count=2):
                pe.wait_ge(st["h2"]["z"], i + 1)
                if not first_of(i):
                    pe.wait_ge(st["h2"]["c"], i)
                for k in range(count):
                    ins = pe.transpose(bank(4, count * D)[:, k * D:(k + 1) * D], zr[:, k, :], ident[:, :])
                ins.then_inc(st["h2"]["t"], 1)

            def own_wide(i, count=2):
                pe.wait_ge(st["h2"]["c"], i + 1)
                if not first_of(i):
                    pe.wait_ge(st["h2"]["r"], i)
                for k in range(count):
                    ins = pe.matmul(bank(5 + k), zt[:, k, :],
                                    wcat[:, TYPES:2 * TYPES + 1, :].rearrange("p k d -> p (k d)"),
                                    start=True, stop=True)
                ins.then_inc(st["h2"]["m"], 1)

            def turn(stage, i, operands=zr, base=0):
                for j in range(STEP):
                    pe.wait_ge(st[stage]["z"], i * STEP + (j + 1))
                    ins = pe.transpose(tslot(j, base), operands[:, j, :], ident[:, :])
                ins.then_inc(st[stage]["t"], 1)

            reduce(0)
            def mlp0(i):
                for h in range(2):
                    pe.matmul(bank(2 + h, HALF), wT[:, 0, :],
                              A[:, bass.ds(i * (2 * HALF) + h * HALF, HALF)], start=True, stop=False)
                    pe.matmul(bank(2 + h, HALF), wT[:, 1, :],
                              zt_flat[:, h * HALF:(h + 1) * HALF],
                              start=False, stop=True).then_inc(st["mlp0"]["m"], 1)

            turn("mlp0", 0)
            with pe.Fori(0, STEPS - 1) as i:
                pe.wait_ge(st["mlp0"]["c"], i + 1)
                turn("mlp0", i + 1)
                mlp0(i)
            pe.wait_ge(st["mlp0"]["c"], STEPS)
            mlp0(STEPS - 1)
            for k, stage in ((1, "mlp1"), (2, "mlp2")):
                def sublayer(i):
                    for h in range(2):
                        pe.matmul(bank(2 + h, HALF), wT[:, 2 + k, :],
                                  A[:, bass.ds(i * (2 * HALF) + h * HALF, HALF)],
                                  start=True, stop=True).then_inc(st[stage]["m"], 1)
                pe.wait_ge(bn_applied, k)
                sublayer(0)
                with pe.Fori(1, STEPS) as i:
                    pe.wait_ge(st[stage]["r"], i * 2)
                    sublayer(i)
            turn("x1", 0)
            with pe.Fori(1, STEPS) as i:
                pe.wait_ge(st["x1"]["r"], i)
                turn("x1", i)
            reduce(1)

            def dense(stage, w, i):
                pe.wait_ge(st[stage]["c"], i + 1)
                for j in range(STEP):
                    ins = pe.matmul(tslot(j, 2), zt[:, j, :], w, start=True, stop=True)
                ins.then_inc(st[stage]["m"], 1)

            def g2_turn(i):
                if not first_of(i):
                    pe.wait_ge(st["g2"]["c"], i)
                turn("g2", i, zr2, 4)

            def g2_wide(i):
                pe.wait_ge(st["g2"]["c"], i + 1)
                for j in range(STEP):
                    pe.wait_ge(st["g2"]["r"], i * STEP + (j + (2 if j == 0 else 1)))
                    pe.matmul(bank(6 + j % 2, TYPES * D), zt2[:, j, :],
                              wcat[:, 0:TYPES, :].rearrange("p k d -> p (k d)"),
                              start=True, stop=True).then_inc(st["g2"]["m"], 1)

            turn("f1", 0)
            pe.wait_ge(st["f1"]["c"], 1)
            turn("f1", 1)
            dense("f1", wT[:, 5, :], 0)
            pe.wait_ge(st["f1"]["c"], 2)
            turn("f1", 2)
            pe.wait_ge(st["f1"]["r"], 1)
            dense("f1", wT[:, 5, :], 1)
            with pe.Fori(2, STEPS - 1) as i:
                pe.wait_ge(st["f1"]["c"], i + 1)
                turn("f1", i + 1)
                g2_turn(i - 2)
                pe.wait_ge(st["f1"]["r"], i)
                dense("f1", wT[:, 5, :], i)
                g2_wide(i - 2)
            g2_turn(STEPS - 3)
            pe.wait_ge(st["f1"]["r"], STEPS - 1)
            dense("f1", wT[:, 5, :], STEPS - 1)
            g2_wide(STEPS - 3)
            g2_turn(STEPS - 2)
            g2_wide(STEPS - 2)
            g2_turn(STEPS - 1)
            g2_wide(STEPS - 1)
            pe.wait_ge(st["g2"]["r"], NEAR + GROUPS)
            own_turn(0, 1)
            own_wide(0, 1)
            reduce(2)
            turn("f2", 0)
            pe.wait_ge(st["f2"]["c"], 1)
            turn("f2", 1)
            dense("f2", wcat[:, 7, :], 0)
            with pe.Fori(1, STEPS - 1) as i:
                pe.wait_ge(st["f2"]["c"], i + 1)
                turn("f2", i + 1)
                pe.wait_ge(st["f2"]["r"], i)
                dense("f2", wcat[:, 7, :], i)
            pe.wait_ge(st["f2"]["r"], STEPS - 1)
            dense("f2", wcat[:, 7, :], STEPS - 1)
            reduce(3)

            def f3(i):
                for h in range(2):
                    pe.matmul(bank(2 + h, HALF), w3[:, :], zt_flat[:, h * HALF:(h + 1) * HALF],
                              start=True, stop=True).then_inc(st["f3"]["m"], 1)

            turn("f3", 0)
            with pe.Fori(0, STEPS - 1) as i:
                pe.wait_ge(st["f3"]["c"], i + 1)
                turn("f3", i + 1)
                f3(i)
            pe.wait_ge(st["f3"]["c"], STEPS)
            f3(STEPS - 1)
            turn("x3", 0)
            with pe.Fori(1, STEPS) as i:
                pe.wait_ge(st["x3"]["r"], i)
                turn("x3", i)

        @block.vector
        def _(dve):
            chain = Chain(dve, chain_sem)
            mark, link, wait = chain.mark, chain.link, chain.wait

            def tile(v, g):
                return v[:, bass.ds(g, 1), :].rearrange("p a d -> p (a d)")

            dve.memset(src_i[:, MAIN:COLS], NO_NODE)
            dve.memset(dst_i[:, MAIN:COLS], NO_NODE)
            dve.memset(type_i[:, MAIN:COLS], 0)
            dve.memset(w_f[:, MAIN:COLS], 0.0)
            dve.memset(X[:, GROUPS - 1, :], 0.0).then_inc(pad_ready, 1)

            def split_key(key, lane1):
                mark(dve.tensor_scalar(tmp_i, key, SHIFT, None, ALU.arith_shift_right))
                link(dve.tensor_scalar(tmp2_i, key, P - 1, None, ALU.bitwise_and))
                mark(dve.tensor_copy(group_b, tmp_i))
                link(dve.tensor_scalar(lane1, tmp2_i, 1.0, None, ALU.add))

            def start_slots(k):
                link(dve.tensor_scalar(small[:, 0, :], ps[:, 7, 2 * GROUPS:3 * GROUPS], P - 1.0, None, ALU.add))
                link(dve.tensor_copy(small_i[:, :], small[:, 0, :]))
                link(dve.tensor_scalar(small_i[:, :], small_i[:, :], SHIFT, None, ALU.arith_shift_right))
                link(dve.tensor_copy(small[:, 1, :], small_i[:, :]))
                link(dve.tensor_tensor_scan(small[:, 2, :], small[:, 1, :], small[:, 1, :], 0.0,
                                            ALU.add, ALU.bypass))
                link(dve.tensor_tensor(small[:, 3, :], small[:, 2, :], small[:, 1, :], ALU.subtract))
                link(dve.scalar_tensor_tensor(out=small[:, 4, :], in0=small[:, 3, :], scalar=float(P),
                                              in1=ps[:, 7, 0:GROUPS], op0=ALU.mult, op1=ALU.add))
                link(dve.tensor_scalar(start_at[:, :], small[:, 4, :], -1.0, None, ALU.add))
                link(dve.tensor_tensor(below[:, :, :],
                                       small[0:BATCHES, 2:3, :].broadcast_to([BATCHES, CH, GROUPS]),
                                       chunk_ids[:, :, None].broadcast_to([BATCHES, CH, GROUPS]), ALU.is_le))
                link(dve.tensor_reduce(tile_of[:, :], below[:, :, :], AX_X, ALU.add))
                if k == 0:
                    dve.tensor_scalar(last_chunk[:, :, 0:STEP],
                                      small[:, 2, :].rearrange("p (i j) -> p i j", j=STEP), -1.0, 0.0,
                                      ALU.add, ALU.max)
                dve.tensor_scalar(at_cols[:, k, :], tile_of[:, :], GROUPS - 1.0, float(AW), ALU.min,
                                  ALU.mult).then_inc(cols_ready, 1)

            def rank(slot, cuts):
                link(dve.memset(pos, 0.0))
                for c0, c1 in zip(cuts, cuts[1:]):
                    part = slice(c0, c1)
                    scans = []
                    for g in range(GROUPS + 1):
                        if g < GROUPS:
                            running = ps[:, 2 * (g % 3):2 * (g % 3) + 2, :].rearrange(
                                "p b n -> p (b n)")[:, 0:c1 - c0]
                            scans.append((running, mark(dve.tensor_tensor_scan(
                                running, masks[:, g, part], masks[:, g, part], start_at[:, g:g + 1],
                                ALU.add, ALU.bypass))))
                        if g:
                            running, scanned = scans[g - 1]
                            wait(last if g > 1 else scanned)
                            if c1 < COLS:
                                dve.tensor_copy(start_at[:, g - 1:g], running[:, c1 - c0 - 1:c1 - c0])
                            last = mark(dve.copy_predicated(pos[:, part], masks[:, g - 1, part], running))
                    wait(last)
                    link(dve.tensor_copy(tmp_i[:, part], pos[:, part]))
                    link(dve.tensor_scalar(tmp2_i[:, part], tmp_i[:, part], P - 1, None, ALU.bitwise_and))
                    link(dve.tensor_scalar(tmp_i[:, part], tmp_i[:, part], SHIFT, None, ALU.arith_shift_right))
                    dve.scalar_tensor_tensor(out=slot[:, part], in0=tmp2_i[:, part], scalar=float(CHUNKS),
                                             in1=tmp_i[:, part], op0=ALU.mult, op1=ALU.add).then_inc(
                        slots_ready, 1)

            def count_masks(i, js):
                for j in js:
                    g = i * STEP + j
                    dve.tensor_scalar(tile(masks, g), group_b, group_ids[:, bass.ds(g, 1)], 0.0,
                                      ALU.is_equal, ALU.add,
                                      accum_out=cnt[:, bass.ds(g, 1)]).then_inc(counted_dve, 1)

            dve.wait_ge(keys_in, 32)
            dve.wait_ge(consts, 7)
            split_key(src_i, lane1_src)
            with dve.Fori(0, STEPS) as i:
                count_masks(i, range(COUNT_SPLIT))
                for j in range(COUNT_SPLIT, STEP):
                    g = i * STEP + j
                    dve.tensor_scalar(tile(masks, g), group_b, group_ids[:, bass.ds(g, 1)], None,
                                      ALU.is_equal).then_inc(masks_made, 1)
            link(dve.scalar_tensor_tensor(out=pay[:, :, P_SRC], in0=tmp2_i, scalar=float(GROUPS), in1=tmp_i,
                                          op0=ALU.mult, op1=ALU.add))
            dve.wait_ge(counts_summed, 1)
            start_slots(0)
            rank(slot_src, (0, FIRST_ROUNDS * SRING * BATCH, COLS))
            dve.wait_ge(slots_ready, 2)
            dve.wait_ge(lists_in, 96)
            split_key(dst_i, pay[:, :, P_LANE1])
            with dve.Fori(0, STEPS) as i:
                count_masks(i, range(STEP))
            dve.wait_ge(counts_summed, 2)
            start_slots(1)
            rank(slot_dst, (0, COLS))
            dve.wait_ge(slots_ready, 3)
            dve.scalar_tensor_tensor(out=pay[:, :, P_SRCT], in0=pay[:, :, P_SRC], scalar=float(TYPES),
                                     in1=type_i, op0=ALU.mult, op1=ALU.add)
            dve.memset(pay[:, :, P_ONE], 1.0)
            for t in range(TYPES):
                dve.tensor_scalar(pay[:, :, P_TYPE + t], type_i, float(t), None, ALU.is_equal)
            dve.tensor_copy(pay[:, :, P_W], w_f).then_inc(pay_ready, 1)

            def own_terms(i, first, count=2):
                dve.wait_ge(st["h2"]["m"], i + 1)
                groups = [(5 + k, first + k) for k in range(count)]
                for t in range(TYPES):
                    for b, g in groups:
                        part = ps[:, b, t * D:(t + 1) * D]
                        share = ctype[:, t, bass.ds(g, 1)]
                        if t == 0:
                            ins = dve.tensor_scalar(tile(At, g), part, share, None, ALU.mult)
                        else:
                            ins = dve.scalar_tensor_tensor(out=tile(At, g), in0=part, scalar=share,
                                                           in1=tile(At, g), op0=ALU.mult, op1=ALU.add)
                        if t < TYPES - 1:
                            mark(ins)
                    if t < TYPES - 1:
                        for b, g in groups if t == 0 else ():
                            dve.tensor_tensor(tile(Bt, g), ps[:, b, TYPES * D:], bc[:, 2 + TYPES, :], ALU.add)
                        wait(chain.last())
                ins.then_inc(st["h2"]["r"], 1)

            def reduce(q):
                width = ONE + 1 if q == 0 else AW if q == 1 else D

                def one_hot(i, r, j):
                    s, to = r % 2, onehot[:, r % 2, j, :]
                    if j == 0:
                        dve.wait_ge(products, i * RING + (q * BATCHES + r + RING - 1))
                        if q == 0:
                            dve.wait_ge(slot_rows_in[r % RING], i * 16 + (r // RING + 1) * 16)
                    if q == 0:
                        ins = dve.tensor_scalar(to, lane_ids[:, :], slot_rows[:, r % RING, j, LANE1:LANE1 + 1],
                                                None, ALU.is_equal)
                    else:
                        edge = ordered[:, bass.ds(i * (RING * CH) + (r * CH + j), 1), :].rearrange(
                            "p a w -> p (a w)")
                        lane1, weight = edge[:, P_LANE1:P_LANE1 + 1], edge[:, P_W:P_W + 1]
                        if q < 3:
                            ins = dve.tensor_scalar(to, lane_ids[:, :], lane1, None, ALU.is_equal)
                        else:
                            ins = dve.tensor_scalar(to, lane_ids[:, :], lane1, weight, ALU.is_equal, ALU.mult)
                    if j == CH - 1:
                        ins.then_inc(onehot_ready, 1)

                def batch(i, r, ahead=True):
                    b = i * RING + r
                    at = nc.values_load_multi_w_load_instructions(
                        (at_src if q == 0 else at_dst)[0:1, bass.ds(b * CH, CH)], engines=[DVE],
                        min_val=0, max_val=(GROUPS - 1) * AW,
                        skip_runtime_bounds_check_because="the tables hold at most GROUPS - 1 times AW")[1]
                    dve.wait_ge(products, b + (q * BATCHES + RING + 1))
                    for j in range(CH):
                        dve.wait_ge(added, b * CH + (2 * CH + q * CHUNKS + j))
                        to = sums_flat[:, bass.ds(at[j], width)]
                        dve.tensor_tensor(to, to, product(r % 2, j, width), ALU.add).then_inc(added, 1)
                        if ahead:
                            one_hot(i, r + 2, j)

                for r in range(2):
                    for j in range(CH):
                        one_hot(0, r, j)

                def rounds(first, end, beside=False):
                    with dve.Fori(first, end) as i:
                        for r in range(RING):
                            batch(i, r)
                            if beside and r == 0:
                                chain.enter(i - first, 4)
                                own_terms(i, i * 2 - 1)
                                chain.leave(end - first)

                if q == 2:
                    rounds(0, 1)
                    rounds(1, OWN_SETS + 1, True)
                    assert OWN_SETS + 1 == RROUNDS - 1
                else:
                    rounds(0, RROUNDS - 1)
                for r in range(RING):
                    batch(RROUNDS - 1, r, r < RING - 2)
                dve.wait_ge(added, 2 * CH + (q + 1) * CHUNKS)

            def step_of(v, i):
                return v[:, bass.ds(i * STEP, STEP), :]

            def group_stats(v, i, js=range(STEP)):
                for j in js:
                    g = i * STEP + j
                    dve.bn_stats(tile(stats, g), tile(v, g)).then_inc(stats_done, 1)

            ln_count = [0]

            def of_step(i):
                return slice(None) if i is None else bass.ds(i * STEP, STEP)

            def variances(i=None):
                part = of_step(i)
                dve.wait_ge(stats_done, GROUPS * (ln_count[0] + 1) if i is None
                            else i * STEP + (STEP + GROUPS * ln_count[0]))
                mean_e, mean_o, var_e, var_o = (stats[:, part, k] for k in (1, 4, 2, 5))
                mark(dve.tensor_tensor(mv[:, 0, part], mean_e, mean_o, ALU.add))
                mark(dve.tensor_tensor(sd[:, part], mean_e, mean_o, ALU.subtract))
                link(dve.tensor_tensor(mv[:, 1, part], var_e, var_o, ALU.add))
                mark(dve.scalar_tensor_tensor(out=sd[:, part], in0=sd[:, part], scalar=0.25, in1=sd[:, part],
                                              op0=ALU.mult, op1=ALU.mult))
                link(dve.tensor_scalar(mv[:, 0, part], mv[:, 0, part], 0.5, None, ALU.mult))
                dve.scalar_tensor_tensor(out=mv[:, 1, part], in0=mv[:, 1, part], scalar=1.0 / D,
                                         in1=sd[:, part], op0=ALU.mult, op1=ALU.add).then_inc(mv_done, 1)

            def scales(i=None):
                part = of_step(i)
                before = sum(MV_COUNT[:ln_count[0]])
                dve.wait_ge(sd_done, before + 1 if i is None else i + (before + 1))
                link(dve.reciprocal(rstd[:, part], sd[:, part]))
                link(dve.scalar_tensor_tensor(out=nmr[:, part], in0=mv[:, 0, part], scalar=-1.0,
                                              in1=rstd[:, part], op0=ALU.mult, op1=ALU.mult))

            def layer_norm_scale():
                variances()
                scales()
                ln_count[0] += 1

            def normalised(to, v, g):
                return dve.tensor_scalar(to, tile(v, g), rstd[:, bass.ds(g, 1)], nmr[:, bass.ds(g, 1)],
                                         ALU.mult, ALU.add)

            dve.sem_inc(added, 2 * CH)
            link(dve.memset(sums_flat, 0.0))
            dve.wait_ge(at_in, 32)
            reduce(0)
            link(dve.tensor_scalar(sd[:, :], sums[:, :, ONE], 1.0, None, ALU.max))
            link(dve.reciprocal(rcnt[:, :], sd[:, :]))

            def edge_means(i):
                for j in range(STEP):
                    g = i * STEP + j
                    dve.tensor_scalar(zr[:, j, :], tile(sums, g)[:, 0:D], rcnt[:, bass.ds(g, 1)], None,
                                      ALU.mult).then_inc(st["mlp0"]["z"], 1)

            edge_means(0)
            with dve.Fori(1, STEPS) as i:
                dve.wait_ge(st["mlp0"]["t"], i)
                edge_means(i)
            dve.wait_ge(st["mlp0"]["z"], GROUPS)
            dve.memset(sums_flat, 0.0).then_inc(sums_zero, 1)
            def column_stats(n):
                return mark(dve.bn_stats(bn_st[:, n, :], A[:, n * BN_COLS:(n + 1) * BN_COLS]))

            def batch_norm(k, stage, first=0):
                gamma = 4 + 2 * k
                dve.wait_ge(st[stage]["r"], 2 * STEPS)
                for n in range(first, NBN):
                    last = column_stats(n)
                wait(last)
                dve.bn_aggr(bn_mv[:, :], bn_st[:, :, :].rearrange("p n s -> p (n s)")).then_inc(bnsd_in, 1)
                dve.wait_ge(bnsd_out, k + 1)
                dve.wait_ge(bnsd_in, k + 1)
                c = bn_c[:, k, :]
                link(dve.reciprocal(c[:, 1:2], c[:, 0:1]))
                link(dve.tensor_tensor(c[:, 2:3], c[:, 1:2], cols[:, gamma:gamma + 1], ALU.mult))
                link(dve.tensor_tensor(c[:, 1:2], bn_mv[:, 0:1], c[:, 2:3], ALU.mult))
                return c, dve.tensor_tensor(c[:, 3:4], cols[:, gamma + 1:gamma + 2], c[:, 1:2], ALU.subtract)

            for k, stage in enumerate(("mlp0", "mlp1")):
                c, ins = batch_norm(k, stage)
                link(ins)
                dve.tensor_scalar(A[:, :], A[:, :], c[:, 2:3], c[:, 3:4], ALU.mult, ALU.add).then_inc(
                    bn_applied, 1)
            batch_norm(2, "mlp2")[1].then_inc(bn_in, 1)

            def add_to_nodes(stage):
                with dve.Fori(0, STEPS) as i:
                    dve.wait_ge(st[stage]["t"], i + 1)
                    dve.tensor_tensor(step_of(X, i), step_of(X, i), grouped(tslots()), ALU.add).then_inc(
                        st[stage]["r"], 1)
                    dve.wait_ge(st[stage]["r"], i + 1)
                    group_stats(X, i)
                layer_norm_scale()

            add_to_nodes("x1")
            with dve.Fori(0, STEPS) as i:
                for j in range(STEP):
                    g = i * STEP + j
                    normalised(tile(X, g), X, g).then_inc(x1_ready, 1)
            dve.wait_ge(x1_ready, GROUPS)

            dve.wait_ge(first_in, 16)
            dve.wait_ge(ordered_in, 16)
            dve.wait_ge(sums_zero, 1)
            reduce(1)
            mark(dve.tensor_scalar(sd[:, :], sums[:, :, D], 1.0, None, ALU.max))
            link(dve.tensor_scalar(deg[:, 0, :], sums[:, :, AW - 1], 1.0, None, ALU.add))
            mark(dve.tensor_scalar(deg[:, 1, :], deg[:, 0, :], 1e-30, None, ALU.max))
            link(dve.reciprocal(rcnt[:, :], sd[:, :]))
            dve.sem_inc(deg_ready, 1)
            for t in range(TYPES):
                mark(dve.tensor_tensor(ctype[:, t, :], sums[:, :, D + 1 + t], rcnt[:, :], ALU.mult))

            def f1_operands(i):
                if not first_of(i):
                    dve.wait_ge(st["f1"]["t"], i)
                for j in range(STEP):
                    g = i * STEP + j
                    dve.scalar_tensor_tensor(out=zr[:, j, :], in0=tile(sums, g)[:, 0:D],
                                             scalar=rcnt[:, bass.ds(g, 1)], in1=tile(X, g),
                                             op0=ALU.mult, op1=ALU.add).then_inc(st["f1"]["z"], 1)

            def f1_results(i, messages=None, operands=None):
                dve.wait_ge(st["f1"]["m"], i + 1)
                link(dve.tensor_tensor(grouped(tslots(2)), grouped(tslots(2)),
                                       bc[:, 3 + TYPES:4 + TYPES, :].broadcast_to([P, STEP, D]), ALU.add))
                dve.scalar_tensor_tensor(out=step_of(X, i), in0=grouped(tslots(2)), scalar=0.0,
                                         in1=step_of(X, i), op0=ALU.max, op1=ALU.add).then_inc(
                    st["f1"]["r"], 1)
                if operands is not None:
                    f1_operands(operands)
                dve.wait_ge(st["f1"]["r"], i + 1)
                for j in range(STEP):
                    if messages is not None:
                        g2_results(messages, (j,))
                    group_stats(X, i, (j,))
                variances(i)

            def g2_results(i, js=range(STEP)):
                for j in js:
                    if j in (0, MSG_CUT) and not first_of(i):
                        dve.wait_ge(msg_out_a if j == 0 else msg_out_b, i * 16)
                    dve.wait_ge(st["g2"]["m"], i * STEP + (j + 1))
                    dve.tensor_tensor(msgs[:, j, :], bank(6 + j % 2, TYPES * D),
                                      bc[:, 2:2 + TYPES, :].rearrange("p k d -> p (k d)"), ALU.add).then_inc(
                        st["g2"]["r"], 1)

            def f1_scales(i):
                scales(i)
                dve.sem_inc(f1_scaled, 1)

            dve.sem_inc(st["g2"]["r"], NEAR)
            f1_operands(0)
            f1_operands(1)
            f1_results(0, None, 2)
            f1_scales(0)
            f1_results(1, None, 3)
            f1_scales(1)
            with dve.Fori(2, STEPS - 2) as i:
                chain.enter(i - 2, 8)
                f1_results(i, i - 2, i + 2)
                f1_scales(i)
                chain.leave(STEPS - 4)
            for i in range(STEPS - 2, STEPS):
                f1_results(i, i - 2)
                f1_scales(i)
            ln_count[0] += 1
            dve.wait_ge(deg_sd, 1)
            link(dve.reciprocal(dinv[:, :], deg[:, 2, :]))
            link(dve.scalar_tensor_tensor(out=dinv[:, :], in0=deg[:, 0, :], scalar=0.0, in1=dinv[:, :],
                                          op0=ALU.is_gt, op1=ALU.mult))
            g2_results(STEPS - 2)
            g2_results(STEPS - 1)
            dve.wait_ge(x_normed, GROUPS)

            own_terms(0, 0, 1)
            dve.wait_ge(sums_zero2, 1)
            reduce(2)
            dve.wait_ge(st["h2"]["r"], OWN_SETS + 1)

            def f2_operands(i):
                if not first_of(i):
                    dve.wait_ge(st["f2"]["t"], i)
                for j in range(STEP):
                    g = i * STEP + j
                    dve.scalar_tensor_tensor(out=zr[:, j, :], in0=tile(sums, g)[:, 0:D],
                                             scalar=rcnt[:, bass.ds(g, 1)], in1=tile(At, g),
                                             op0=ALU.mult, op1=ALU.add).then_inc(st["f2"]["z"], 1)

            def f2_results(i, operands=None):
                dve.wait_ge(st["f2"]["m"], i + 1)
                dve.tensor_tensor(step_of(Bt, i), grouped(tslots(2)), step_of(Bt, i), ALU.add).then_inc(
                    st["f2"]["r"], 1)
                if operands is not None:
                    f2_operands(operands)
                dve.wait_ge(st["f2"]["r"], i + 1)
                group_stats(Bt, i)
                variances(i)
                scales(i)
                dve.sem_inc(f2_scaled, 1)

            f2_operands(0)
            f2_operands(1)
            with dve.Fori(0, STEPS - 2) as i:
                chain.enter(i, 7)
                f2_results(i, i + 2)
                chain.leave(STEPS - 2)
            f2_results(STEPS - 2)
            f2_results(STEPS - 1)
            ln_count[0] += 1

            def add_gelu(i):
                dve.wait_ge(gelu_done, i + 1)
                link(dve.scalar_tensor_tensor(out=step_of(X, i), in0=step_of(X, i), scalar=2.0,
                                              in1=step_of(Bt, i), op0=ALU.mult, op1=ALU.add))
                group_stats(X, i)

            with dve.Fori(0, STEPS) as i:
                chain.enter(i, 1)
                add_gelu(i)
                chain.leave(STEPS)
            layer_norm_scale()

            mark(dve.tensor_tensor(small[:, 0, :], rstd[:, :], dinv[:, :], ALU.mult))
            link(dve.tensor_tensor(small[:, 1, :], nmr[:, :], dinv[:, :], ALU.mult))
            dve.sem_inc(z_scaled, 1)
            with dve.Fori(0, STEPS) as i:
                for j in range(Z_CUT):
                    g = i * STEP + j
                    ins = dve.tensor_scalar(tile(At, g), tile(X, g), small[:, 0, bass.ds(g, 1)],
                                            small[:, 1, bass.ds(g, 1)], ALU.mult, ALU.add)
                ins.then_inc(st["g3"]["r"], 1)
            dve.wait_ge(x_normed, 2 * GROUPS)
            dve.wait_ge(sums_zero2, 2)
            reduce(3)

            def f3_operands(i):
                for j in range(STEP):
                    g = i * STEP + j
                    dve.scalar_tensor_tensor(out=zr[:, j, :], in0=tile(sums, g)[:, 0:D],
                                             scalar=dinv[:, bass.ds(g, 1)], in1=tile(At, g),
                                             op0=ALU.mult, op1=ALU.add).then_inc(st["f3"]["z"], 1)

            dve.wait_ge(loops_ready, GROUPS)
            blocks = 0
            for i in range(STEPS):
                if i:
                    dve.wait_ge(st["f3"]["t"], i)
                f3_operands(i)
                if i > 1:
                    dve.wait_ge(st["f3"]["r"], 2 * (i - 1))
                    while (blocks + 1) * BN_COLS <= (i - 1) * STEP * P:
                        column_stats(blocks)
                        blocks += 1
            batch_norm(3, "f3", blocks)[1].then_inc(bn_in, 1)
            add_to_nodes("x3")
            dve.sem_inc(y_scaled, 1)
            with dve.Fori(0, STEPS) as i:
                for j in range(Y_CUT):
                    g = i * STEP + j
                    normalised(tile(X, g), X, g).then_inc(y_ready, 1)


_INS = ["x", "src", "dst", "edge_attr_128", "edge_type_3", "edge_weight",
        "L0_gnn_u", "L0_gnn_W0", "L0_gnn_b0", "L0_gnn_W1", "L0_gnn_b1", "L0_gnn_W2", "L0_gnn_b2",
        "L0_gnn_g0", "L0_gnn_bt0", "L0_gnn_g1", "L0_gnn_bt1", "L0_gnn_g2", "L0_gnn_bt2",
        "L1_gnn_W", "L1_gnn_b", "L2_gnn_Wmsg", "L2_gnn_bmsg", "L2_gnn_Wupd", "L2_gnn_bupd",
        "L2_gnn_gamma", "L2_gnn_beta", "L3_gnn_W", "L3_gnn_b", "L3_gnn_gamma", "L3_gnn_beta"]


def kernel(**inputs):
    import numpy as _np
    import concourse.bacc as _bacc
    from concourse import mybir as _mybir
    from concourse.bass_utils import run_bass_kernel_spmd as _run

    nc = _bacc.Bacc("TRN2", target_bir_lowering=False, num_devices=1)
    arrays, args = {}, []
    for name in _INS:
        a = _np.ascontiguousarray(inputs[name])
        arrays[f"in_{name}"] = a
        args.append(nc.dram_tensor(f"in_{name}", a.shape, _mybir.dt.from_np(a.dtype), kind="ExternalInput").ap())
    args.append(nc.dram_tensor("out_nodes", (N, D), _mybir.dt.float32, kind="ExternalOutput").ap())
    gnn_kernel(nc, *args)
    r = _run(nc, [arrays], core_ids=[0])
    return r.results[0]["out_nodes"]
```
